# Optimizing a Trainium2 kernel written in Bass

```python
import numpy as np
import jax
import jax.numpy as jnp

def _softmax(x, axis=-1):
    return jax.nn.softmax(x, axis=axis)

def _gelu(x):
    return jax.nn.gelu(x, approximate=True)

def _silu(x):
    return jax.nn.silu(x)

def _sigmoid(x):
    return jax.nn.sigmoid(x)

def _layernorm(x, axis=-1, eps=1e-05):
    m = jnp.mean(x, axis=axis, keepdims=True)
    v = jnp.var(x, axis=axis, keepdims=True)
    return (x - m) / jnp.sqrt(v + eps)

def _scatter_add(tgt, idx, src, axis=0):
    return tgt.at[idx].add(src)

def _segment_sum(src, seg, n):
    return jax.ops.segment_sum(src, seg, n)
kernel_name = 'mk_gnn_resnorm_d2_gnn_r32_3b1dcd'

def setup_inputs(seed: int=0):
    np.random.seed(seed)
    _w = jnp.asarray

    def _rec_inputs():
        import jax
        import jax.numpy as jnp
        _gk = jax.random.key(seed)
        x = -0.0003713 + 1 * jax.random.normal(jax.random.fold_in(_gk, 1), (50000, 256), jnp.float32)
        src = jax.random.randint(jax.random.fold_in(_gk, 2), (50000,), 0, 50000, jnp.int32)
        dst = jax.random.randint(jax.random.fold_in(_gk, 3), (50000,), 0, 50000, jnp.int32)
        _o = jnp.argsort(dst, stable=True)
        src = src[_o]
        dst = dst[_o]
        edge_attr_128 = -5.16925e-05 + 1.00005 * jax.random.normal(jax.random.fold_in(_gk, 11), (50000, 128), jnp.float32)
        return (x, src, dst, edge_attr_128)
    x, src, dst, edge_attr_128 = _rec_inputs()

    def _L0_gnn_setup():
        import jax, jax.numpy as jnp
        import numpy as np
        N_NODES = 50000
        N_EDGES = 25000
        IN_DIM = 256
        OUT_DIM = 256
        EDGE_DIM = 128
        BN_EPS = 1e-05
        key = jax.random.key(seed)
        ks = jax.random.split(key, 10)
        s = lambda d: 1.0 / np.sqrt(d)
        return {'x': jax.random.normal(ks[0], (N_NODES, IN_DIM), dtype=jnp.float32), 'edge_index': jax.random.randint(ks[1], (2, N_EDGES), 0, N_NODES, dtype=jnp.int64), 'edge_attr': jax.random.normal(ks[2], (N_EDGES, EDGE_DIM), dtype=jnp.float32), 'W_edge': jax.random.uniform(ks[3], (EDGE_DIM, IN_DIM), jnp.float32, -s(EDGE_DIM), s(EDGE_DIM)), 'b_edge': jnp.zeros((IN_DIM,), jnp.float32), 'W1': jax.random.uniform(ks[4], (IN_DIM, OUT_DIM), jnp.float32, -s(IN_DIM), s(IN_DIM)), 'b1': jnp.zeros((OUT_DIM,), jnp.float32), 'W2': jax.random.uniform(ks[5], (OUT_DIM, OUT_DIM), jnp.float32, -s(OUT_DIM), s(OUT_DIM)), 'b2': jnp.zeros((OUT_DIM,), jnp.float32), 'eps': jnp.float32(0.0), 'gamma': jnp.ones((OUT_DIM,), jnp.float32), 'beta': jnp.zeros((OUT_DIM,), jnp.float32)}
    _L0_gnn_all = _L0_gnn_setup()
    _L0_gnn_in = {k: v for k, v in _L0_gnn_all.items() if k in ('W_edge', 'b_edge', 'W1', 'b1', 'W2', 'b2', 'eps', 'gamma', 'beta')}
    del _L0_gnn_all

    def _L1_gnn_setup():
        import jax, jax.numpy as jnp
        import numpy as np
        N, E, D, H = (10000, 10000, 256, 256)
        key = jax.random.key(seed)
        ks = jax.random.split(key, 8)
        s = 1.0 / np.sqrt(D)
        return {'x': jax.random.normal(ks[0], (N, D), jnp.float32), 'edge_index': jax.random.randint(ks[1], (2, E), 0, N, dtype=jnp.int32), 'W1': jax.random.normal(ks[2], (H, D), jnp.float32) * s, 'b1': jnp.zeros((H,), jnp.float32), 'W2': jax.random.normal(ks[3], (H, H), jnp.float32) * s, 'b2': jnp.zeros((H,), jnp.float32), 'W3': jax.random.normal(ks[4], (H, H), jnp.float32) * s, 'b3': jnp.zeros((H,), jnp.float32)}
    _L1_gnn_all = _L1_gnn_setup()
    _L1_gnn_in = {k: v for k, v in _L1_gnn_all.items() if k in ('W1', 'b1', 'W2', 'b2', 'W3', 'b3')}
    del _L1_gnn_all
    return {'x': x, 'src': src, 'dst': dst, 'edge_attr_128': edge_attr_128, 'L0_gnn_W_edge': _L0_gnn_in['W_edge'], 'L0_gnn_b_edge': _L0_gnn_in['b_edge'], 'L0_gnn_W1': _L0_gnn_in['W1'], 'L0_gnn_b1': _L0_gnn_in['b1'], 'L0_gnn_W2': _L0_gnn_in['W2'], 'L0_gnn_b2': _L0_gnn_in['b2'], 'L0_gnn_eps': _L0_gnn_in['eps'], 'L0_gnn_gamma': _L0_gnn_in['gamma'], 'L0_gnn_beta': _L0_gnn_in['beta'], 'L1_gnn_W1': _L1_gnn_in['W1'], 'L1_gnn_b1': _L1_gnn_in['b1'], 'L1_gnn_W2': _L1_gnn_in['W2'], 'L1_gnn_b2': _L1_gnn_in['b2'], 'L1_gnn_W3': _L1_gnn_in['W3'], 'L1_gnn_b3': _L1_gnn_in['b3']}

def reference(x, src, dst, edge_attr_128, L0_gnn_W_edge, L0_gnn_b_edge, L0_gnn_W1, L0_gnn_b1, L0_gnn_W2, L0_gnn_b2, L0_gnn_eps, L0_gnn_gamma, L0_gnn_beta, L1_gnn_W1, L1_gnn_b1, L1_gnn_W2, L1_gnn_b2, L1_gnn_W3, L1_gnn_b3):
    import jax
    import jax.numpy as jnp

    def _L0_gnn_ref(x, edge_index, edge_attr, W_edge, b_edge, W1, b1, W2, b2, eps, gamma, beta):
        import jax, jax.numpy as jnp
        import numpy as np
        N_NODES = 50000
        N_EDGES = 25000
        IN_DIM = 256
        OUT_DIM = 256
        EDGE_DIM = 128
        BN_EPS = 1e-05
        src, dst = (edge_index[0], edge_index[1])
        e = edge_attr @ W_edge + b_edge
        msg = jax.nn.relu(x[src] + e)
        agg = jax.ops.segment_sum(msg, dst, num_segments=x.shape[0])
        h = (1.0 + eps) * x + agg
        h = jax.nn.relu(h @ W1 + b1) @ W2 + b2
        mean = jnp.mean(h, axis=0)
        var = jnp.var(h, axis=0)
        h = (h - mean) * jax.lax.rsqrt(var + BN_EPS) * gamma + beta
        return jax.nn.relu(h)

    def _L1_gnn_ref(x, edge_index, W1, b1, W2, b2, W3, b3):
        import jax, jax.numpy as jnp
        import numpy as np
        N, E, D, H = (10000, 10000, 256, 256)
        n = x.shape[0]
        loop = jnp.arange(n, dtype=edge_index.dtype)
        src = jnp.concatenate([edge_index[0], loop])
        dst = jnp.concatenate([edge_index[1], loop])
        deg = jax.ops.segment_sum(jnp.ones_like(dst, jnp.float32), dst, num_segments=n)
        dinv = jnp.where(deg > 0, jax.lax.rsqrt(deg), 0.0)
        norm = dinv[src] * dinv[dst]

        def layer(h, W, b):
            h = h @ W.T
            msg = h[src] * norm[:, None]
            agg = jax.ops.segment_sum(msg, dst, num_segments=n)
            return jax.nn.relu(agg + b)
        h = layer(x, W1, b1)
        h = layer(h, W2, b2)
        h = layer(h, W3, b3)
        return h
    edge_index = jnp.stack([src, dst])
    x = _layernorm(x + _L0_gnn_ref(x, edge_index, edge_attr_128, L0_gnn_W_edge, L0_gnn_b_edge, L0_gnn_W1, L0_gnn_b1, L0_gnn_W2, L0_gnn_b2, L0_gnn_eps, L0_gnn_gamma, L0_gnn_beta), axis=-1)
    x = _layernorm(x + _L1_gnn_ref(x, edge_index, L1_gnn_W1, L1_gnn_b1, L1_gnn_W2, L1_gnn_b2, L1_gnn_W3, L1_gnn_b3), axis=-1)
    return x

_drawn_inputs = setup_inputs


def setup_inputs(seed=0):
    import zlib

    import numpy as np

    out = dict(_drawn_inputs(seed))
    spreads = {'L0_gnn_b_edge': (0.0, 0.1),
     'L0_gnn_b1': (0.0, 0.1),
     'L0_gnn_b2': (0.0, 0.1),
     'L0_gnn_gamma': (1.0, 0.2),
     'L0_gnn_beta': (0.0, 0.1),
     'L1_gnn_b1': (0.0, 0.1),
     'L1_gnn_b2': (0.0, 0.1),
     'L1_gnn_b3': (0.0, 0.1)}
    factors = {}
    for name, (base, spread) in spreads.items():
        noise = np.random.default_rng([zlib.crc32(name.encode()), seed]).standard_normal(out[name].shape)
        drawn = base * np.exp(spread * noise) if base else spread * noise
        out[name] = jnp.asarray(drawn.astype(out[name].dtype))
    for name, factor in factors.items():
        out[name] = (out[name] * factor).astype(out[name].dtype)
    return out
```

```python
from contextlib import ExitStack

import concourse.bass as bass
from concourse import mybir

P = 128
D = 256
N = 50000
E = 50000
DE = 128
PAIR = 2 * P
NP = -(-N // PAIR)
NT = 2 * NP
NPAD = NP * PAIR
BLOCKS = 3
SLOTS = BLOCKS * P
EPAD = NPAD + SLOTS
TAIL = N - (NP - 1) * PAIR
NO_ROW = 1 << 20
FAR = 1 << 20
RING = 4
MAX_LAG = 7
GROUPS = -(-(NP + MAX_LAG) // RING)
PEEL = 3
LOOP_END = NP // RING - 1
BN_EPS = 1e-5
LN_EPS = 1e-5

ALU = mybir.AluOpType
ACT = mybir.ActivationFunctionType
AX = mybir.AxisListType
F32 = mybir.dt.float32
F32R = mybir.dt.float32r
F16 = mybir.dt.float16
BF16 = mybir.dt.bfloat16
I32 = mybir.dt.int32
U32 = mybir.dt.uint32


SPLIT = ("w_edge", "w1", "g1", "g2", "g3")


class Pair:

    def __init__(self, turn, slot):
        self.turn, self.slot = turn, slot
        self.q = turn * RING + slot

    def done(self, per=1):
        return (self.q + 1) * per

    def before(self, back):
        return self.q + 1 - back

    def has(self, back):
        return not isinstance(self.q, int) or self.q >= back

    def landed(self, dmas):
        return (self.turn + 1) * (16 * dmas)

    def last(self):
        return isinstance(self.q, int) and self.q == NP - 1


def pipeline(eng, step):

    def group(turn):
        for k in range(RING):
            def pair_at(lag, k=k):
                pair = Pair(turn + (k - lag) // RING, (k - lag) % RING)
                if isinstance(pair.q, int) and not 0 <= pair.q < NP:
                    return None
                return pair
            step(pair_at)

    for turn in range(PEEL):
        group(turn)
    with eng.Fori(PEEL, LOOP_END) as turn:
        group(turn)
    for turn in range(LOOP_END, GROUPS):
        group(turn)


def rows_of(dram, q):
    return dram[bass.ds(q * PAIR, PAIR), :].rearrange("(j p) d -> p j d", p=P)


class Memory:

    def __init__(self, nc, stack):
        self.nc, self.stack = nc, stack

    def sb(self, name, shape, dt=F32):
        return self.stack.enter_context(self.nc.sbuf_tensor(name, shape, dt))

    def ps(self, name, shape=(P, 2, D)):
        return self.stack.enter_context(self.nc.psum_tensor(name, list(shape), F32))

    def sem(self, name):
        return self.stack.enter_context(self.nc.semaphore(name))


def constants(nc, keep, dram):
    c = keep
    with ExitStack() as stack:
        m = Memory(nc, stack)
        weights_in = m.sem("weights_in")
        pool_done = m.sem("const_pool_done")
        dve_done = m.sem("const_dve_done")
        iota_i = m.sb("iota_i", [P, NT], I32)
        pair_b = m.sb("b_edge_twice", [2, D])
        row_hi = m.sb("b_edge_hi", [2, D])
        row_i = m.sb("row_number_i", [2, 1], I32)
        row = m.sb("row_number", [2, 1])
        with nc.Block() as block:

            @block.sync
            def _(sp):
                def load(out, in_):
                    sp.dma_start(out, in_).then_inc(weights_in, 16)

                load(c["w_edge"][:], dram["w_edge"][:, :])
                for name in ("w1", "w2", "g1", "g2", "g3"):
                    load(c[name][:], dram[name].rearrange("(c p) m -> p c m", p=P))
                for name in ("b1", "b2", "gamma", "beta"):
                    for h in range(2):
                        load(c[name][:, h:h + 1], dram[name][h * P:(h + 1) * P].rearrange("(p o) -> p o", o=1))
                sp.wait_ge(weights_in, 16 * (6 + 8))

            @block.scalar
            def _(act):
                for name in ("b_edge", "gb1", "gb2", "gb3"):
                    act.dma_start(c[name][:], dram[name].rearrange("(o d) -> o d", o=1)
                                  .broadcast_to([P, D])).then_inc(c["rows_in"], 16)
                act.dma_start(c["eps"][:], dram["eps"].rearrange("(o d) -> o d", o=1)
                              .broadcast_to([P, 1])).then_inc(c["rows_in"], 16)
                act.dma_start(pair_b[:], dram["b_edge"].rearrange("(o d) -> o d", o=1)
                              .broadcast_to([2, D])).then_inc(c["rows_in"], 16)
                act.wait_ge(c["rows_in"], 16 * 6)

            @block.gpsimd
            def _(pool):
                nc.gpsimd.memset(c["ident"][:], 0.0).then_inc(pool_done, 1)
                nc.gpsimd.memset(c["ones"][:], 1.0).then_inc(pool_done, 1)
                nc.gpsimd.memset(c["ln_eps"][:], LN_EPS).then_inc(pool_done, 1)
                nc.gpsimd.iota(iota_i[:], pattern=[[1, NT]], base=0, channel_multiplier=0).then_inc(pool_done, 1)
                nc.gpsimd.iota(row_i[:], pattern=[[0, 1]], base=0, channel_multiplier=1).then_inc(pool_done, 1)
                pool.wait_ge(pool_done, 5)
                nc.gpsimd.affine_select(out=c["below"][:], in_=c["ones"][:], compare_op=ALU.is_gt, fill=0.0,
                                        base=0, pattern=[[-1, P]], channel_multiplier=1).then_inc(pool_done, 1)
                nc.gpsimd.affine_select(out=c["ident"][:], in_=c["ident"][:], compare_op=ALU.not_equal, fill=1.0,
                                        base=0, pattern=[[-1, P]], channel_multiplier=1).then_inc(pool_done, 1)

            @block.vector
            def _(dve):
                for s in range(RING):
                    nc.vector.memset(c["rows"][:, s], 0.0)
                nc.vector.memset(c["eps1"][:, 1:2], 1.0)
                dve.wait_ge(pool_done, 7)
                nc.vector.tensor_copy(c["iota16"][:], iota_i[:])
                nc.vector.tensor_copy(c["iota32"][:], iota_i[:, 0:PAIR])
                dve.wait_ge(weights_in, 16 * (6 + 8))
                for name in SPLIT:
                    nc.vector.tensor_copy(c[name + "_hi"][:], c[name][:]).then_inc(dve_done, 1)
                dve.wait_ge(dve_done, len(SPLIT))
                for name in SPLIT:
                    nc.vector.tensor_tensor(c[name + "_lo"][:], c[name][:], c[name + "_hi"][:].bitcast(F32),
                                            ALU.subtract)
                dve.wait_ge(c["rows_in"], 16 * 6)
                nc.vector.tensor_copy(c["two_ones"][:], c["ones"][0:2, :])
                nc.vector.tensor_copy(c["b_edge2"][:], pair_b[:]).then_inc(dve_done, 1)
                nc.vector.tensor_copy(row[:], row_i[:]).then_inc(dve_done, 1)
                dve.wait_ge(dve_done, len(SPLIT) + 2)
                nc.vector.tensor_scalar(row_hi[:], c["b_edge2"][:].bitcast(F32), row[:, 0:1], None, ALU.mult)\
                    .then_inc(dve_done, 1)
                dve.wait_ge(dve_done, len(SPLIT) + 3)
                nc.vector.tensor_tensor(c["b_edge2"][:], pair_b[:], row_hi[:], ALU.subtract)


def degrees(nc, keep, dram):
    c = keep
    COLS = NT
    UNROLL = 8
    DEPTH = 4
    with ExitStack() as stack:
        m = Memory(nc, stack)
        edges = m.sb("edges_sb", [P, COLS, 2], I32)
        after = m.sb("edges_next", [P, COLS, 2], I32)
        hi_i = m.sb("hi_i", [P, COLS], I32)
        lo_i = m.sb("lo_i", [P, COLS], I32)
        hi = m.sb("hi", [P, COLS])
        lo = m.sb("lo", [P, COLS])
        hot_hi = m.sb("hot_hi", [P, DEPTH, NT], BF16)
        hot_lo = m.sb("hot_lo", [P, DEPTH, P], BF16)
        deg = m.sb("deg", [P, NT])
        deg1 = m.sb("deg1", [P, NT])
        root = m.sb("root", [P, NT])
        zero = m.sb("zero_row", [P, NT])
        counts = m.sb("counts", [P, NT])
        ends = m.sb("ends", [P, NT])
        starts = m.sb("starts", [P, NT])
        falls = m.sb("falls", [P, NT])
        nfalls = m.sb("nfalls", [P, 1])
        most = m.sb("most", [P, 2])
        fits = m.sb("fits", [P, 3])
        pair_counts = m.sb("pair_counts", [P, NP])
        root2 = m.sb("root2", [P, NT])
        hist = m.ps("hist", [P, NT])
        colsum = m.ps("colsum", [P, NT])
        fallsum = m.ps("fallsum", [P, 1])
        edges_in = m.sem("edges_in")
        split = m.sem("split")
        hot = m.sem("hot")
        used = m.sem("hot_used")
        chain = m.sem("deg_chain")
        deg_steps = m.sem("deg_steps")
        summed = m.sem("summed")
        rooted = m.sem("rooted")

        with nc.Block() as block:

            @block.sync
            def _(sp):
                sp.dma_start(edges[:], dram["edges"][0:P * COLS, :].rearrange("(p c) t -> p c t", p=P))\
                    .then_inc(edges_in, 16)
                sp.dma_start(after[:], dram["edges"][1:P * COLS + 1, :].rearrange("(p c) t -> p c t", p=P))\
                    .then_inc(edges_in, 16)

            @block.vector
            def _(dve):
                dve.wait_ge(edges_in, 32)
                nc.vector.tensor_scalar(hi_i[:], edges[:, :, 1], 7, None, ALU.arith_shift_right).then_inc(split, 1)
                nc.vector.tensor_scalar(lo_i[:], edges[:, :, 1], P - 1, None, ALU.bitwise_and).then_inc(split, 1)
                dve.wait_ge(split, 2)
                nc.vector.tensor_copy(hi[:], hi_i[:]).then_inc(split, 1)
                nc.vector.tensor_copy(lo[:], lo_i[:]).then_inc(split, 1)
                dve.wait_ge(split, 4)

                def hot_step(t, k):
                    if not isinstance(t, int) or t >= DEPTH:
                        dve.wait_ge(used, t - DEPTH + 1)
                    nc.vector.tensor_scalar(hot_lo[:, k % DEPTH], c["iota16"][:, 0:P], lo[:, bass.ds(t, 1)], None,
                                            ALU.is_equal)
                    nc.vector.tensor_scalar(hot_hi[:, k % DEPTH], c["iota16"][:], hi[:, bass.ds(t, 1)], None,
                                            ALU.is_equal).then_inc(hot, 1)

                for k in range(UNROLL):
                    hot_step(k, k)
                with dve.Fori(1, COLS // UNROLL) as i:
                    for k in range(UNROLL):
                        hot_step(i * UNROLL + k, k)

                dve.wait_ge(used, COLS)
                nc.vector.tensor_copy(deg[:], hist[:]).then_inc(deg_steps, 1)
                dve.wait_ge(deg_steps, 1)
                nc.vector.tensor_scalar(deg1[:], deg[:], 1.0, None, ALU.add).then_inc(deg_steps, 1)
                nc.vector.tensor_tensor(falls[:], edges[:, :, 1], after[:, :, 1], ALU.is_gt).then_inc(chain, 1)
                nc.vector.memset(zero[:], 0.0).then_inc(chain, 1)
                dve.wait_ge(chain, 2)
                nc.vector.tensor_reduce(nfalls[:], falls[:], AX.X, ALU.add).then_inc(chain, 1)
                dve.wait_ge(summed, 1)
                nc.vector.tensor_copy(counts[:], colsum[:]).then_inc(chain, 1)
                dve.wait_ge(chain, 4)
                nc.vector.tensor_tensor_scan(ends[:], counts[:], zero[:], 0.0, ALU.add, ALU.add).then_inc(chain, 1)
                pairs = counts[:].rearrange("p (q j) -> p q j", j=2)
                nc.vector.tensor_tensor(pair_counts[:], pairs[:, :, 0], pairs[:, :, 1], ALU.add).then_inc(chain, 1)
                dve.wait_ge(chain, 6)
                nc.vector.tensor_reduce(most[:, 0:1], pair_counts[:], AX.X, ALU.max).then_inc(chain, 1)
                nc.vector.tensor_reduce(most[:, 1:2], pairs[:, :, 0], AX.X, ALU.max).then_inc(chain, 1)
                dve.wait_ge(chain, 8)
                nc.vector.tensor_tensor(starts[:], ends[:], counts[:], ALU.subtract).then_inc(chain, 1)
                nc.vector.tensor_scalar(fits[:, 0:1], most[:, 0:1], float(SLOTS), None, ALU.is_le).then_inc(chain, 1)
                nc.vector.tensor_scalar(fits[:, 1:2], most[:, 1:2], float(SLOTS - P), None, ALU.is_le)\
                    .then_inc(chain, 1)
                dve.wait_ge(chain, 11)
                nc.vector.tensor_copy(c["starts"][:], starts[:]).then_inc(chain, 1)
                nc.vector.tensor_tensor(fits[:, 2:3], fits[:, 0:1], fits[:, 1:2], ALU.mult).then_inc(chain, 1)
                dve.wait_ge(chain, 13)
                dve.wait_ge(summed, 2)
                nc.vector.scalar_tensor_tensor(out=c["fast"][:], in0=fallsum[:], scalar=0.0, in1=fits[:, 2:3],
                                               op0=ALU.is_equal, op1=ALU.mult).then_inc(chain, 1)
                dve.wait_ge(rooted, 1)
                nc.vector.reciprocal(falls[:], root[:]).then_inc(chain, 1)
                dve.wait_ge(chain, 15)
                nc.vector.tensor_tensor(zero[:], falls[:], deg1[:], ALU.mult).then_inc(chain, 1)
                dve.wait_ge(chain, 16)
                nc.vector.tensor_tensor(root2[:], zero[:], root[:], ALU.add).then_inc(chain, 1)
                dve.wait_ge(chain, 17)
                nc.vector.tensor_scalar(root2[:], root2[:], 0.5, None, ALU.mult).then_inc(chain, 1)
                dve.wait_ge(chain, 18)
                nc.vector.reciprocal(c["dinv"][:], root2[:]).then_inc(chain, 1)
                nc.vector.tensor_copy(c["fast_i"][:], c["fast"][:]).then_inc(chain, 1)
                nc.vector.tensor_scalar(c["eps1"][:, 0:1], c["eps"][:], 1.0, None, ALU.add).then_inc(chain, 1)
                nc.vector.tensor_scalar(c["self_w"][:], c["eps"][:], c["fast"][:, 0:1], 1.0, ALU.mult, ALU.add)\
                    .then_inc(chain, 1)

            @block.tensor
            def _(pe):
                def count_step(t, k):
                    pe.wait_ge(hot, t + 1)
                    nc.tensor.matmul(hist[:], hot_lo[:, k % DEPTH], hot_hi[:, k % DEPTH],
                                     start=isinstance(t, int) and t == 0,
                                     stop=isinstance(t, int) and t == COLS - 1,
                                     skip_group_check=True).then_inc(used, 1)

                for k in range(UNROLL):
                    count_step(k, k)
                with pe.Fori(1, COLS // UNROLL) as i:
                    for k in range(UNROLL):
                        count_step(i * UNROLL + k, k)
                pe.wait_ge(deg_steps, 1)
                nc.tensor.matmul(colsum[:], c["ones"][:], deg[:], start=True, stop=True).then_inc(summed, 1)
                pe.wait_ge(chain, 3)
                nc.tensor.matmul(fallsum[:], c["ones"][:], nfalls[:], start=True, stop=True).then_inc(summed, 1)

            @block.scalar
            def _(act):
                act.wait_ge(deg_steps, 2)
                nc.scalar.activation(root[:], deg1[:], ACT.Sqrt).then_inc(rooted, 1)


def slot_tables(nc, keep, dram):
    c = keep
    with ExitStack() as stack:
        m = Memory(nc, stack)
        window = m.sb("window", [P, NP, BLOCKS, 2], I32)
        base_i = m.sb("base_i", [P, NP, BLOCKS], I32)
        base = m.sb("base", [P, NP, BLOCKS])
        place = m.sb("raw_place", [P, NP, BLOCKS])
        low = m.sb("low", [P, NP, BLOCKS])
        valid = m.sb("valid", [P, NP, BLOCKS])
        node = m.sb("node", [P, NP, BLOCKS])
        windows_in = m.sem("windows_in")
        base_ready = m.sem("base_ready")
        chain = m.sem("slot_chain")
        UNROLL = 2

        def windows(eng, first):
            with eng.Fori(0, NP // (2 * UNROLL)) as i:
                for k in range(UNROLL):
                    q = i * (2 * UNROLL) + 2 * k + first
                    start = eng.value_load(c["starts"][0:1, bass.ds(q * 2, 1)], min_val=0, max_val=E)
                    eng.dma_start(window[:, bass.ds(q, 1)].rearrange("p o b t -> p (o b) t"),
                                  dram["edges"][bass.ds(start, SLOTS), :].rearrange("(b p) t -> p b t", p=P))\
                       .then_inc(windows_in, 16)

        with nc.Block() as block:

            @block.sync
            def _(sp):
                windows(sp, 0)

            @block.scalar
            def _(act):
                windows(act, 1)

            @block.gpsimd
            def _(pool):
                nc.gpsimd.iota(base_i[:], pattern=[[PAIR, NP], [0, BLOCKS]], base=0, channel_multiplier=0)\
                    .then_inc(base_ready, 1)

            @block.vector
            def _(dve):
                dve.wait_ge(base_ready, 1)
                nc.vector.tensor_copy(base[:], base_i[:]).then_inc(chain, 1)
                dve.wait_ge(chain, 1)
                dve.wait_ge(windows_in, 16 * NP)
                nc.vector.tensor_tensor(place[:], window[:, :, :, 1], base[:], ALU.subtract).then_inc(chain, 1)
                dve.wait_ge(chain, 2)
                nc.vector.tensor_scalar(low[:], place[:], 0.0, c["fast"][:, 0:1], ALU.is_ge, ALU.mult)\
                    .then_inc(chain, 1)
                dve.wait_ge(chain, 3)
                nc.vector.scalar_tensor_tensor(out=valid[:], in0=place[:], scalar=float(PAIR), in1=low[:],
                                               op0=ALU.is_lt, op1=ALU.mult).then_inc(chain, 1)
                dve.wait_ge(chain, 4)
                nc.vector.scalar_tensor_tensor(out=node[:], in0=window[:, :, :, 0], scalar=float(-NO_ROW),
                                               in1=valid[:], op0=ALU.add, op1=ALU.mult).then_inc(chain, 1)
                nc.vector.scalar_tensor_tensor(out=base[:], in0=place[:], scalar=1.0, in1=valid[:],
                                               op0=ALU.add, op1=ALU.mult).then_inc(chain, 1)
                dve.wait_ge(chain, 6)
                nc.vector.tensor_scalar(c["node"][:], node[:], float(NO_ROW), None, ALU.add).then_inc(chain, 1)
                nc.vector.tensor_scalar(c["place"][:], base[:], -1.0, None, ALU.add).then_inc(chain, 1)


def gather_rows(nc, pool, c, pair, source, bound, index_copied, gathered, rows_free):
    s = pair.slot
    if pair.has(RING):
        pool.wait_ge(rows_free, pair.before(RING))
    nc.gpsimd.tensor_copy(c["index"][:, s], c["node"][:, bass.ds(pair.q, 1), :]).then_inc(index_copied, 1)
    pool.wait_ge(index_copied, pair.done())
    nc.gpsimd.tensor_tensor(c["spare"][:, 0:1], c["ln_eps"][:], c["ln_eps"][:], ALU.add)
    for b in range(BLOCKS):
        pool.indirect_dma_start(out=c["rows"][:, s, b], out_offset=None, in_=source[:, :],
                                in_offset=bass.IndirectOffsetOnAxis(ap=c["index"][:, s, b:b + 1], axis=0),
                                bounds_check=bound, oob_is_err=False).then_inc(gathered[s], 16)


def select_matrices(nc, c, pair, select):
    for b in range(BLOCKS):
        first = 0 if b < BLOCKS - 1 else P
        last = nc.vector.tensor_scalar(select[:, b, first:PAIR], c["iota32"][:, first:PAIR],
                                       c["place"][:, bass.ds(pair.q, 1), b], None, ALU.is_equal)
    return last


def sum_into_nodes(nc, out, select, parts, more=False):
    for j in range(2):
        terms = [(b, rows) for b in range(BLOCKS - 1 + j) for rows in parts]
        for n, (b, rows) in enumerate(terms):
            last = nc.tensor.matmul(out[:, j], select[:, b, j * P:(j + 1) * P], rows[:, b],
                                    start=n == 0, stop=n == len(terms) - 1)
    return last


def transpose_rows(nc, c, out, rows):
    for j in range(2):
        for h in range(2):
            last = nc.tensor.transpose(out[:, h, j * P:(j + 1) * P], rows[:, j, h * P:(h + 1) * P], c["ident"][:])
    return last


def products(parts, weight):
    if len(parts) == 1:
        return [(parts[0], weight[0])]
    (hi, lo), (w_hi, w_lo) = parts, weight
    return [(hi, w_hi), (lo, w_hi), (hi, w_lo)]


def dense_rows(nc, out, parts, weight):
    terms = [(h, a, w) for h in range(2) for a, w in products(parts, weight)]
    for j in range(2):
        for n, (h, a, w) in enumerate(terms):
            last = nc.tensor.matmul(out[:, j], a[:, h, j * P:(j + 1) * P], w[:, h],
                                    start=n == 0, stop=n == len(terms) - 1)
    return last


def dense_cols(nc, out, parts, weight):
    terms = [(h, a, w) for h in range(2) for a, w in products(parts, weight)]
    for m in range(2):
        for n, (h, a, w) in enumerate(terms):
            last = nc.tensor.matmul(out[:, m], w[:, h, m * P:(m + 1) * P], a[:, h],
                                    start=n == 0, stop=n == len(terms) - 1)
    return last


def load_own(sp, fast, out, source, base, pair, landed, slot_free):
    for ran, rows in ((1, source), (0, base)):
        with sp.If(fast == ran):
            if pair.has(RING):
                sp.wait_ge(slot_free, pair.before(RING))
            sp.dma_start(out, rows_of(rows, pair.q)).then_inc(landed, 16)


def layer_stats(nc, dve, pair, rows, stats, mv, stats_done, var_ready, spare):
    for j in range(2):
        last = nc.vector.bn_stats(stats[:, j], rows[:, j])
    last.then_inc(stats_done, 1)
    dve.wait_ge(stats_done, pair.done())
    nc.vector.memset(spare, 0.0)
    for j in range(2):
        last = nc.vector.bn_aggr(mv[:, j], stats[:, j])
    last.then_inc(var_ready, 1)


def general_sum(nc, keep, dram, number, source, gin):
    c = keep
    base = dram["base"]
    sems = c["general_sems"]
    (copy_in, scaled, copy_out, block_in, ids_ready, spread, turned, same_ready, index_steps, index_ready,
     attr_turned, attr_copied, edge_done, msg_steps, msg_ready, summed, source_in, current_in, added,
     scattered) = sems
    done_pairs, done_blocks = number * NP, number * NT
    loads = 2 if gin else 1
    with ExitStack() as stack:
        m = Memory(nc, stack)
        name = f"gen{number}_"
        own = m.sb(name + "own", [P, 2, D])
        own_out = m.sb(name + "own_out", [P, 2, D])
        ids = m.sb(name + "ids", [P, 2], I32)
        src = m.sb(name + "src", [P, 1], U32)
        dst = m.sb(name + "dst", [P, 1])
        dst_cols = m.sb(name + "dst_cols", [P, P])
        same = m.sb(name + "same", [P, P])
        earlier = m.sb(name + "earlier", [P, P])
        count = m.sb(name + "count", [P, 1])
        first = m.sb(name + "first", [P, 1])
        index_f = m.sb(name + "index_f", [P, 1])
        index = m.sb(name + "index", [P, 1], U32)
        attr = m.sb(name + "attr", [P, DE])
        attr_t = m.sb(name + "attr_t", [P, P])
        msg0 = m.sb(name + "msg0", [P, D])
        msg1 = m.sb(name + "msg1", [P, D])
        msg = m.sb(name + "msg", [P, D])
        total = m.sb(name + "total", [P, D])
        rows = c["rows"][:, 0, 0]
        current = c["rows"][:, 0, 1]
        dst_ps = m.ps(name + "dst_ps", [P, P])
        attr_ps = m.ps(name + "attr_ps", [P, P])
        edge_ps = m.ps(name + "edge_ps", [P, D])
        sum_ps = m.ps(name + "sum_ps", [P, D])

        with nc.Block() as block:

            @block.sync
            def _(sp):
                fast = sp.value_load(c["fast_i"][0:1, 0:1], min_val=0, max_val=1)
                with sp.If(fast == 0):
                    def copy_rows(q):
                        sp.dma_start(own[:], rows_of(source, q)).then_inc(copy_in, 16)
                        sp.wait_ge(scaled, q + (done_pairs + 1))
                        sp.dma_start(rows_of(base, q), own_out[:]).then_inc(copy_out, 16)

                    def load_block(e):
                        sp.dma_start(ids[:], dram["edges"][bass.ds(e * P, P), :]).then_inc(block_in, 16)
                        if gin:
                            sp.dma_start(attr[:], dram["edge_attr"][bass.ds(e * P, P), :]).then_inc(block_in, 16)

                    copy_rows(0)
                    with sp.Fori(1, NP) as q:
                        sp.wait_ge(copy_out, (q + done_pairs) * 16)
                        copy_rows(q)
                    sp.wait_ge(copy_out, (done_pairs + NP) * 16)
                    load_block(0)
                    with sp.Fori(1, NT) as e:
                        sp.wait_ge(scattered, (e + done_blocks) * 16)
                        load_block(e)
                    sp.wait_ge(scattered, (done_blocks + NT) * 16)

            @block.gpsimd
            def _(pool):
                bound = pool.to_reg(NPAD - 1)
                fast = pool.value_load(c["fast_i"][0:1, 0:1], min_val=0, max_val=1)

                def carry():
                    nc.gpsimd.tensor_tensor(c["spare"][:, 0:1], c["ln_eps"][:], c["ln_eps"][:], ALU.add)

                with pool.If(fast == 0):
                    with pool.Fori(0, NT) as e:
                        turn = e + (done_blocks + 1)
                        pool.wait_ge(ids_ready, turn)
                        carry()
                        pool.indirect_dma_start(out=rows, out_offset=None, in_=source[:, :],
                                                in_offset=bass.IndirectOffsetOnAxis(ap=src[:, 0:1], axis=0),
                                                bounds_check=bound, oob_is_err=False).then_inc(source_in, 16)
                        pool.wait_ge(index_ready, turn)
                        carry()
                        pool.indirect_dma_start(out=current, out_offset=None, in_=base[:, :],
                                                in_offset=bass.IndirectOffsetOnAxis(ap=index[:, 0:1], axis=0),
                                                bounds_check=bound, oob_is_err=False).then_inc(current_in, 16)
                        pool.wait_ge(added, turn)
                        carry()
                        pool.indirect_dma_start(out=base[:, :], in_=total[:], in_offset=None,
                                                out_offset=bass.IndirectOffsetOnAxis(ap=index[:, 0:1], axis=0),
                                                bounds_check=bound, oob_is_err=False).then_inc(scattered, 16)

            @block.vector
            def _(dve):
                fast = dve.value_load(c["fast_i"][0:1, 0:1], min_val=0, max_val=1)
                with dve.If(fast == 0):
                    with dve.Fori(0, NP) as q:
                        dve.wait_ge(copy_in, (q + (done_pairs + 1)) * 16)
                        factor = c["eps1"][:, 0:1] if gin else c["eps1"][:, 1:2]
                        nc.vector.tensor_scalar(own_out[:], own[:], factor, None, ALU.mult).then_inc(scaled, 1)
                    with dve.Fori(0, NT) as e:
                        turn = e + (done_blocks + 1)
                        dve.wait_ge(block_in, (e + 1) * (16 * loads) + (0 if gin else 16 * (done_blocks + NT)))
                        nc.vector.tensor_copy(src[:], ids[:, 0:1])
                        nc.vector.tensor_copy(dst[:], ids[:, 1:2]).then_inc(ids_ready, 1)
                        dve.wait_ge(ids_ready, turn)
                        nc.vector.tensor_scalar(dst_cols[:], c["ones"][:], dst[:, 0:1], None, ALU.mult)\
                            .then_inc(spread, 1)
                        dve.wait_ge(turned, turn)
                        nc.vector.tensor_scalar(same[:], dst_ps[:], dst[:, 0:1], None, ALU.is_equal)\
                            .then_inc(same_ready, 1)
                        dve.wait_ge(same_ready, turn)
                        nc.vector.tensor_tensor(earlier[:], same[:], c["below"][:], ALU.mult).then_inc(index_steps, 1)
                        dve.wait_ge(index_steps, turn * 4 - 3)
                        nc.vector.tensor_reduce(count[:], earlier[:], AX.X, ALU.add).then_inc(index_steps, 1)
                        dve.wait_ge(index_steps, turn * 4 - 2)
                        nc.vector.tensor_scalar(first[:], count[:], 0.0, None, ALU.is_equal).then_inc(index_steps, 1)
                        dve.wait_ge(index_steps, turn * 4 - 1)
                        nc.vector.scalar_tensor_tensor(out=index_f[:], in0=dst[:], scalar=float(-NO_ROW),
                                                       in1=first[:], op0=ALU.add, op1=ALU.mult)\
                            .then_inc(index_steps, 1)
                        dve.wait_ge(index_steps, turn * 4)
                        nc.vector.tensor_scalar(index[:], index_f[:], float(NO_ROW), None, ALU.add)\
                            .then_inc(index_ready, 1)
                        dve.wait_ge(source_in, turn * 16)
                        if gin:
                            dve.wait_ge(edge_done, e + 1)
                            nc.vector.tensor_tensor(msg0[:], edge_ps[:], rows, ALU.add).then_inc(msg_steps, 1)
                            dve.wait_ge(msg_steps, e * 2 + 1)
                            nc.vector.tensor_tensor(msg1[:], msg0[:], c["b_edge"][:], ALU.add).then_inc(msg_steps, 1)
                            dve.wait_ge(msg_steps, e * 2 + 2)
                            nc.vector.tensor_scalar(msg[:], msg1[:], 0.0, None, ALU.max).then_inc(msg_ready, 1)
                        else:
                            nc.vector.tensor_copy(msg[:], rows).then_inc(msg_ready, 1)
                        dve.wait_ge(summed, turn)
                        dve.wait_ge(current_in, turn * 16)
                        nc.vector.tensor_tensor(total[:], sum_ps[:], current, ALU.add).then_inc(added, 1)

            @block.tensor
            def _(pe):
                fast = pe.value_load(c["fast_i"][0:1, 0:1], min_val=0, max_val=1)
                with pe.If(fast == 0):
                    with pe.Fori(0, NT) as e:
                        turn = e + (done_blocks + 1)
                        pe.wait_ge(spread, turn)
                        nc.tensor.transpose(dst_ps[:], dst_cols[:], c["ident"][:]).then_inc(turned, 1)
                        if gin:
                            pe.wait_ge(block_in, (e + 1) * 32)
                            nc.tensor.transpose(attr_ps[:], attr[:], c["ident"][:]).then_inc(attr_turned, 1)
                            pe.wait_ge(attr_copied, e + 1)
                            nc.tensor.matmul(edge_ps[:], attr_t[:], c["w_edge"][:], start=True, stop=True)\
                                .then_inc(edge_done, 1)
                        pe.wait_ge(msg_ready, turn)
                        pe.wait_ge(same_ready, turn)
                        nc.tensor.matmul(sum_ps[:], same[:], msg[:], start=True, stop=True).then_inc(summed, 1)

            if gin:
                @block.scalar
                def _(act):
                    fast = act.value_load(c["fast_i"][0:1, 0:1], min_val=0, max_val=1)
                    with act.If(fast == 0):
                        with act.Fori(0, NT) as e:
                            act.wait_ge(attr_turned, e + 1)
                            nc.scalar.copy(attr_t[:], attr_ps[:]).then_inc(attr_copied, 1)


def gin_pass(nc, keep, dram):
    c = keep
    with ExitStack() as stack:
        m = Memory(nc, stack)
        attr = m.sb("attr", [P, RING, BLOCKS, DE])
        own = m.sb("own", [P, RING, 2, D])
        attr_hi = m.sb("attr_hi", [P, 2, BLOCKS * P], F32R)
        attr_lo = m.sb("attr_lo", [P, 2, BLOCKS * P], F32R)
        raw = m.sb("raw", [P, 2, BLOCKS, D])
        msg_hi = m.sb("msg_hi", [P, 2, BLOCKS, D], F32R)
        msg_lo = m.sb("msg_lo", [P, 2, BLOCKS, D], F32R)
        select = m.sb("gin_select", [P, 2, BLOCKS, PAIR], F32R)
        h0 = m.sb("h0", [P, 2, 2, D])
        h0t_hi = m.sb("h0t_hi", [P, 2, 2, D], F32R)
        h0t_lo = m.sb("h0t_lo", [P, 2, 2, D], F32R)
        h1t = m.sb("h1t", [P, 2, 2, D])
        h2t = m.sb("h2t", [P, RING, 2, D])
        attr_ps = m.ps("attr_ps", [P, 512])
        edge_ps = m.ps("edge_ps", [P, 4, D])
        agg_ps = m.ps("agg_ps")
        h0t_ps = m.ps("h0t_ps")
        h1t_ps = m.ps("h1t_ps")
        h2t_ps = m.ps("h2t_ps")
        loaded = [m.sem(f"gin_loaded{s}") for s in range(RING)]
        gathered = [m.sem(f"gin_gathered{s}") for s in range(RING)]
        stored = [m.sem(f"gin_stored{s}") for s in range(RING)]
        names = ("index_copied attr_turned attr_rounded attr_split edge_done select_done rows_added msg_rounded "
                 "msg_split agg_done h0_done h0_turned h0_rounded h0_split h1_done h1_ready h2_done h2_ready stats_done")
        (index_copied, attr_turned, attr_rounded, attr_split, edge_done, select_done, rows_added, msg_rounded,
         msg_split, agg_done, h0_done, h0_turned, h0_rounded, h0_split, h1_done, h1_ready, h2_done, h2_ready,
         stats_done) = (m.sem("gin_" + n) for n in names.split())

        with nc.Block() as block:

            @block.sync
            def _(sp):
                fast = sp.value_load(c["fast_i"][0:1, 0:1], min_val=0, max_val=1)

                def step(at):
                    if pair := at(0):
                        s = pair.slot
                        start = sp.value_load(c["starts"][0:1, bass.ds(pair.q * 2, 1)], min_val=0, max_val=E)
                        if pair.has(RING):
                            sp.wait_ge(attr_turned, pair.before(RING))
                        sp.dma_start(attr[:, s], dram["edge_attr"][bass.ds(start, SLOTS), :]
                                     .rearrange("(b p) k -> p b k", p=P)).then_inc(loaded[s], 16)
                        load_own(sp, fast, own[:, s], dram["x"], dram["base"], pair, loaded[s], h0_done)
                    if pair := at(6):
                        sp.wait_ge(h2_ready, pair.done())
                        sp.dma_start(dram["h2"][bass.ds(pair.q, 1)].rearrange("o p c n -> p (o c) n"),
                                     h2t[:, pair.slot]).then_inc(stored[pair.slot], 16)

                pipeline(sp, step)
                for s in range(RING):
                    sp.wait_ge(stored[s], 16 * (NP // RING))

            @block.gpsimd
            def _(pool):
                bound = pool.to_reg(NPAD - 1)

                def step(at):
                    if pair := at(0):
                        gather_rows(nc, pool, c, pair, dram["x"], bound, index_copied, gathered, rows_added)

                pipeline(pool, step)

            @block.tensor
            def _(pe):
                def step(at):
                    if pair := at(3):
                        b = pair.slot % 2
                        pe.wait_ge(msg_split, pair.done())
                        pe.wait_ge(select_done, pair.done())
                        if pair.has(1):
                            pe.wait_ge(h0_done, pair.before(1))
                        sum_into_nodes(nc, agg_ps, select[:, b], [msg_hi[:, b], msg_lo[:, b]]).then_inc(agg_done, 1)
                    if pair := at(2):
                        b = pair.slot % 2
                        pe.wait_ge(attr_split, pair.done())
                        if pair.has(1):
                            pe.wait_ge(rows_added, pair.before(1))
                        terms = products([attr_hi[:, b], attr_lo[:, b]], [c["w_edge_hi"], c["w_edge_lo"]])
                        for k in range(BLOCKS):
                            nc.tensor.matmul(edge_ps[:, k], c["two_ones"][:], c["b_edge2"][:], start=True, stop=False)
                            for n, (a, w) in enumerate(terms):
                                last = nc.tensor.matmul(edge_ps[:, k], a[:, k * P:(k + 1) * P], w[:],
                                                        start=False, stop=n == len(terms) - 1)
                        last.then_inc(edge_done, 1)
                    if pair := at(4):
                        b = pair.slot % 2
                        pe.wait_ge(h0_split, pair.done())
                        if pair.has(1):
                            pe.wait_ge(h1_ready, pair.before(1))
                        dense_cols(nc, h1t_ps, [h0t_hi[:, b], h0t_lo[:, b]], [c["w1_hi"], c["w1_lo"]])\
                            .then_inc(h1_done, 1)
                    if pair := at(1):
                        s = pair.slot
                        pe.wait_ge(loaded[s], pair.landed(2))
                        if pair.has(1):
                            pe.wait_ge(attr_split, pair.before(1))
                        for k in range(BLOCKS):
                            last = nc.tensor.transpose(attr_ps[:, k * P:(k + 1) * P], attr[:, s, k], c["ident"][:])
                        last.then_inc(attr_turned, 1)
                    if pair := at(3):
                        pe.wait_ge(h0_done, pair.done())
                        if pair.has(1):
                            pe.wait_ge(h0_split, pair.before(1))
                        transpose_rows(nc, c, h0t_ps, h0[:, pair.slot % 2]).then_inc(h0_turned, 1)
                    if pair := at(5):
                        pe.wait_ge(h1_ready, pair.done())
                        if pair.has(1):
                            pe.wait_ge(h2_ready, pair.before(1))
                        dense_cols(nc, h2t_ps, [h1t[:, pair.slot % 2]], [c["w2"]]).then_inc(h2_done, 1)

                pipeline(pe, step)

            @block.scalar
            def _(act):
                def step(at):
                    if pair := at(2):
                        b = pair.slot % 2
                        act.wait_ge(rows_added, pair.done())
                        if pair.has(2):
                            act.wait_ge(agg_done, pair.before(2))
                        nc.scalar.activation(msg_hi[:, b], raw[:, b], ACT.Relu).then_inc(msg_rounded, 1)
                    if pair := at(4):
                        b = pair.slot % 2
                        act.wait_ge(h1_done, pair.done())
                        if pair.has(2):
                            act.wait_ge(h2_done, pair.before(2))
                        for h in range(2):
                            last = nc.scalar.activation(h1t[:, b, h], h1t_ps[:, h], ACT.Relu, bias=c["b1"][:, h:h + 1])
                        last.then_inc(h1_ready, 1)
                    if pair := at(1):
                        b = pair.slot % 2
                        act.wait_ge(attr_turned, pair.done())
                        if pair.has(2):
                            act.wait_ge(edge_done, pair.before(2))
                        nc.scalar.copy(attr_hi[:, b], attr_ps[:, 0:BLOCKS * P]).then_inc(attr_rounded, 1)
                    if pair := at(3):
                        b = pair.slot % 2
                        act.wait_ge(h0_turned, pair.done())
                        if pair.has(2):
                            act.wait_ge(h1_done, pair.before(2))
                        nc.scalar.copy(h0t_hi[:, b], h0t_ps[:]).then_inc(h0_rounded, 1)
                    if pair := at(5):
                        s = pair.slot
                        act.wait_ge(h2_done, pair.done())
                        if pair.has(RING):
                            act.wait_ge(stored[s], pair.turn * 16)
                            act.wait_ge(stats_done, pair.before(RING))
                        for h in range(2):
                            last = nc.scalar.activation(h2t[:, s, h], h2t_ps[:, h], ACT.Identity,
                                                        bias=c["b2"][:, h:h + 1])
                        last.then_inc(h2_ready, 1)

                pipeline(act, step)

            @block.vector
            def _(dve):
                def step(at):
                    if pair := at(3):
                        b, s = pair.slot % 2, pair.slot
                        dve.wait_ge(agg_done, pair.done())
                        dve.wait_ge(loaded[s], pair.landed(2))
                        if pair.has(2):
                            dve.wait_ge(h0_turned, pair.before(2))
                        nc.vector.scalar_tensor_tensor(out=h0[:, b], in0=own[:, s], scalar=c["self_w"][:, 0:1],
                                                       in1=agg_ps[:], op0=ALU.mult, op1=ALU.add).then_inc(h0_done, 1)
                    if pair := at(2):
                        b, s = pair.slot % 2, pair.slot
                        if pair.has(2):
                            dve.wait_ge(agg_done, pair.before(2))
                        select_matrices(nc, c, pair, select[:, b]).then_inc(select_done, 1)
                        dve.wait_ge(edge_done, pair.done())
                        dve.wait_ge(gathered[s], pair.landed(BLOCKS))
                        if pair.has(2):
                            dve.wait_ge(msg_rounded, pair.before(2))
                            dve.wait_ge(msg_split, pair.before(2))
                        nc.vector.tensor_tensor(raw[:, b], edge_ps[:, 0:BLOCKS], c["rows"][:, s], ALU.add)\
                            .then_inc(rows_added, 1)
                    if pair := at(6):
                        dve.wait_ge(h2_ready, pair.done())
                        nodes = TAIL if pair.last() else PAIR
                        for h in range(2):
                            last = nc.vector.bn_stats(c["bn_stats"][:, h, bass.ds(pair.q, 1), :],
                                                      h2t[:, pair.slot, h, 0:nodes])
                        last.then_inc(stats_done, 1)
                    if pair := at(2):
                        b = pair.slot % 2
                        dve.wait_ge(msg_rounded, pair.done())
                        nc.vector.scalar_tensor_tensor(out=msg_lo[:, b], in0=raw[:, b], scalar=0.0,
                                                       in1=msg_hi[:, b].bitcast(F32), op0=ALU.max, op1=ALU.subtract)\
                            .then_inc(msg_split, 1)
                    if pair := at(1):
                        b = pair.slot % 2
                        dve.wait_ge(attr_rounded, pair.done())
                        if pair.has(2):
                            dve.wait_ge(edge_done, pair.before(2))
                        nc.vector.tensor_tensor(attr_lo[:, b], attr_ps[:, 0:BLOCKS * P], attr_hi[:, b].bitcast(F32),
                                                ALU.subtract).then_inc(attr_split, 1)
                    if pair := at(3):
                        b = pair.slot % 2
                        dve.wait_ge(h0_rounded, pair.done())
                        if pair.has(2):
                            dve.wait_ge(h1_done, pair.before(2))
                        nc.vector.tensor_tensor(h0t_lo[:, b], h0t_ps[:], h0t_hi[:, b].bitcast(F32),
                                                ALU.subtract).then_inc(h0_split, 1)

                pipeline(dve, step)


def batch_norm_scale(nc, keep):
    c = keep
    with ExitStack() as stack:
        m = Memory(nc, stack)
        mv = m.sb("bn_mv", [P, 2, 2])
        sd = m.sb("bn_sd", [P, 2])
        rs = m.sb("bn_rs", [P, 2])
        ma = m.sb("bn_ma", [P, 2])
        chain = m.sem("bn_chain")
        rooted = m.sem("bn_rooted")
        with nc.Block() as block:

            @block.vector
            def _(dve):
                for h in range(2):
                    nc.vector.bn_aggr(mv[:, h], c["bn_stats"][:, h].rearrange("p a b -> p (a b)")).then_inc(chain, 1)
                dve.wait_ge(rooted, 1)
                nc.vector.reciprocal(rs[:], sd[:]).then_inc(chain, 1)
                dve.wait_ge(chain, 3)
                nc.vector.tensor_tensor(c["bn_a"][:], c["gamma"][:], rs[:], ALU.mult).then_inc(chain, 1)
                dve.wait_ge(chain, 4)
                nc.vector.tensor_tensor(ma[:], mv[:, :, 0], c["bn_a"][:], ALU.mult).then_inc(chain, 1)
                dve.wait_ge(chain, 5)
                nc.vector.tensor_tensor(c["bn_c"][:], c["beta"][:], ma[:], ALU.subtract).then_inc(chain, 1)

            @block.scalar
            def _(act):
                act.wait_ge(chain, 2)
                nc.scalar.activation(sd[:], mv[:, :, 1], ACT.Sqrt, bias=c["ln_eps"][:, 0:1]).then_inc(rooted, 1)


def norm_pass(nc, keep, dram):
    c = keep
    with ExitStack() as stack:
        m = Memory(nc, stack)
        h2t = m.sb("h2t_in", [P, RING, 2, D])
        own = m.sb("x_sb", [P, RING, 2, D])
        zt = m.sb("zt", [P, 2, 2, D])
        res = m.sb("res", [P, 2, 2, D])
        x1 = m.sb("x1", [P, RING, 2, D])
        x1t_hi = m.sb("x1t_hi", [P, 2, 2, D], F32R)
        x1t_lo = m.sb("x1t_lo", [P, 2, 2, D], F32R)
        g = m.sb("g_out", [P, RING, 2, D])
        stats = m.sb("ln_stats", [P, 2, 2, 6])
        mv = m.sb("ln_mv", [P, 2, 2, 2])
        sd = m.sb("ln_sd", [P, 2, 2])
        rs = m.sb("ln_rs", [P, 2, 2])
        z_ps = m.ps("z_ps")
        x1t_ps = m.ps("x1t_ps")
        g_ps = m.ps("g_ps")
        loaded = [m.sem(f"nrm_loaded{s}") for s in range(RING)]
        stored = [m.sem(f"nrm_stored{s}") for s in range(RING)]
        names = ("z_ready z_turned res_added stats_done var_ready sd_ready rs_ready x1_ready x1_turned x1_rounded "
                 "x1_split dense_done g_ready")
        (z_ready, z_turned, res_added, stats_done, var_ready, sd_ready, rs_ready, x1_ready, x1_turned, x1_rounded,
         x1_split, dense_done, g_ready) = (m.sem("nrm_" + n) for n in names.split())

        with nc.Block() as block:

            @block.sync
            def _(sp):
                def step(at):
                    if pair := at(0):
                        s = pair.slot
                        if pair.has(RING):
                            sp.wait_ge(z_ready, pair.before(RING))
                            sp.wait_ge(res_added, pair.before(RING))
                        sp.dma_start(h2t[:, s], dram["h2"][bass.ds(pair.q, 1)].rearrange("o p c n -> p (o c) n"))\
                            .then_inc(loaded[s], 16)
                        sp.dma_start(own[:, s], rows_of(dram["x"], pair.q)).then_inc(loaded[s], 16)
                    if pair := at(5):
                        sp.wait_ge(x1_ready, pair.done())
                        sp.dma_start(rows_of(dram["x1"], pair.q), x1[:, pair.slot]).then_inc(stored[pair.slot], 16)
                    if pair := at(7):
                        sp.wait_ge(g_ready, pair.done())
                        sp.dma_start(rows_of(dram["ga"], pair.q), g[:, pair.slot]).then_inc(stored[pair.slot], 16)

                pipeline(sp, step)
                for s in range(RING):
                    sp.wait_ge(stored[s], 32 * (NP // RING))

            @block.scalar
            def _(act):
                def step(at):
                    if pair := at(2):
                        b, s = pair.slot % 2, pair.slot
                        act.wait_ge(loaded[s], pair.landed(2))
                        if pair.has(2):
                            act.wait_ge(z_turned, pair.before(2))
                        for h in range(2):
                            last = nc.scalar.activation(zt[:, b, h], h2t[:, s, h], ACT.Relu,
                                                        bias=c["bn_c"][:, h:h + 1], scale=c["bn_a"][:, h:h + 1])
                        last.then_inc(z_ready, 1)
                    if pair := at(6):
                        s = pair.slot
                        act.wait_ge(dense_done, pair.done())
                        if pair.has(RING):
                            act.wait_ge(stored[s], pair.turn * 32)
                        for j in range(2):
                            last = nc.scalar.activation(g[:, s, j], g_ps[:, j], ACT.Identity,
                                                        scale=c["dinv"][:, bass.ds(pair.q * 2 + j, 1)])
                        last.then_inc(g_ready, 1)
                    if pair := at(5):
                        b = pair.slot % 2
                        act.wait_ge(x1_turned, pair.done())
                        if pair.has(2):
                            act.wait_ge(dense_done, pair.before(2))
                        nc.scalar.copy(x1t_hi[:, b], x1t_ps[:]).then_inc(x1_rounded, 1)
                    if pair := at(3):
                        b = pair.slot % 2
                        act.wait_ge(var_ready, pair.done())
                        nc.scalar.activation(sd[:, b], mv[:, b, :, 1], ACT.Sqrt, bias=c["ln_eps"][:, 0:1])\
                            .then_inc(sd_ready, 1)

                pipeline(act, step)

            @block.tensor
            def _(pe):
                def step(at):
                    if pair := at(3):
                        pe.wait_ge(z_ready, pair.done())
                        if pair.has(1):
                            pe.wait_ge(res_added, pair.before(1))
                        zh = zt[:, pair.slot % 2]
                        for j in range(2):
                            for h in range(2):
                                last = nc.tensor.transpose(z_ps[:, j, h * P:(h + 1) * P], zh[:, h, j * P:(j + 1) * P],
                                                           c["ident"][:])
                        last.then_inc(z_turned, 1)
                    if pair := at(6):
                        b = pair.slot % 2
                        pe.wait_ge(x1_split, pair.done())
                        if pair.has(1):
                            pe.wait_ge(g_ready, pair.before(1))
                        dense_rows(nc, g_ps, [x1t_hi[:, b], x1t_lo[:, b]], [c["g1_hi"], c["g1_lo"]])\
                            .then_inc(dense_done, 1)
                    if pair := at(5):
                        pe.wait_ge(x1_ready, pair.done())
                        if pair.has(1):
                            pe.wait_ge(x1_split, pair.before(1))
                        transpose_rows(nc, c, x1t_ps, x1[:, pair.slot]).then_inc(x1_turned, 1)

                pipeline(pe, step)

            @block.vector
            def _(dve):
                def step(at):
                    if pair := at(4):
                        b, s = pair.slot % 2, pair.slot
                        dve.wait_ge(sd_ready, pair.done())
                        nc.vector.reciprocal(rs[:, b], sd[:, b]).then_inc(rs_ready, 1)
                        dve.wait_ge(rs_ready, pair.done())
                        if pair.has(RING):
                            dve.wait_ge(stored[s], pair.turn * 32)
                            dve.wait_ge(x1_turned, pair.before(RING))
                        for j in range(2):
                            last = nc.vector.tensor_scalar(x1[:, s, j], res[:, b, j], mv[:, b, j, 0:1],
                                                           rs[:, b, j:j + 1], ALU.subtract, ALU.mult)
                        last.then_inc(x1_ready, 1)
                    if pair := at(3):
                        b, s = pair.slot % 2, pair.slot
                        dve.wait_ge(z_turned, pair.done())
                        dve.wait_ge(loaded[s], pair.landed(2))
                        if pair.has(2):
                            dve.wait_ge(x1_ready, pair.before(2))
                        nc.vector.tensor_tensor(res[:, b], z_ps[:], own[:, s], ALU.add).then_inc(res_added, 1)
                        dve.wait_ge(res_added, pair.done())
                        layer_stats(nc, dve, pair, res[:, b], stats[:, b], mv[:, b], stats_done, var_ready,
                                    c["spare"][:, 1:2])
                    if pair := at(5):
                        b = pair.slot % 2
                        dve.wait_ge(x1_rounded, pair.done())
                        if pair.has(2):
                            dve.wait_ge(dense_done, pair.before(2))
                        nc.vector.tensor_tensor(x1t_lo[:, b], x1t_ps[:], x1t_hi[:, b].bitcast(F32),
                                                ALU.subtract).then_inc(x1_split, 1)

                pipeline(dve, step)


def gcn_pass(nc, keep, dram, name, source, target, bias, weight):
    c = keep
    with ExitStack() as stack:
        m = Memory(nc, stack)
        own = m.sb(name + "own", [P, RING, 2, D])
        rows_hi = m.sb(name + "rows_hi", [P, 2, BLOCKS, D], F32R)
        rows_lo = m.sb(name + "rows_lo", [P, 2, BLOCKS, D], F32R)
        select = m.sb(name + "select", [P, 2, BLOCKS, PAIR], F32R)
        tot = m.sb(name + "tot", [P, 2, 2, D])
        h = m.sb(name + "h", [P, 2, 2, D])
        ht = m.sb(name + "ht", [P, 2, 2, D])
        g = m.sb(name + "g", [P, RING, 2, D])
        agg_ps = m.ps(name + "agg_ps")
        ht_ps = m.ps(name + "ht_ps")
        g_ps = m.ps(name + "g_ps")
        loaded = [m.sem(f"{name}loaded{s}") for s in range(RING)]
        gathered = [m.sem(f"{name}gathered{s}") for s in range(RING)]
        stored = [m.sem(f"{name}stored{s}") for s in range(RING)]
        names = ("index_copied rows_rounded rows_split select_done agg_done total_done h_ready h_turned h_copied "
                 "dense_done g_ready")
        (index_copied, rows_rounded, rows_split, select_done, agg_done, total_done, h_ready, h_turned, h_copied,
         dense_done, g_ready) = (m.sem(name + n) for n in names.split())

        with nc.Block() as block:

            @block.sync
            def _(sp):
                fast = sp.value_load(c["fast_i"][0:1, 0:1], min_val=0, max_val=1)

                def step(at):
                    if pair := at(0):
                        s = pair.slot
                        load_own(sp, fast, own[:, s], source, dram["base"], pair, loaded[s], total_done)
                    if pair := at(6):
                        s = pair.slot
                        sp.wait_ge(g_ready, pair.done())
                        sp.dma_start(rows_of(target, pair.q), g[:, s]).then_inc(stored[s], 16)

                pipeline(sp, step)
                for s in range(RING):
                    sp.wait_ge(stored[s], 16 * (NP // RING))

            @block.gpsimd
            def _(pool):
                bound = pool.to_reg(NPAD - 1)

                def step(at):
                    if pair := at(0):
                        gather_rows(nc, pool, c, pair, source, bound, index_copied, gathered, rows_split)

                pipeline(pool, step)

            @block.tensor
            def _(pe):
                def step(at):
                    if pair := at(3):
                        b = pair.slot % 2
                        pe.wait_ge(rows_split, pair.done())
                        pe.wait_ge(select_done, pair.done())
                        if pair.has(1):
                            pe.wait_ge(total_done, pair.before(1))
                        sum_into_nodes(nc, agg_ps, select[:, b], [rows_hi[:, b], rows_lo[:, b]]).then_inc(agg_done, 1)
                    if pair := at(5):
                        pe.wait_ge(h_copied, pair.done())
                        if pair.has(1):
                            pe.wait_ge(g_ready, pair.before(1))
                        dense_rows(nc, g_ps, [ht[:, pair.slot % 2]], [weight]).then_inc(dense_done, 1)
                    if pair := at(4):
                        pe.wait_ge(h_ready, pair.done())
                        if pair.has(1):
                            pe.wait_ge(h_copied, pair.before(1))
                        transpose_rows(nc, c, ht_ps, h[:, pair.slot % 2]).then_inc(h_turned, 1)

                pipeline(pe, step)

            @block.vector
            def _(dve):
                def step(at):
                    if pair := at(2):
                        b, s = pair.slot % 2, pair.slot
                        if pair.has(2):
                            dve.wait_ge(agg_done, pair.before(2))
                        select_matrices(nc, c, pair, select[:, b]).then_inc(select_done, 1)
                    if pair := at(3):
                        b, s = pair.slot % 2, pair.slot
                        dve.wait_ge(agg_done, pair.done())
                        dve.wait_ge(loaded[s], pair.landed(1))
                        nc.vector.tensor_tensor(tot[:, b], agg_ps[:], own[:, s], ALU.add).then_inc(total_done, 1)
                        dve.wait_ge(total_done, pair.done())
                        if pair.has(2):
                            dve.wait_ge(h_turned, pair.before(2))
                        for j in range(2):
                            last = nc.vector.scalar_tensor_tensor(
                                out=h[:, b, j], in0=tot[:, b, j], scalar=c["dinv"][:, bass.ds(pair.q * 2 + j, 1)],
                                in1=bias[:], op0=ALU.mult, op1=ALU.add)
                        last.then_inc(h_ready, 1)
                    if pair := at(2):
                        b, s = pair.slot % 2, pair.slot
                        dve.wait_ge(rows_rounded, pair.done())
                        nc.vector.tensor_tensor(rows_lo[:, b], c["rows"][:, s], rows_hi[:, b].bitcast(F32),
                                                ALU.subtract).then_inc(rows_split, 1)

                pipeline(dve, step)

            @block.scalar
            def _(act):
                def step(at):
                    if pair := at(2):
                        b, s = pair.slot % 2, pair.slot
                        act.wait_ge(gathered[s], pair.landed(BLOCKS))
                        if pair.has(2):
                            act.wait_ge(agg_done, pair.before(2))
                        nc.scalar.copy(rows_hi[:, b], c["rows"][:, s]).then_inc(rows_rounded, 1)
                    if pair := at(5):
                        s = pair.slot
                        act.wait_ge(dense_done, pair.done())
                        if pair.has(RING):
                            act.wait_ge(stored[s], pair.turn * 16)
                        for j in range(2):
                            last = nc.scalar.activation(g[:, s, j], g_ps[:, j], ACT.Identity,
                                                        scale=c["dinv"][:, bass.ds(pair.q * 2 + j, 1)])
                        last.then_inc(g_ready, 1)
                    if pair := at(4):
                        b = pair.slot % 2
                        act.wait_ge(h_turned, pair.done())
                        if pair.has(2):
                            act.wait_ge(dense_done, pair.before(2))
                        nc.scalar.activation(ht[:, b], ht_ps[:], ACT.Relu).then_inc(h_copied, 1)

                pipeline(act, step)


def last_pass(nc, keep, dram, source, bias):
    c = keep
    with ExitStack() as stack:
        m = Memory(nc, stack)
        own = m.sb("fin_own", [P, RING, 2, D])
        x1 = m.sb("fin_x1", [P, RING, 2, D])
        select = m.sb("fin_select", [P, 2, BLOCKS, PAIR])
        h = m.sb("fin_h", [P, 2, 2, D])
        res = m.sb("fin_res", [P, 2, 2, D])
        y = m.sb("fin_y", [P, RING, 2, D])
        stats = m.sb("fin_stats", [P, 2, 2, 6])
        mv = m.sb("fin_mv", [P, 2, 2, 2])
        sd = m.sb("fin_sd", [P, 2, 2])
        rs = m.sb("fin_rs", [P, 2, 2])
        shift = m.sb("fin_shift", [P, 2, 2])
        agg_ps = m.ps("fin_agg_ps", [P, 2, 2, D])
        loaded = [m.sem(f"fin_loaded{s}") for s in range(RING)]
        gathered = [m.sem(f"fin_gathered{s}") for s in range(RING)]
        stored = [m.sem(f"fin_stored{s}") for s in range(RING)]
        names = ("index_copied select_done agg_done h_ready res_added stats_done var_ready sd_ready "
                 "scale_steps y_ready")
        (index_copied, select_done, agg_done, h_ready, res_added, stats_done, var_ready, sd_ready,
         scale_steps, y_ready) = (m.sem("fin_" + n) for n in names.split())

        with nc.Block() as block:

            @block.sync
            def _(sp):
                fast = sp.value_load(c["fast_i"][0:1, 0:1], min_val=0, max_val=1)

                def step(at):
                    if pair := at(0):
                        s = pair.slot
                        load_own(sp, fast, own[:, s], source, dram["base"], pair, loaded[s], agg_done)
                        if pair.has(RING):
                            sp.wait_ge(res_added, pair.before(RING))
                        sp.dma_start(x1[:, s], rows_of(dram["x1"], pair.q)).then_inc(loaded[s], 16)
                    if pair := at(5):
                        s = pair.slot
                        sp.wait_ge(y_ready, pair.done())
                        sp.dma_start(rows_of(dram["out"], pair.q), y[:, s]).then_inc(stored[s], 16)

                pipeline(sp, step)
                for s in range(RING):
                    sp.wait_ge(stored[s], 16 * (NP // RING))

            @block.gpsimd
            def _(pool):
                bound = pool.to_reg(NPAD - 1)

                def step(at):
                    if pair := at(0):
                        gather_rows(nc, pool, c, pair, source, bound, index_copied, gathered, agg_done)

                pipeline(pool, step)

            @block.tensor
            def _(pe):
                def step(at):
                    if pair := at(2):
                        b, s = pair.slot % 2, pair.slot
                        pe.wait_ge(gathered[s], pair.landed(BLOCKS))
                        pe.wait_ge(loaded[s], pair.landed(2))
                        pe.wait_ge(select_done, pair.done())
                        if pair.has(2):
                            pe.wait_ge(h_ready, pair.before(2))
                        for j in range(2):
                            nc.tensor.matmul(agg_ps[:, b, j], c["ident"][:], own[:, s, j], start=True, stop=False)
                            blocks = BLOCKS - 1 + j
                            for k in range(blocks):
                                last = nc.tensor.matmul(agg_ps[:, b, j], select[:, b, k, j * P:(j + 1) * P],
                                                        c["rows"][:, s, k], start=False, stop=k == blocks - 1)
                        last.then_inc(agg_done, 1)

                pipeline(pe, step)

            @block.vector
            def _(dve):
                def step(at):
                    if pair := at(1):
                        if pair.has(2):
                            dve.wait_ge(agg_done, pair.before(2))
                        select_matrices(nc, c, pair, select[:, pair.slot % 2]).then_inc(select_done, 1)
                    if pair := at(4):
                        b = pair.slot % 2
                        dve.wait_ge(sd_ready, pair.done())
                        nc.vector.reciprocal(rs[:, b], sd[:, b]).then_inc(scale_steps, 1)
                        dve.wait_ge(scale_steps, pair.q * 2 + 1)
                        nc.vector.scalar_tensor_tensor(out=shift[:, b], in0=mv[:, b, :, 0], scalar=-1.0,
                                                       in1=rs[:, b], op0=ALU.mult, op1=ALU.mult)\
                            .then_inc(scale_steps, 1)
                    if pair := at(3):
                        b, s = pair.slot % 2, pair.slot
                        dve.wait_ge(agg_done, pair.done())
                        for j in range(2):
                            last = nc.vector.scalar_tensor_tensor(
                                out=h[:, b, j], in0=agg_ps[:, b, j], scalar=c["dinv"][:, bass.ds(pair.q * 2 + j, 1)],
                                in1=bias[:], op0=ALU.mult, op1=ALU.add)
                        last.then_inc(h_ready, 1)
                        dve.wait_ge(h_ready, pair.done())
                        dve.wait_ge(loaded[s], pair.landed(2))
                        if pair.has(2):
                            dve.wait_ge(y_ready, pair.before(2))
                        nc.vector.scalar_tensor_tensor(out=res[:, b], in0=h[:, b], scalar=0.0, in1=x1[:, s],
                                                       op0=ALU.max, op1=ALU.add).then_inc(res_added, 1)
                        dve.wait_ge(res_added, pair.done())
                        layer_stats(nc, dve, pair, res[:, b], stats[:, b], mv[:, b], stats_done, var_ready,
                                    c["spare"][:, 1:2])

                pipeline(dve, step)

            @block.scalar
            def _(act):
                def step(at):
                    if pair := at(4):
                        b, s = pair.slot % 2, pair.slot
                        act.wait_ge(scale_steps, pair.done(2))
                        if pair.has(RING):
                            act.wait_ge(stored[s], pair.turn * 16)
                        for j in range(2):
                            last = nc.scalar.activation(y[:, s, j], res[:, b, j], ACT.Identity,
                                                        bias=shift[:, b, j:j + 1], scale=rs[:, b, j:j + 1])
                        last.then_inc(y_ready, 1)
                    if pair := at(3):
                        b = pair.slot % 2
                        act.wait_ge(var_ready, pair.done())
                        nc.scalar.activation(sd[:, b], mv[:, b, :, 1], ACT.Sqrt, bias=c["ln_eps"][:, 0:1])\
                            .then_inc(sd_ready, 1)

                pipeline(act, step)


def gnn(nc, dram):
    with ExitStack() as stack:
        m = Memory(nc, stack)
        dram = dict(dram)
        dram["h2"] = nc.dram_tensor("h2_scratch", [NP, P, 2, D], F32).ap()
        for name in ("x1", "ga", "gb", "base"):
            dram[name] = nc.dram_tensor(name + "_scratch", [NPAD, D], F32).ap()
        keep = {
            "w_edge": m.sb("w_edge", [DE, D]),
            "below": m.sb("below", [P, P]), "two_ones": m.sb("two_ones", [2, P], F32R),
            "b_edge2": m.sb("b_edge2", [2, D], F32R),
            "ident": m.sb("ident", [P, P]), "ones": m.sb("ones", [P, P]),
            "ln_eps": m.sb("ln_eps", [P, 1]), "eps": m.sb("eps_sb", [P, 1]),
            "iota16": m.sb("iota16", [P, NT], F16), "iota32": m.sb("iota32", [P, PAIR]),
            "rows": m.sb("rows", [P, RING, BLOCKS, D]), "index": m.sb("index", [P, RING, BLOCKS], U32),
            "dinv": m.sb("dinv", [P, NT]), "starts": m.sb("starts_i", [P, NT], I32),
            "fast": m.sb("fast", [P, 1]), "fast_i": m.sb("fast_i", [P, 1], I32),
            "eps1": m.sb("eps1", [P, 2]), "self_w": m.sb("self_w", [P, 1]),
            "place": m.sb("place", [P, NP, BLOCKS]), "node": m.sb("node_i", [P, NP, BLOCKS], U32),
            "bn_stats": m.sb("bn_stats", [P, 2, NP, 6]), "bn_a": m.sb("bn_a", [P, 2]), "bn_c": m.sb("bn_c", [P, 2]),
            "rows_in": m.sem("rows_in"), "spare": m.sb("spare", [P, 2]),
            "general_sems": [m.sem(f"gen_{n}") for n in (
                "copy_in scaled copy_out block_in ids_ready spread turned same_ready index_steps index_ready "
                "attr_turned attr_copied edge_done msg_steps msg_ready summed source_in current_in added "
                "scattered").split()],
        }
        for name in ("w1", "w2", "g1", "g2", "g3"):
            keep[name] = m.sb(name + "_sb", [P, 2, D])
        for name in SPLIT:
            for part in ("_hi", "_lo"):
                keep[name + part] = m.sb(name + part, [P, D] if name == "w_edge" else [P, 2, D], F32R)
        for name in ("b1", "b2", "gamma", "beta"):
            keep[name] = m.sb(name + "_sb", [P, 2])
        for name in ("b_edge", "gb1", "gb2", "gb3"):
            keep[name] = m.sb(name + "_sb", [P, D])

        constants(nc, keep, dram)
        degrees(nc, keep, dram)
        slot_tables(nc, keep, dram)
        general_sum(nc, keep, dram, 0, dram["x"], True)
        gin_pass(nc, keep, dram)
        batch_norm_scale(nc, keep)
        norm_pass(nc, keep, dram)
        general_sum(nc, keep, dram, 1, dram["ga"], False)
        gcn_pass(nc, keep, dram, "gcn1_", dram["ga"], dram["gb"], keep["gb1"], keep["g2"])
        general_sum(nc, keep, dram, 2, dram["gb"], False)
        gcn_pass(nc, keep, dram, "gcn2_", dram["gb"], dram["ga"], keep["gb2"], keep["g3"])
        general_sum(nc, keep, dram, 3, dram["ga"], False)
        last_pass(nc, keep, dram, dram["ga"], keep["gb3"])


def kernel(x, src, dst, edge_attr_128, L0_gnn_W_edge, L0_gnn_b_edge, L0_gnn_W1, L0_gnn_b1, L0_gnn_W2, L0_gnn_b2,
           L0_gnn_eps, L0_gnn_gamma, L0_gnn_beta, L1_gnn_W1, L1_gnn_b1, L1_gnn_W2, L1_gnn_b2, L1_gnn_W3, L1_gnn_b3):
    import numpy as np
    import concourse.bacc as bacc
    from concourse.bass_utils import run_bass_kernel_spmd

    def padded(a, rows, fill=0):
        a = np.asarray(a)
        return np.concatenate([a, np.full((rows - a.shape[0],) + a.shape[1:], fill, a.dtype)])

    edges = padded(np.stack([np.asarray(src), np.asarray(dst)], axis=1), EPAD, FAR)
    edges[E:, 0] = 0
    arrays = {
        "x": padded(x, NPAD), "edges": edges, "edge_attr": padded(edge_attr_128, EPAD),
        "w_edge": L0_gnn_W_edge, "b_edge": L0_gnn_b_edge, "w1": L0_gnn_W1, "b1": L0_gnn_b1, "w2": L0_gnn_W2,
        "b2": L0_gnn_b2, "eps": np.asarray(L0_gnn_eps).reshape(1), "gamma": L0_gnn_gamma, "beta": L0_gnn_beta,
        "g1": np.asarray(L1_gnn_W1).T, "gb1": L1_gnn_b1, "g2": np.asarray(L1_gnn_W2).T, "gb2": L1_gnn_b2,
        "g3": np.asarray(L1_gnn_W3).T, "gb3": L1_gnn_b3,
    }
    nc = bacc.Bacc("TRN2", target_bir_lowering=False, num_devices=1)
    arrays = {name: np.ascontiguousarray(a) for name, a in arrays.items()}
    dram = {name: nc.dram_tensor(name + "_in", a.shape, mybir.dt.from_np(a.dtype), kind="ExternalInput").ap()
            for name, a in arrays.items()}
    dram["out"] = nc.dram_tensor("out", (NPAD, D), F32, kind="ExternalOutput").ap()
    gnn(nc, dram)
    result = run_bass_kernel_spmd(nc, [{name + "_in": a for name, a in arrays.items()}], core_ids=[0])
    return result.results[0]["out"][:N]
```

```python
from contextlib import ExitStack

import concourse.bass as bass
from concourse import mybir

P = 128
D = 256
N = 50000
E = 50000
DE = 128
PAIR = 2 * P
NP = -(-N // PAIR)
NT = 2 * NP
NPAD = NP * PAIR
QUAD = 2 * PAIR
NQ = NP // 2
BLOCKS = 5
FIRST = 3
SLOTS = BLOCKS * P
EPAD = NPAD + SLOTS
TAIL = N - (NP - 1) * PAIR
NO_ROW = 1 << 20
FAR = 1 << 20
RING = 4
GROUP = 8
QUAD_RING = GROUP // 2
MAX_LAG = 7
GROUPS = -(-(NP + MAX_LAG) // GROUP)
PEEL = 2
LOOP_END = NP // GROUP - 1
BN_EPS = 1e-5
LN_EPS = 1e-5

ALU = mybir.AluOpType
ACT = mybir.ActivationFunctionType
AX = mybir.AxisListType
F32 = mybir.dt.float32
F32R = mybir.dt.float32r
F16 = mybir.dt.float16
BF16 = mybir.dt.bfloat16
I32 = mybir.dt.int32
U32 = mybir.dt.uint32


SPLIT = ("w_edge", "w1", "g1")


class Pair:

    def __init__(self, group, place):
        self.group = group
        self.q = group * GROUP + place
        self.turn, self.slot = group * (GROUP // RING) + place // RING, place % RING
        self.quad, self.quad_slot = group * QUAD_RING + place // 2, place // 2
        self.odd = place % 2
        self.blocks = (FIRST, BLOCKS) if self.odd else (0, FIRST)
        self.new = self.blocks[1] - self.blocks[0]
        self.block_life = 4 if self.odd else 3

    def done(self, per=1):
        return (self.q + 1) * per

    def before(self, back):
        return self.q + 1 - back

    def has(self, back):
        return not isinstance(self.q, int) or self.q >= back

    def landed(self, dmas):
        return (self.turn + 1) * (16 * dmas)

    def rows_landed(self):
        return (self.group + 1) * (16 * BLOCKS)

    def last(self):
        return isinstance(self.q, int) and self.q == NP - 1


def pipeline(eng, step):

    def group(number):
        for k in range(GROUP):
            def pair_at(lag, k=k):
                pair = Pair(number + (k - lag) // GROUP, (k - lag) % GROUP)
                if isinstance(pair.q, int) and not 0 <= pair.q < NP:
                    return None
                return pair
            step(pair_at)

    for number in range(PEEL):
        group(number)
    with eng.Fori(PEEL, LOOP_END) as number:
        group(number)
    for number in range(LOOP_END, GROUPS):
        group(number)


def rows_of(dram, q):
    return dram[bass.ds(q * PAIR, PAIR), :].rearrange("(j p) d -> p j d", p=P)


class Memory:

    def __init__(self, nc, stack):
        self.nc, self.stack = nc, stack

    def sb(self, name, shape, dt=F32):
        return self.stack.enter_context(self.nc.sbuf_tensor(name, shape, dt))

    def ps(self, name, shape=(P, 2, D)):
        return self.stack.enter_context(self.nc.psum_tensor(name, list(shape), F32))

    def sem(self, name):
        return self.stack.enter_context(self.nc.semaphore(name))


def constants(nc, keep, dram):
    c = keep
    with ExitStack() as stack:
        m = Memory(nc, stack)
        weights_in = m.sem("weights_in")
        pool_done = m.sem("const_pool_done")
        dve_done = m.sem("const_dve_done")
        iota_i = m.sb("iota_i", [P, QUAD], I32)
        pair_b = m.sb("b_edge_twice", [2, D])
        row_hi = m.sb("b_edge_hi", [2, D])
        row_i = m.sb("row_number_i", [2, 1], I32)
        row = m.sb("row_number", [2, 1])
        with nc.Block() as block:

            @block.sync
            def _(sp):
                def load(out, in_):
                    sp.dma_start(out, in_).then_inc(weights_in, 16)

                load(c["w_edge"][:], dram["w_edge"][:, :])
                for name in ("w1", "w2", "g1", "g2", "g3"):
                    load(c[name][:], dram[name].rearrange("(c p) m -> p c m", p=P))
                for name in ("b1", "b2", "gamma", "beta", "gb1", "gb2"):
                    for h in range(2):
                        load(c[name][:, h:h + 1], dram[name][h * P:(h + 1) * P].rearrange("(p o) -> p o", o=1))
                sp.wait_ge(weights_in, 16 * (6 + 12))

            @block.scalar
            def _(act):
                for name in ("b_edge", "gb3"):
                    act.dma_start(c[name][:], dram[name].rearrange("(o d) -> o d", o=1)
                                  .broadcast_to([P, D])).then_inc(c["rows_in"], 16)
                act.dma_start(c["eps"][:], dram["eps"].rearrange("(o d) -> o d", o=1)
                              .broadcast_to([P, 1])).then_inc(c["rows_in"], 16)
                act.dma_start(pair_b[:], dram["b_edge"].rearrange("(o d) -> o d", o=1)
                              .broadcast_to([2, D])).then_inc(c["rows_in"], 16)
                act.wait_ge(c["rows_in"], 16 * 4)

            @block.gpsimd
            def _(pool):
                nc.gpsimd.memset(c["ident"][:], 0.0).then_inc(pool_done, 1)
                nc.gpsimd.memset(c["ones"][:], 1.0).then_inc(pool_done, 1)
                nc.gpsimd.memset(c["ln_eps"][:], LN_EPS).then_inc(pool_done, 1)
                nc.gpsimd.iota(iota_i[:], pattern=[[1, QUAD]], base=0, channel_multiplier=0).then_inc(pool_done, 1)
                nc.gpsimd.iota(row_i[:], pattern=[[0, 1]], base=0, channel_multiplier=1).then_inc(pool_done, 1)
                pool.wait_ge(pool_done, 5)
                nc.gpsimd.affine_select(out=c["below"][:], in_=c["ones"][:], compare_op=ALU.is_gt, fill=0.0,
                                        base=0, pattern=[[-1, P]], channel_multiplier=1).then_inc(pool_done, 1)
                nc.gpsimd.affine_select(out=c["ident"][:], in_=c["ident"][:], compare_op=ALU.not_equal, fill=1.0,
                                        base=0, pattern=[[-1, P]], channel_multiplier=1).then_inc(pool_done, 1)

            @block.vector
            def _(dve):
                for s in range(QUAD_RING):
                    nc.vector.memset(c["rows"][:, s], 0.0)
                nc.vector.memset(c["eps1"][:, 1:2], 1.0)
                dve.wait_ge(pool_done, 7)
                nc.vector.tensor_copy(c["iota16"][:], iota_i[:, 0:NT])
                nc.vector.tensor_copy(c["iota32"][:], iota_i[:])
                dve.wait_ge(weights_in, 16 * (6 + 12))
                for name in SPLIT:
                    nc.vector.tensor_copy(c[name + "_hi"][:], c[name][:]).then_inc(dve_done, 1)
                dve.wait_ge(dve_done, len(SPLIT))
                for name in SPLIT:
                    nc.vector.tensor_tensor(c[name + "_lo"][:], c[name][:], c[name + "_hi"][:].bitcast(F32),
                                            ALU.subtract)
                dve.wait_ge(c["rows_in"], 16 * 4)
                nc.vector.tensor_copy(c["two_ones"][:], c["ones"][0:2, :])
                nc.vector.tensor_copy(c["b_edge2"][:], pair_b[:]).then_inc(dve_done, 1)
                nc.vector.tensor_copy(row[:], row_i[:]).then_inc(dve_done, 1)
                dve.wait_ge(dve_done, len(SPLIT) + 2)
                nc.vector.tensor_scalar(row_hi[:], c["b_edge2"][:].bitcast(F32), row[:, 0:1], None, ALU.mult)\
                    .then_inc(dve_done, 1)
                dve.wait_ge(dve_done, len(SPLIT) + 3)
                nc.vector.tensor_tensor(c["b_edge2"][:], pair_b[:], row_hi[:], ALU.subtract)


def degrees(nc, keep, dram):
    c = keep
    COLS = NT
    UNROLL = 8
    DEPTH = 4
    with ExitStack() as stack:
        m = Memory(nc, stack)
        edges = m.sb("edges_sb", [P, COLS, 2], I32)
        after = m.sb("edges_next", [P, COLS, 2], I32)
        hi_i = m.sb("hi_i", [P, COLS], I32)
        lo_i = m.sb("lo_i", [P, COLS], I32)
        hi = m.sb("hi", [P, COLS])
        lo = m.sb("lo", [P, COLS])
        hot_hi = m.sb("hot_hi", [P, DEPTH, NT], BF16)
        hot_lo = m.sb("hot_lo", [P, DEPTH, P], BF16)
        deg = m.sb("deg", [P, NT])
        deg1 = m.sb("deg1", [P, NT])
        root = m.sb("root", [P, NT])
        zero = m.sb("zero_row", [P, NT])
        counts = m.sb("counts", [P, NT])
        ends = m.sb("ends", [P, NT])
        starts = m.sb("starts", [P, NT])
        falls = m.sb("falls", [P, NT])
        nfalls = m.sb("nfalls", [P, 1])
        outside = m.sb("outside", [P, 6, NQ])
        most = m.sb("most", [P, 1])
        fits = m.sb("fits", [P, 1])
        root2 = m.sb("root2", [P, NT])
        hist = m.ps("hist", [P, NT])
        colsum = m.ps("colsum", [P, NT])
        fallsum = m.ps("fallsum", [P, 1])
        edges_in = m.sem("edges_in")
        split = m.sem("split")
        hot = m.sem("hot")
        used = m.sem("hot_used")
        chain = m.sem("deg_chain")
        deg_steps = m.sem("deg_steps")
        summed = m.sem("summed")
        rooted = m.sem("rooted")

        with nc.Block() as block:

            @block.sync
            def _(sp):
                sp.dma_start(edges[:], dram["edges"][0:P * COLS, :].rearrange("(p c) t -> p c t", p=P))\
                    .then_inc(edges_in, 16)
                sp.dma_start(after[:], dram["edges"][1:P * COLS + 1, :].rearrange("(p c) t -> p c t", p=P))\
                    .then_inc(edges_in, 16)

            @block.vector
            def _(dve):
                dve.wait_ge(edges_in, 32)
                nc.vector.tensor_scalar(hi_i[:], edges[:, :, 1], 7, None, ALU.arith_shift_right).then_inc(split, 1)
                nc.vector.tensor_scalar(lo_i[:], edges[:, :, 1], P - 1, None, ALU.bitwise_and).then_inc(split, 1)
                dve.wait_ge(split, 2)
                nc.vector.tensor_copy(hi[:], hi_i[:]).then_inc(split, 1)
                nc.vector.tensor_copy(lo[:], lo_i[:]).then_inc(split, 1)
                dve.wait_ge(split, 4)

                def hot_step(t, k):
                    if not isinstance(t, int) or t >= DEPTH:
                        dve.wait_ge(used, t - DEPTH + 1)
                    nc.vector.tensor_scalar(hot_lo[:, k % DEPTH], c["iota16"][:, 0:P], lo[:, bass.ds(t, 1)], None,
                                            ALU.is_equal)
                    nc.vector.tensor_scalar(hot_hi[:, k % DEPTH], c["iota16"][:], hi[:, bass.ds(t, 1)], None,
                                            ALU.is_equal).then_inc(hot, 1)

                for k in range(UNROLL):
                    hot_step(k, k)
                with dve.Fori(1, COLS // UNROLL) as i:
                    for k in range(UNROLL):
                        hot_step(i * UNROLL + k, k)

                dve.wait_ge(used, COLS)
                nc.vector.tensor_copy(deg[:], hist[:]).then_inc(deg_steps, 1)
                dve.wait_ge(deg_steps, 1)
                nc.vector.tensor_scalar(deg1[:], deg[:], 1.0, None, ALU.add).then_inc(deg_steps, 1)
                nc.vector.tensor_tensor(falls[:], edges[:, :, 1], after[:, :, 1], ALU.is_gt).then_inc(chain, 1)
                nc.vector.memset(zero[:], 0.0).then_inc(chain, 1)
                dve.wait_ge(chain, 2)
                nc.vector.tensor_reduce(nfalls[:], falls[:], AX.X, ALU.add).then_inc(chain, 1)
                dve.wait_ge(summed, 1)
                nc.vector.tensor_copy(counts[:], colsum[:]).then_inc(chain, 1)
                dve.wait_ge(chain, 4)
                nc.vector.tensor_tensor_scan(ends[:], counts[:], zero[:], 0.0, ALU.add, ALU.add).then_inc(chain, 1)
                dve.wait_ge(chain, 5)
                nc.vector.tensor_tensor(starts[:], ends[:], counts[:], ALU.subtract).then_inc(chain, 1)
                dve.wait_ge(chain, 6)
                nc.vector.tensor_copy(c["starts"][:], starts[:]).then_inc(chain, 1)
                quad_ends = ends[:].rearrange("p (q t) -> p q t", t=4)
                quad_start = starts[:].rearrange("p (q t) -> p q t", t=4)[:, :, 0]
                for t in range(4):
                    nc.vector.scalar_tensor_tensor(out=outside[:, t], in0=quad_ends[:, :, t],
                                                   scalar=float(-(t + 2) * P), in1=quad_start,
                                                   op0=ALU.add, op1=ALU.subtract).then_inc(chain, 1)
                for t in (1, 2):
                    nc.vector.scalar_tensor_tensor(out=outside[:, 3 + t], in0=quad_start, scalar=float(t * P),
                                                   in1=quad_ends[:, :, t], op0=ALU.add, op1=ALU.subtract)\
                        .then_inc(chain, 1)
                dve.wait_ge(chain, 13)
                nc.vector.tensor_reduce(most[:], outside[:].rearrange("p t q -> p (t q)"), AX.X, ALU.max)\
                    .then_inc(chain, 1)
                dve.wait_ge(chain, 14)
                nc.vector.tensor_scalar(fits[:], most[:], 0.0, None, ALU.is_le).then_inc(chain, 1)
                dve.wait_ge(chain, 15)
                dve.wait_ge(summed, 2)
                nc.vector.scalar_tensor_tensor(out=c["fast"][:], in0=fallsum[:], scalar=0.0, in1=fits[:],
                                               op0=ALU.is_equal, op1=ALU.mult).then_inc(chain, 1)
                dve.wait_ge(rooted, 1)
                nc.vector.reciprocal(falls[:], root[:]).then_inc(chain, 1)
                dve.wait_ge(chain, 17)
                nc.vector.tensor_tensor(zero[:], falls[:], deg1[:], ALU.mult).then_inc(chain, 1)
                dve.wait_ge(chain, 18)
                nc.vector.tensor_tensor(root2[:], zero[:], root[:], ALU.add).then_inc(chain, 1)
                dve.wait_ge(chain, 19)
                nc.vector.tensor_scalar(root2[:], root2[:], 0.5, None, ALU.mult).then_inc(chain, 1)
                dve.wait_ge(chain, 20)
                nc.vector.reciprocal(c["dinv"][:], root2[:]).then_inc(chain, 1)
                nc.vector.tensor_copy(c["fast_i"][:], c["fast"][:]).then_inc(chain, 1)
                nc.vector.tensor_scalar(c["eps1"][:, 0:1], c["eps"][:], 1.0, None, ALU.add).then_inc(chain, 1)
                nc.vector.tensor_scalar(c["self_w"][:], c["eps"][:], c["fast"][:, 0:1], 1.0, ALU.mult, ALU.add)\
                    .then_inc(chain, 1)

            @block.tensor
            def _(pe):
                def count_step(t, k):
                    pe.wait_ge(hot, t + 1)
                    nc.tensor.matmul(hist[:], hot_lo[:, k % DEPTH], hot_hi[:, k % DEPTH],
                                     start=isinstance(t, int) and t == 0,
                                     stop=isinstance(t, int) and t == COLS - 1,
                                     skip_group_check=True).then_inc(used, 1)

                for k in range(UNROLL):
                    count_step(k, k)
                with pe.Fori(1, COLS // UNROLL) as i:
                    for k in range(UNROLL):
                        count_step(i * UNROLL + k, k)
                pe.wait_ge(deg_steps, 1)
                nc.tensor.matmul(colsum[:], c["ones"][:], deg[:], start=True, stop=True).then_inc(summed, 1)
                pe.wait_ge(chain, 3)
                nc.tensor.matmul(fallsum[:], c["ones"][:], nfalls[:], start=True, stop=True).then_inc(summed, 1)

            @block.scalar
            def _(act):
                act.wait_ge(deg_steps, 2)
                nc.scalar.activation(root[:], deg1[:], ACT.Sqrt).then_inc(rooted, 1)


def slot_tables(nc, keep, dram):
    c = keep
    with ExitStack() as stack:
        m = Memory(nc, stack)
        window = m.sb("window", [P, NQ, BLOCKS, 2], I32)
        base_i = m.sb("base_i", [P, NQ, BLOCKS], I32)
        base = m.sb("base", [P, NQ, BLOCKS])
        place = m.sb("raw_place", [P, NQ, BLOCKS])
        low = m.sb("low", [P, NQ, BLOCKS])
        valid = m.sb("valid", [P, NQ, BLOCKS])
        node = m.sb("node", [P, NQ, BLOCKS])
        windows_in = m.sem("windows_in")
        base_ready = m.sem("base_ready")
        chain = m.sem("slot_chain")
        UNROLL = 7

        def windows(eng, first):
            with eng.Fori(0, NQ // (2 * UNROLL)) as i:
                for k in range(UNROLL):
                    q = i * (2 * UNROLL) + 2 * k + first
                    start = eng.value_load(c["starts"][0:1, bass.ds(q * 4, 1)], min_val=0, max_val=E)
                    eng.dma_start(window[:, bass.ds(q, 1)].rearrange("p o b t -> p (o b) t"),
                                  dram["edges"][bass.ds(start, SLOTS), :].rearrange("(b p) t -> p b t", p=P))\
                       .then_inc(windows_in, 16)

        with nc.Block() as block:

            @block.sync
            def _(sp):
                windows(sp, 0)

            @block.scalar
            def _(act):
                windows(act, 1)

            @block.gpsimd
            def _(pool):
                nc.gpsimd.iota(base_i[:], pattern=[[QUAD, NQ], [0, BLOCKS]], base=0, channel_multiplier=0)\
                    .then_inc(base_ready, 1)

            @block.vector
            def _(dve):
                dve.wait_ge(base_ready, 1)
                nc.vector.tensor_copy(base[:], base_i[:]).then_inc(chain, 1)
                dve.wait_ge(chain, 1)
                dve.wait_ge(windows_in, 16 * NQ)
                nc.vector.tensor_tensor(place[:], window[:, :, :, 1], base[:], ALU.subtract).then_inc(chain, 1)
                dve.wait_ge(chain, 2)
                nc.vector.tensor_scalar(low[:], place[:], 0.0, c["fast"][:, 0:1], ALU.is_ge, ALU.mult)\
                    .then_inc(chain, 1)
                dve.wait_ge(chain, 3)
                nc.vector.scalar_tensor_tensor(out=valid[:], in0=place[:], scalar=float(QUAD), in1=low[:],
                                               op0=ALU.is_lt, op1=ALU.mult).then_inc(chain, 1)
                dve.wait_ge(chain, 4)
                nc.vector.scalar_tensor_tensor(out=node[:], in0=window[:, :, :, 0], scalar=float(-NO_ROW),
                                               in1=valid[:], op0=ALU.add, op1=ALU.mult).then_inc(chain, 1)
                nc.vector.scalar_tensor_tensor(out=base[:], in0=place[:], scalar=1.0, in1=valid[:],
                                               op0=ALU.add, op1=ALU.mult).then_inc(chain, 1)
                dve.wait_ge(chain, 6)
                nc.vector.tensor_scalar(c["node"][:], node[:], float(NO_ROW), None, ALU.add).then_inc(chain, 1)
                nc.vector.tensor_scalar(c["place"][:], base[:], -1.0, None, ALU.add).then_inc(chain, 1)


def gather_rows(nc, pool, c, pair, source, bound, index_copied, gathered, rows_free):
    s = pair.quad_slot
    if pair.has(GROUP):
        pool.wait_ge(rows_free, pair.before(GROUP - 1))
    nc.gpsimd.tensor_copy(c["index"][:, s], c["node"][:, bass.ds(pair.quad, 1), :]).then_inc(index_copied, 1)
    pool.wait_ge(index_copied, pair.quad + 1)
    nc.gpsimd.tensor_tensor(c["spare"][:, 0:1], c["ln_eps"][:], c["ln_eps"][:], ALU.add)
    for b in range(BLOCKS):
        pool.indirect_dma_start(out=c["rows"][:, s, b], out_offset=None, in_=source[:, :],
                                in_offset=bass.IndirectOffsetOnAxis(ap=c["index"][:, s, b:b + 1], axis=0),
                                bounds_check=bound, oob_is_err=False).then_inc(gathered[s], 16)


def tile_blocks(pair, j):
    t = 2 * pair.odd + j
    return range(max(t - 1, 0) - pair.odd, t + 2 - pair.odd)


def select_matrices(nc, c, pair, select):
    for b in range(FIRST + pair.odd):
        tiles = [j for j in range(2) if b in tile_blocks(pair, j)]
        first, end = tiles[0] * P, (tiles[-1] + 1) * P
        last = nc.vector.tensor_scalar(select[:, b, first:end],
                                       c["iota32"][:, pair.odd * PAIR + first:pair.odd * PAIR + end],
                                       c["place"][:, bass.ds(pair.quad, 1), pair.odd + b], None, ALU.is_equal)
    return last


def sum_into_nodes(nc, pair, out, select, parts):
    for j in range(2):
        terms = [(b, rows) for b in tile_blocks(pair, j) for rows in parts]
        for n, (b, rows) in enumerate(terms):
            last = nc.tensor.matmul(out[:, j], select[:, b, j * P:(j + 1) * P], rows[:, pair.odd + b],
                                    start=n == 0, stop=n == len(terms) - 1)
    return last


def transpose_rows(nc, c, out, rows):
    for j in range(2):
        for h in range(2):
            last = nc.tensor.transpose(out[:, h, j * P:(j + 1) * P], rows[:, j, h * P:(h + 1) * P], c["ident"][:])
    return last


def products(parts, weight):
    if len(parts) == 1:
        return [(parts[0], weight[0])]
    (hi, lo), (w_hi, w_lo) = parts, weight
    return [(hi, w_hi), (lo, w_hi), (hi, w_lo)]


def dense_rows(nc, out, parts, weight):
    terms = [(h, a, w) for h in range(2) for a, w in products(parts, weight)]
    for j in range(2):
        for n, (h, a, w) in enumerate(terms):
            last = nc.tensor.matmul(out[:, j], a[:, h, j * P:(j + 1) * P], w[:, h],
                                    start=n == 0, stop=n == len(terms) - 1)
    return last


def dense_cols(nc, out, parts, weight):
    terms = [(h, a, w) for h in range(2) for a, w in products(parts, weight)]
    for m in range(2):
        for n, (h, a, w) in enumerate(terms):
            last = nc.tensor.matmul(out[:, m], w[:, h, m * P:(m + 1) * P], a[:, h],
                                    start=n == 0, stop=n == len(terms) - 1)
    return last


def load_own(sp, fast, out, source, base, pair, landed, slot_free):
    for ran, rows in ((1, source), (0, base)):
        with sp.If(fast == ran):
            if pair.has(RING):
                sp.wait_ge(slot_free, pair.before(RING))
            sp.dma_start(out, rows_of(rows, pair.q)).then_inc(landed, 16)


def layer_stats(nc, dve, pair, rows, stats, mv, stats_done, var_ready, spare):
    for j in range(2):
        last = nc.vector.bn_stats(stats[:, j], rows[:, j])
    last.then_inc(stats_done, 1)
    dve.wait_ge(stats_done, pair.done())
    nc.vector.memset(spare, 0.0)
    for j in range(2):
        last = nc.vector.bn_aggr(mv[:, j], stats[:, j])
    last.then_inc(var_ready, 1)


def general_sum(nc, keep, dram, number, source, gin):
    c = keep
    base = dram["base"]
    sems = c["general_sems"]
    (copy_in, scaled, copy_out, block_in, ids_steps, turned, same_ready, index_steps, index_ready,
     attr_turned, attr_copied, edge_done, msg_steps, msg_ready, summed, gathered, added,
     scattered, carried) = sems
    done_pairs, done_blocks = number * NP, number * NT
    loads = 2 if gin else 1
    with ExitStack() as stack:
        m = Memory(nc, stack)
        name = f"gen{number}_"
        own = m.sb(name + "own", [P, 2, D])
        own_out = m.sb(name + "own_out", [P, 2, D])
        ids = m.sb(name + "ids", [P, 2], I32)
        src = m.sb(name + "src", [P, 1], U32)
        dst = m.sb(name + "dst", [P, 1])
        dst_cols = m.sb(name + "dst_cols", [P, P])
        same = m.sb(name + "same", [P, P])
        earlier = m.sb(name + "earlier", [P, P])
        count = m.sb(name + "count", [P, 1])
        first = m.sb(name + "first", [P, 1])
        index_f = m.sb(name + "index_f", [P, 1])
        index = m.sb(name + "index", [P, 1], U32)
        attr = m.sb(name + "attr", [P, DE])
        attr_t = m.sb(name + "attr_t", [P, P])
        msg0 = m.sb(name + "msg0", [P, D])
        msg1 = m.sb(name + "msg1", [P, D])
        msg = m.sb(name + "msg", [P, D])
        total = m.sb(name + "total", [P, D])
        rows = c["rows"][:, 0, 0]
        current = c["rows"][:, 0, 1]
        dst_ps = m.ps(name + "dst_ps", [P, P])
        attr_ps = m.ps(name + "attr_ps", [P, P])
        edge_ps = m.ps(name + "edge_ps", [P, D])
        sum_ps = m.ps(name + "sum_ps", [P, D])

        with nc.Block() as block:

            @block.sync
            def _(sp):
                fast = sp.value_load(c["fast_i"][0:1, 0:1], min_val=0, max_val=1)
                with sp.If(fast == 0):
                    def copy_rows(q):
                        sp.dma_start(own[:], rows_of(source, q)).then_inc(copy_in, 16)
                        sp.wait_ge(scaled, q + (done_pairs + 1))
                        sp.dma_start(rows_of(base, q), own_out[:]).then_inc(copy_out, 16)

                    def load_block(e):
                        sp.dma_start(ids[:], dram["edges"][bass.ds(e * P, P), :]).then_inc(block_in, 16)
                        if gin:
                            sp.dma_start(attr[:], dram["edge_attr"][bass.ds(e * P, P), :]).then_inc(block_in, 16)

                    copy_rows(0)
                    with sp.Fori(1, NP) as q:
                        sp.wait_ge(copy_out, (q + done_pairs) * 16)
                        copy_rows(q)
                    sp.wait_ge(copy_out, (done_pairs + NP) * 16)
                    load_block(0)
                    with sp.Fori(1, NT) as e:
                        sp.wait_ge(scattered, (e + done_blocks) * 16)
                        load_block(e)
                    sp.wait_ge(scattered, (done_blocks + NT) * 16)

            @block.gpsimd
            def _(pool):
                bound = pool.to_reg(NPAD - 1)
                fast = pool.value_load(c["fast_i"][0:1, 0:1], min_val=0, max_val=1)

                def carry():
                    nc.gpsimd.tensor_tensor(c["spare"][:, 2:3], c["ln_eps"][:], c["ln_eps"][:], ALU.add)\
                        .then_inc(carried, 1)

                with pool.If(fast == 0):
                    carry()
                    with pool.Fori(0, NT) as e:
                        turn = e + (done_blocks + 1)
                        pool.wait_ge(ids_steps, turn * 2 - 1)
                        pool.wait_ge(carried, turn * 3 + (number - 2))
                        carry()
                        pool.indirect_dma_start(out=rows, out_offset=None, in_=source[:, :],
                                                in_offset=bass.IndirectOffsetOnAxis(ap=src[:, 0:1], axis=0),
                                                bounds_check=bound, oob_is_err=False).then_inc(gathered, 16)
                        pool.wait_ge(index_ready, turn)
                        pool.wait_ge(carried, turn * 3 + (number - 1))
                        carry()
                        pool.indirect_dma_start(out=current, out_offset=None, in_=base[:, :],
                                                in_offset=bass.IndirectOffsetOnAxis(ap=index[:, 0:1], axis=0),
                                                bounds_check=bound, oob_is_err=False).then_inc(gathered, 16)
                        pool.wait_ge(added, turn)
                        pool.wait_ge(carried, turn * 3 + (number - 0))
                        carry()
                        pool.indirect_dma_start(out=base[:, :], in_=total[:], in_offset=None,
                                                out_offset=bass.IndirectOffsetOnAxis(ap=index[:, 0:1], axis=0),
                                                bounds_check=bound, oob_is_err=False).then_inc(scattered, 16)

            @block.vector
            def _(dve):
                fast = dve.value_load(c["fast_i"][0:1, 0:1], min_val=0, max_val=1)
                with dve.If(fast == 0):
                    with dve.Fori(0, NP) as q:
                        dve.wait_ge(copy_in, (q + (done_pairs + 1)) * 16)
                        factor = c["eps1"][:, 0:1] if gin else c["eps1"][:, 1:2]
                        nc.vector.tensor_scalar(own_out[:], own[:], factor, None, ALU.mult).then_inc(scaled, 1)
                    with dve.Fori(0, NT) as e:
                        turn = e + (done_blocks + 1)
                        dve.wait_ge(block_in, (e + 1) * (16 * loads) + (0 if gin else 16 * (done_blocks + NT)))
                        nc.vector.tensor_copy(src[:], ids[:, 0:1])
                        nc.vector.tensor_copy(dst[:], ids[:, 1:2]).then_inc(ids_steps, 1)
                        dve.wait_ge(ids_steps, turn * 2 - 1)
                        nc.vector.tensor_scalar(dst_cols[:], c["ones"][:], dst[:, 0:1], None, ALU.mult)\
                            .then_inc(ids_steps, 1)
                        dve.wait_ge(turned, turn)
                        nc.vector.tensor_scalar(same[:], dst_ps[:], dst[:, 0:1], None, ALU.is_equal)\
                            .then_inc(same_ready, 1)
                        dve.wait_ge(same_ready, turn)
                        nc.vector.tensor_tensor(earlier[:], same[:], c["below"][:], ALU.mult).then_inc(index_steps, 1)
                        dve.wait_ge(index_steps, turn * 4 - 3)
                        nc.vector.tensor_reduce(count[:], earlier[:], AX.X, ALU.add).then_inc(index_steps, 1)
                        dve.wait_ge(index_steps, turn * 4 - 2)
                        nc.vector.tensor_scalar(first[:], count[:], 0.0, None, ALU.is_equal).then_inc(index_steps, 1)
                        dve.wait_ge(index_steps, turn * 4 - 1)
                        nc.vector.scalar_tensor_tensor(out=index_f[:], in0=dst[:], scalar=float(-NO_ROW),
                                                       in1=first[:], op0=ALU.add, op1=ALU.mult)\
                            .then_inc(index_steps, 1)
                        dve.wait_ge(index_steps, turn * 4)
                        nc.vector.tensor_scalar(index[:], index_f[:], float(NO_ROW), None, ALU.add)\
                            .then_inc(index_ready, 1)
                        dve.wait_ge(gathered, turn * 32)
                        if gin:
                            dve.wait_ge(edge_done, e + 1)
                            nc.vector.tensor_tensor(msg0[:], edge_ps[:], rows, ALU.add).then_inc(msg_steps, 1)
                            dve.wait_ge(msg_steps, e * 2 + 1)
                            nc.vector.tensor_tensor(msg1[:], msg0[:], c["b_edge"][:], ALU.add).then_inc(msg_steps, 1)
                            dve.wait_ge(msg_steps, e * 2 + 2)
                            nc.vector.tensor_scalar(msg[:], msg1[:], 0.0, None, ALU.max).then_inc(msg_ready, 1)
                        else:
                            nc.vector.tensor_copy(msg[:], rows).then_inc(msg_ready, 1)
                        dve.wait_ge(summed, turn)
                        nc.vector.tensor_tensor(total[:], sum_ps[:], current, ALU.add).then_inc(added, 1)

            @block.tensor
            def _(pe):
                fast = pe.value_load(c["fast_i"][0:1, 0:1], min_val=0, max_val=1)
                with pe.If(fast == 0):
                    with pe.Fori(0, NT) as e:
                        turn = e + (done_blocks + 1)
                        pe.wait_ge(ids_steps, turn * 2)
                        nc.tensor.transpose(dst_ps[:], dst_cols[:], c["ident"][:]).then_inc(turned, 1)
                        if gin:
                            pe.wait_ge(block_in, (e + 1) * 32)
                            nc.tensor.transpose(attr_ps[:], attr[:], c["ident"][:]).then_inc(attr_turned, 1)
                            pe.wait_ge(attr_copied, e + 1)
                            nc.tensor.matmul(edge_ps[:], attr_t[:], c["w_edge"][:], start=True, stop=True)\
                                .then_inc(edge_done, 1)
                        pe.wait_ge(msg_ready, turn)
                        pe.wait_ge(same_ready, turn)
                        nc.tensor.matmul(sum_ps[:], same[:], msg[:], start=True, stop=True).then_inc(summed, 1)

            if gin:
                @block.scalar
                def _(act):
                    fast = act.value_load(c["fast_i"][0:1, 0:1], min_val=0, max_val=1)
                    with act.If(fast == 0):
                        with act.Fori(0, NT) as e:
                            act.wait_ge(attr_turned, e + 1)
                            nc.scalar.copy(attr_t[:], attr_ps[:]).then_inc(attr_copied, 1)


def gin_pass(nc, keep, dram):
    c = keep
    with ExitStack() as stack:
        m = Memory(nc, stack)
        attr = m.sb("attr", [P, RING, FIRST, DE])
        own = m.sb("own", [P, RING, 2, D])
        attr_hi = m.sb("attr_hi", [P, 2, FIRST * P], F32R)
        attr_lo = m.sb("attr_lo", [P, 2, FIRST * P], F32R)
        raw = m.sb("raw", [P, 2, FIRST, D])
        msg_hi = m.sb("msg_hi", [P, 2, BLOCKS, D], F32R)
        msg_lo = m.sb("msg_lo", [P, 2, BLOCKS, D], F32R)
        select = m.sb("gin_select", [P, 2, FIRST + 1, PAIR], F32R)
        h0 = m.sb("h0", [P, 2, 2, D])
        h0t_hi = m.sb("h0t_hi", [P, 2, 2, D], F32R)
        h0t_lo = m.sb("h0t_lo", [P, 2, 2, D], F32R)
        h1t = m.sb("h1t", [P, 2, 2, D])
        h2t = m.sb("h2t", [P, RING, 2, D])
        attr_ps = m.ps("attr_ps", [P, 512])
        edge_ps = m.ps("edge_ps", [P, 4, D])
        agg_ps = m.ps("agg_ps")
        h0t_ps = m.ps("h0t_ps")
        h1t_ps = m.ps("h1t_ps")
        h2t_ps = m.ps("h2t_ps")
        loaded = [m.sem(f"gin_loaded{s}") for s in range(RING)]
        gathered = [m.sem(f"gin_gathered{s}") for s in range(RING)]
        stored = [m.sem(f"gin_stored{s}") for s in range(RING)]
        names = ("index_copied attr_turned attr_rounded attr_split edge_done select_done rows_added msg_rounded "
                 "msg_split agg_done h0_done h0_turned h0_rounded h0_split h1_done h1_ready h2_done h2_ready stats_done")
        (index_copied, attr_turned, attr_rounded, attr_split, edge_done, select_done, rows_added, msg_rounded,
         msg_split, agg_done, h0_done, h0_turned, h0_rounded, h0_split, h1_done, h1_ready, h2_done, h2_ready,
         stats_done) = (m.sem("gin_" + n) for n in names.split())

        with nc.Block() as block:

            @block.sync
            def _(sp):
                fast = sp.value_load(c["fast_i"][0:1, 0:1], min_val=0, max_val=1)

                def step(at):
                    if pair := at(0):
                        s = pair.slot
                        start = sp.value_load(c["starts"][0:1, bass.ds(pair.quad * 4, 1)], min_val=0, max_val=E)
                        if pair.has(RING):
                            sp.wait_ge(attr_turned, pair.before(RING))
                        sp.dma_start(attr[:, s, 0:pair.new],
                                     dram["edge_attr"][bass.ds(start + pair.blocks[0] * P, pair.new * P), :]
                                     .rearrange("(b p) k -> p b k", p=P)).then_inc(loaded[s], 16)
                        load_own(sp, fast, own[:, s], dram["x"], dram["base"], pair, loaded[s], h0_done)
                    if pair := at(6):
                        sp.wait_ge(h2_ready, pair.done())
                        sp.dma_start(dram["h2"][bass.ds(pair.q, 1)].rearrange("o p c n -> p (o c) n"),
                                     h2t[:, pair.slot]).then_inc(stored[pair.slot], 16)

                pipeline(sp, step)
                for s in range(RING):
                    sp.wait_ge(stored[s], 16 * (NP // RING))

            @block.gpsimd
            def _(pool):
                bound = pool.to_reg(NPAD - 1)

                def step(at):
                    if (pair := at(0)) and not pair.odd:
                        gather_rows(nc, pool, c, pair, dram["x"], bound, index_copied, gathered, rows_added)

                pipeline(pool, step)

            @block.tensor
            def _(pe):
                def step(at):
                    if pair := at(3):
                        b, half = pair.slot % 2, pair.quad_slot % 2
                        pe.wait_ge(msg_split, pair.done())
                        pe.wait_ge(select_done, pair.done())
                        if pair.has(1):
                            pe.wait_ge(h0_done, pair.before(1))
                        sum_into_nodes(nc, pair, agg_ps, select[:, b], [msg_hi[:, half], msg_lo[:, half]]).then_inc(agg_done, 1)
                    if pair := at(2):
                        b = pair.slot % 2
                        pe.wait_ge(attr_split, pair.done())
                        if pair.has(1):
                            pe.wait_ge(rows_added, pair.before(1))
                        terms = products([attr_hi[:, b], attr_lo[:, b]], [c["w_edge_hi"], c["w_edge_lo"]])
                        for k in range(pair.new):
                            nc.tensor.matmul(edge_ps[:, k], c["two_ones"][:], c["b_edge2"][:], start=True, stop=False)
                            for n, (a, w) in enumerate(terms):
                                last = nc.tensor.matmul(edge_ps[:, k], a[:, k * P:(k + 1) * P], w[:],
                                                        start=False, stop=n == len(terms) - 1)
                        last.then_inc(edge_done, 1)
                    if pair := at(4):
                        b = pair.slot % 2
                        pe.wait_ge(h0_split, pair.done())
                        if pair.has(1):
                            pe.wait_ge(h1_ready, pair.before(1))
                        dense_cols(nc, h1t_ps, [h0t_hi[:, b], h0t_lo[:, b]], [c["w1_hi"], c["w1_lo"]])\
                            .then_inc(h1_done, 1)
                    if pair := at(1):
                        s = pair.slot
                        pe.wait_ge(loaded[s], pair.landed(2))
                        if pair.has(1):
                            pe.wait_ge(attr_split, pair.before(1))
                        for k in range(pair.new):
                            last = nc.tensor.transpose(attr_ps[:, k * P:(k + 1) * P], attr[:, s, k], c["ident"][:])
                        last.then_inc(attr_turned, 1)
                    if pair := at(3):
                        pe.wait_ge(h0_done, pair.done())
                        if pair.has(1):
                            pe.wait_ge(h0_split, pair.before(1))
                        transpose_rows(nc, c, h0t_ps, h0[:, pair.slot % 2]).then_inc(h0_turned, 1)
                    if pair := at(5):
                        pe.wait_ge(h1_ready, pair.done())
                        if pair.has(1):
                            pe.wait_ge(h2_ready, pair.before(1))
                        dense_cols(nc, h2t_ps, [h1t[:, pair.slot % 2]], [c["w2"]]).then_inc(h2_done, 1)

                pipeline(pe, step)

            @block.scalar
            def _(act):
                def step(at):
                    if pair := at(2):
                        b = pair.slot % 2
                        act.wait_ge(rows_added, pair.done())
                        half, blocks = pair.quad_slot % 2, slice(*pair.blocks)
                        if pair.has(pair.block_life):
                            act.wait_ge(agg_done, pair.before(pair.block_life))
                        nc.scalar.activation(msg_hi[:, half, blocks], raw[:, b, 0:pair.new], ACT.Relu).then_inc(msg_rounded, 1)
                    if pair := at(4):
                        b = pair.slot % 2
                        act.wait_ge(h1_done, pair.done())
                        if pair.has(2):
                            act.wait_ge(h2_done, pair.before(2))
                        for h in range(2):
                            last = nc.scalar.activation(h1t[:, b, h], h1t_ps[:, h], ACT.Relu, bias=c["b1"][:, h:h + 1])
                        last.then_inc(h1_ready, 1)
                    if pair := at(1):
                        b = pair.slot % 2
                        act.wait_ge(attr_turned, pair.done())
                        if pair.has(2):
                            act.wait_ge(edge_done, pair.before(2))
                        nc.scalar.copy(attr_hi[:, b, 0:pair.new * P], attr_ps[:, 0:pair.new * P]).then_inc(attr_rounded, 1)
                    if pair := at(3):
                        b = pair.slot % 2
                        act.wait_ge(h0_turned, pair.done())
                        if pair.has(2):
                            act.wait_ge(h1_done, pair.before(2))
                        nc.scalar.copy(h0t_hi[:, b], h0t_ps[:]).then_inc(h0_rounded, 1)
                    if pair := at(5):
                        s = pair.slot
                        act.wait_ge(h2_done, pair.done())
                        if pair.has(RING):
                            act.wait_ge(stored[s], pair.turn * 16)
                            act.wait_ge(stats_done, pair.before(RING))
                        for h in range(2):
                            last = nc.scalar.activation(h2t[:, s, h], h2t_ps[:, h], ACT.Identity,
                                                        bias=c["b2"][:, h:h + 1])
                        last.then_inc(h2_ready, 1)

                pipeline(act, step)

            @block.vector
            def _(dve):
                def step(at):
                    if pair := at(3):
                        b, s = pair.slot % 2, pair.slot
                        dve.wait_ge(agg_done, pair.done())
                        dve.wait_ge(loaded[s], pair.landed(2))
                        if pair.has(2):
                            dve.wait_ge(h0_turned, pair.before(2))
                        nc.vector.scalar_tensor_tensor(out=h0[:, b], in0=own[:, s], scalar=c["self_w"][:, 0:1],
                                                       in1=agg_ps[:], op0=ALU.mult, op1=ALU.add).then_inc(h0_done, 1)
                    if pair := at(2):
                        b, s = pair.slot % 2, pair.slot
                        if pair.has(2):
                            dve.wait_ge(agg_done, pair.before(2))
                        select_matrices(nc, c, pair, select[:, b]).then_inc(select_done, 1)
                        dve.wait_ge(edge_done, pair.done())
                        dve.wait_ge(gathered[pair.quad_slot], pair.rows_landed())
                        if pair.has(2):
                            dve.wait_ge(msg_rounded, pair.before(2))
                            dve.wait_ge(msg_split, pair.before(2))
                        nc.vector.tensor_tensor(raw[:, b, 0:pair.new], edge_ps[:, 0:pair.new],
                                                c["rows"][:, pair.quad_slot, slice(*pair.blocks)], ALU.add)\
                            .then_inc(rows_added, 1)
                    if pair := at(6):
                        dve.wait_ge(h2_ready, pair.done())
                        nodes = TAIL if pair.last() else PAIR
                        for h in range(2):
                            last = nc.vector.bn_stats(c["bn_stats"][:, h, bass.ds(pair.q, 1), :],
                                                      h2t[:, pair.slot, h, 0:nodes])
                        last.then_inc(stats_done, 1)
                    if pair := at(2):
                        b = pair.slot % 2
                        half, blocks = pair.quad_slot % 2, slice(*pair.blocks)
                        dve.wait_ge(msg_rounded, pair.done())
                        nc.vector.scalar_tensor_tensor(out=msg_lo[:, half, blocks], in0=raw[:, b, 0:pair.new],
                                                       scalar=0.0, in1=msg_hi[:, half, blocks].bitcast(F32), op0=ALU.max, op1=ALU.subtract)\
                            .then_inc(msg_split, 1)
                    if pair := at(1):
                        b = pair.slot % 2
                        dve.wait_ge(attr_rounded, pair.done())
                        if pair.has(2):
                            dve.wait_ge(edge_done, pair.before(2))
                        nc.vector.tensor_tensor(attr_lo[:, b, 0:pair.new * P], attr_ps[:, 0:pair.new * P],
                                                attr_hi[:, b, 0:pair.new * P].bitcast(F32),
                                                ALU.subtract).then_inc(attr_split, 1)
                    if pair := at(3):
                        b = pair.slot % 2
                        dve.wait_ge(h0_rounded, pair.done())
                        if pair.has(2):
                            dve.wait_ge(h1_done, pair.before(2))
                        nc.vector.tensor_tensor(h0t_lo[:, b], h0t_ps[:], h0t_hi[:, b].bitcast(F32),
                                                ALU.subtract).then_inc(h0_split, 1)

                pipeline(dve, step)


def batch_norm_scale(nc, keep):
    c = keep
    with ExitStack() as stack:
        m = Memory(nc, stack)
        mv = m.sb("bn_mv", [P, 2, 2])
        sd = m.sb("bn_sd", [P, 2])
        rs = m.sb("bn_rs", [P, 2])
        ma = m.sb("bn_ma", [P, 2])
        chain = m.sem("bn_chain")
        rooted = m.sem("bn_rooted")
        with nc.Block() as block:

            @block.vector
            def _(dve):
                for h in range(2):
                    nc.vector.bn_aggr(mv[:, h], c["bn_stats"][:, h].rearrange("p a b -> p (a b)")).then_inc(chain, 1)
                dve.wait_ge(rooted, 1)
                nc.vector.reciprocal(rs[:], sd[:]).then_inc(chain, 1)
                dve.wait_ge(chain, 3)
                nc.vector.tensor_tensor(c["bn_a"][:], c["gamma"][:], rs[:], ALU.mult).then_inc(chain, 1)
                dve.wait_ge(chain, 4)
                nc.vector.tensor_tensor(ma[:], mv[:, :, 0], c["bn_a"][:], ALU.mult).then_inc(chain, 1)
                dve.wait_ge(chain, 5)
                nc.vector.tensor_tensor(c["bn_c"][:], c["beta"][:], ma[:], ALU.subtract).then_inc(chain, 1)

            @block.scalar
            def _(act):
                act.wait_ge(chain, 2)
                nc.scalar.activation(sd[:], mv[:, :, 1], ACT.Sqrt, bias=c["ln_eps"][:, 0:1]).then_inc(rooted, 1)


def norm_pass(nc, keep, dram):
    c = keep
    with ExitStack() as stack:
        m = Memory(nc, stack)
        h2t = m.sb("h2t_in", [P, RING, 2, D])
        own = m.sb("x_sb", [P, RING, 2, D])
        zt = m.sb("zt", [P, 2, 2, D])
        res = m.sb("res", [P, 2, 2, D])
        x1 = m.sb("x1", [P, RING, 2, D])
        x1t_hi = m.sb("x1t_hi", [P, 2, 2, D], F32R)
        x1t_lo = m.sb("x1t_lo", [P, 2, 2, D], F32R)
        g = m.sb("g_out", [P, RING, 2, D])
        stats = m.sb("ln_stats", [P, 2, 2, 6])
        mv = m.sb("ln_mv", [P, 2, 2, 2])
        sd = m.sb("ln_sd", [P, 2, 2])
        rs = m.sb("ln_rs", [P, 2, 2])
        z_ps = m.ps("z_ps")
        x1t_ps = m.ps("x1t_ps")
        g_ps = m.ps("g_ps")
        loaded = [m.sem(f"nrm_loaded{s}") for s in range(RING)]
        stored = [m.sem(f"nrm_stored{s}") for s in range(RING)]
        names = ("z_ready z_turned res_added stats_done var_ready sd_ready rs_ready x1_ready x1_turned x1_rounded "
                 "x1_split dense_done g_ready")
        (z_ready, z_turned, res_added, stats_done, var_ready, sd_ready, rs_ready, x1_ready, x1_turned, x1_rounded,
         x1_split, dense_done, g_ready) = (m.sem("nrm_" + n) for n in names.split())

        with nc.Block() as block:

            @block.sync
            def _(sp):
                def step(at):
                    if pair := at(0):
                        s = pair.slot
                        if pair.has(RING):
                            sp.wait_ge(z_ready, pair.before(RING))
                            sp.wait_ge(res_added, pair.before(RING))
                        sp.dma_start(h2t[:, s], dram["h2"][bass.ds(pair.q, 1)].rearrange("o p c n -> p (o c) n"))\
                            .then_inc(loaded[s], 16)
                        sp.dma_start(own[:, s], rows_of(dram["x"], pair.q)).then_inc(loaded[s], 16)
                    if pair := at(5):
                        sp.wait_ge(x1_ready, pair.done())
                        sp.dma_start(rows_of(dram["x1"], pair.q), x1[:, pair.slot]).then_inc(stored[pair.slot], 16)
                    if pair := at(7):
                        sp.wait_ge(g_ready, pair.done())
                        sp.dma_start(rows_of(dram["ga"], pair.q), g[:, pair.slot]).then_inc(stored[pair.slot], 16)

                pipeline(sp, step)
                for s in range(RING):
                    sp.wait_ge(stored[s], 32 * (NP // RING))

            @block.scalar
            def _(act):
                def step(at):
                    if pair := at(2):
                        b, s = pair.slot % 2, pair.slot
                        act.wait_ge(loaded[s], pair.landed(2))
                        if pair.has(2):
                            act.wait_ge(z_turned, pair.before(2))
                        for h in range(2):
                            last = nc.scalar.activation(zt[:, b, h], h2t[:, s, h], ACT.Relu,
                                                        bias=c["bn_c"][:, h:h + 1], scale=c["bn_a"][:, h:h + 1])
                        last.then_inc(z_ready, 1)
                    if pair := at(6):
                        s = pair.slot
                        act.wait_ge(dense_done, pair.done())
                        if pair.has(RING):
                            act.wait_ge(stored[s], pair.turn * 32)
                        for j in range(2):
                            last = nc.scalar.activation(g[:, s, j], g_ps[:, j], ACT.Identity,
                                                        scale=c["dinv"][:, bass.ds(pair.q * 2 + j, 1)])
                        last.then_inc(g_ready, 1)
                    if pair := at(5):
                        b = pair.slot % 2
                        act.wait_ge(x1_turned, pair.done())
                        if pair.has(2):
                            act.wait_ge(dense_done, pair.before(2))
                        nc.scalar.copy(x1t_hi[:, b], x1t_ps[:]).then_inc(x1_rounded, 1)
                    if pair := at(3):
                        b = pair.slot % 2
                        act.wait_ge(var_ready, pair.done())
                        nc.scalar.activation(sd[:, b], mv[:, b, :, 1], ACT.Sqrt, bias=c["ln_eps"][:, 0:1])\
                            .then_inc(sd_ready, 1)

                pipeline(act, step)

            @block.tensor
            def _(pe):
                def step(at):
                    if pair := at(3):
                        pe.wait_ge(z_ready, pair.done())
                        if pair.has(1):
                            pe.wait_ge(res_added, pair.before(1))
                        zh = zt[:, pair.slot % 2]
                        for j in range(2):
                            for h in range(2):
                                last = nc.tensor.transpose(z_ps[:, j, h * P:(h + 1) * P], zh[:, h, j * P:(j + 1) * P],
                                                           c["ident"][:])
                        last.then_inc(z_turned, 1)
                    if pair := at(6):
                        b = pair.slot % 2
                        pe.wait_ge(x1_split, pair.done())
                        if pair.has(1):
                            pe.wait_ge(g_ready, pair.before(1))
                        dense_rows(nc, g_ps, [x1t_hi[:, b], x1t_lo[:, b]], [c["g1_hi"], c["g1_lo"]])\
                            .then_inc(dense_done, 1)
                    if pair := at(5):
                        pe.wait_ge(x1_ready, pair.done())
                        if pair.has(1):
                            pe.wait_ge(x1_split, pair.before(1))
                        transpose_rows(nc, c, x1t_ps, x1[:, pair.slot]).then_inc(x1_turned, 1)

                pipeline(pe, step)

            @block.vector
            def _(dve):
                def step(at):
                    if pair := at(4):
                        b, s = pair.slot % 2, pair.slot
                        dve.wait_ge(sd_ready, pair.done())
                        nc.vector.reciprocal(rs[:, b], sd[:, b]).then_inc(rs_ready, 1)
                        dve.wait_ge(rs_ready, pair.done())
                        if pair.has(RING):
                            dve.wait_ge(stored[s], pair.turn * 32)
                            dve.wait_ge(x1_turned, pair.before(RING))
                        for j in range(2):
                            last = nc.vector.tensor_scalar(x1[:, s, j], res[:, b, j], mv[:, b, j, 0:1],
                                                           rs[:, b, j:j + 1], ALU.subtract, ALU.mult)
                        last.then_inc(x1_ready, 1)
                    if pair := at(3):
                        b, s = pair.slot % 2, pair.slot
                        dve.wait_ge(z_turned, pair.done())
                        dve.wait_ge(loaded[s], pair.landed(2))
                        if pair.has(2):
                            dve.wait_ge(x1_ready, pair.before(2))
                        nc.vector.tensor_tensor(res[:, b], z_ps[:], own[:, s], ALU.add).then_inc(res_added, 1)
                        dve.wait_ge(res_added, pair.done())
                        layer_stats(nc, dve, pair, res[:, b], stats[:, b], mv[:, b], stats_done, var_ready,
                                    c["spare"][:, 1:2])
                    if pair := at(5):
                        b = pair.slot % 2
                        dve.wait_ge(x1_rounded, pair.done())
                        if pair.has(2):
                            dve.wait_ge(dense_done, pair.before(2))
                        nc.vector.tensor_tensor(x1t_lo[:, b], x1t_ps[:], x1t_hi[:, b].bitcast(F32),
                                                ALU.subtract).then_inc(x1_split, 1)

                pipeline(dve, step)


def gcn_pass(nc, keep, dram, name, source, target, bias, weight):
    c = keep
    with ExitStack() as stack:
        m = Memory(nc, stack)
        own = m.sb(name + "own", [P, RING, 2, D])
        rows_hi = m.sb(name + "rows_hi", [P, 2, BLOCKS, D], F32R)
        rows_lo = m.sb(name + "rows_lo", [P, 2, BLOCKS, D], F32R)
        select = m.sb(name + "select", [P, 2, FIRST + 1, PAIR], F32R)
        total = m.sb(name + "total", [P, 2, 2, D])
        scaled = m.sb(name + "scaled", [P, 2, 2, D])
        ht = m.sb(name + "ht", [P, 2, 2, D])
        g = m.sb(name + "g", [P, RING, 2, D])
        agg_ps = m.ps(name + "agg_ps")
        ht_ps = m.ps(name + "ht_ps")
        g_ps = m.ps(name + "g_ps")
        loaded = [m.sem(f"{name}loaded{s}") for s in range(RING)]
        gathered = [m.sem(f"{name}gathered{s}") for s in range(RING)]
        stored = [m.sem(f"{name}stored{s}") for s in range(RING)]
        names = ("index_copied rows_rounded rows_split select_done agg_done total_done total_scaled h_turned h_copied "
                 "dense_done g_ready")
        (index_copied, rows_rounded, rows_split, select_done, agg_done, total_done, total_scaled, h_turned, h_copied,
         dense_done, g_ready) = (m.sem(name + n) for n in names.split())

        with nc.Block() as block:

            @block.sync
            def _(sp):
                fast = sp.value_load(c["fast_i"][0:1, 0:1], min_val=0, max_val=1)

                def step(at):
                    if pair := at(0):
                        s = pair.slot
                        load_own(sp, fast, own[:, s], source, dram["base"], pair, loaded[s], total_done)
                    if pair := at(6):
                        s = pair.slot
                        sp.wait_ge(g_ready, pair.done())
                        sp.dma_start(rows_of(target, pair.q), g[:, s]).then_inc(stored[s], 16)

                pipeline(sp, step)
                for s in range(RING):
                    sp.wait_ge(stored[s], 16 * (NP // RING))

            @block.gpsimd
            def _(pool):
                bound = pool.to_reg(NPAD - 1)

                def step(at):
                    if (pair := at(0)) and not pair.odd:
                        gather_rows(nc, pool, c, pair, source, bound, index_copied, gathered, rows_split)

                pipeline(pool, step)

            @block.tensor
            def _(pe):
                def step(at):
                    if pair := at(3):
                        b, half = pair.slot % 2, pair.quad_slot % 2
                        pe.wait_ge(rows_split, pair.done())
                        pe.wait_ge(select_done, pair.done())
                        if pair.has(1):
                            pe.wait_ge(total_done, pair.before(1))
                        sum_into_nodes(nc, pair, agg_ps, select[:, b], [rows_hi[:, half], rows_lo[:, half]]).then_inc(agg_done, 1)
                    if pair := at(5):
                        pe.wait_ge(h_copied, pair.done())
                        if pair.has(1):
                            pe.wait_ge(g_ready, pair.before(1))
                        dense_rows(nc, g_ps, [ht[:, pair.slot % 2]], [weight]).then_inc(dense_done, 1)
                    if pair := at(4):
                        pe.wait_ge(total_scaled, pair.done())
                        if pair.has(1):
                            pe.wait_ge(h_copied, pair.before(1))
                        transpose_rows(nc, c, ht_ps, scaled[:, pair.slot % 2]).then_inc(h_turned, 1)

                pipeline(pe, step)

            @block.vector
            def _(dve):
                def step(at):
                    if pair := at(2):
                        b = pair.slot % 2
                        if pair.has(2):
                            dve.wait_ge(agg_done, pair.before(2))
                        select_matrices(nc, c, pair, select[:, b]).then_inc(select_done, 1)
                    if pair := at(3):
                        b, s = pair.slot % 2, pair.slot
                        dve.wait_ge(agg_done, pair.done())
                        dve.wait_ge(loaded[s], pair.landed(1))
                        if pair.has(2):
                            dve.wait_ge(total_scaled, pair.before(2))
                        nc.vector.tensor_tensor(total[:, b], agg_ps[:], own[:, s], ALU.add).then_inc(total_done, 1)
                    if pair := at(2):
                        half, blocks = pair.quad_slot % 2, slice(*pair.blocks)
                        dve.wait_ge(rows_rounded, pair.done())
                        if pair.has(pair.block_life):
                            dve.wait_ge(agg_done, pair.before(pair.block_life))
                        nc.vector.tensor_tensor(rows_lo[:, half, blocks], c["rows"][:, pair.quad_slot, blocks],
                                                rows_hi[:, half, blocks].bitcast(F32), ALU.subtract)\
                            .then_inc(rows_split, 1)

                pipeline(dve, step)

            @block.scalar
            def _(act):
                def step(at):
                    if pair := at(2):
                        half, blocks = pair.quad_slot % 2, slice(*pair.blocks)
                        act.wait_ge(gathered[pair.quad_slot], pair.rows_landed())
                        if pair.has(pair.block_life):
                            act.wait_ge(agg_done, pair.before(pair.block_life))
                        nc.scalar.copy(rows_hi[:, half, blocks], c["rows"][:, pair.quad_slot, blocks])\
                            .then_inc(rows_rounded, 1)
                    if pair := at(5):
                        act.wait_ge(dense_done, pair.done())
                        if pair.has(RING):
                            act.wait_ge(stored[pair.slot], pair.turn * 16)
                    if pair := at(4):
                        b = pair.slot % 2
                        act.wait_ge(h_turned, pair.done())
                        if pair.has(2):
                            act.wait_ge(dense_done, pair.before(2))
                        for h in range(2):
                            last = nc.scalar.activation(ht[:, b, h], ht_ps[:, h], ACT.Relu, bias=bias[:, h:h + 1])
                        last.then_inc(h_copied, 1)
                    if pair := at(5):
                        s = pair.slot
                        for j in range(2):
                            last = nc.scalar.activation(g[:, s, j], g_ps[:, j], ACT.Identity,
                                                        scale=c["dinv"][:, bass.ds(pair.q * 2 + j, 1)])
                        last.then_inc(g_ready, 1)
                    if pair := at(3):
                        b = pair.slot % 2
                        act.wait_ge(total_done, pair.done())
                        if pair.has(2):
                            act.wait_ge(h_turned, pair.before(2))
                        for j in range(2):
                            last = nc.scalar.activation(scaled[:, b, j], total[:, b, j], ACT.Identity,
                                                        scale=c["dinv"][:, bass.ds(pair.q * 2 + j, 1)])
                        last.then_inc(total_scaled, 1)

                pipeline(act, step)


def last_pass(nc, keep, dram, source, bias):
    c = keep
    with ExitStack() as stack:
        m = Memory(nc, stack)
        own = m.sb("fin_own", [P, RING, 2, D])
        x1 = m.sb("fin_x1", [P, RING, 2, D])
        select = m.sb("fin_select", [P, 2, FIRST + 1, PAIR])
        h = m.sb("fin_h", [P, 2, 2, D])
        res = m.sb("fin_res", [P, 2, 2, D])
        y = m.sb("fin_y", [P, RING, 2, D])
        stats = m.sb("fin_stats", [P, 2, 2, 6])
        mv = m.sb("fin_mv", [P, 2, 2, 2])
        sd = m.sb("fin_sd", [P, 2, 2])
        rs = m.sb("fin_rs", [P, 2, 2])
        shift = m.sb("fin_shift", [P, 2, 2])
        agg_ps = m.ps("fin_agg_ps", [P, 2, 2, D])
        loaded = [m.sem(f"fin_loaded{s}") for s in range(RING)]
        gathered = [m.sem(f"fin_gathered{s}") for s in range(RING)]
        stored = [m.sem(f"fin_stored{s}") for s in range(RING)]
        names = ("index_copied select_done agg_done h_ready res_added stats_done var_ready sd_ready "
                 "scale_steps y_ready")
        (index_copied, select_done, agg_done, h_ready, res_added, stats_done, var_ready, sd_ready,
         scale_steps, y_ready) = (m.sem("fin_" + n) for n in names.split())

        with nc.Block() as block:

            @block.sync
            def _(sp):
                fast = sp.value_load(c["fast_i"][0:1, 0:1], min_val=0, max_val=1)

                def step(at):
                    if pair := at(0):
                        s = pair.slot
                        load_own(sp, fast, own[:, s], source, dram["base"], pair, loaded[s], agg_done)
                        if pair.has(RING):
                            sp.wait_ge(res_added, pair.before(RING))
                        sp.dma_start(x1[:, s], rows_of(dram["x1"], pair.q)).then_inc(loaded[s], 16)
                    if pair := at(5):
                        s = pair.slot
                        sp.wait_ge(y_ready, pair.done())
                        sp.dma_start(rows_of(dram["out"], pair.q), y[:, s]).then_inc(stored[s], 16)

                pipeline(sp, step)
                for s in range(RING):
                    sp.wait_ge(stored[s], 16 * (NP // RING))

            @block.gpsimd
            def _(pool):
                bound = pool.to_reg(NPAD - 1)

                def step(at):
                    if (pair := at(0)) and not pair.odd:
                        gather_rows(nc, pool, c, pair, source, bound, index_copied, gathered, agg_done)

                pipeline(pool, step)

            @block.tensor
            def _(pe):
                def step(at):
                    if pair := at(2):
                        b, s = pair.slot % 2, pair.slot
                        pe.wait_ge(gathered[pair.quad_slot], pair.rows_landed())
                        pe.wait_ge(loaded[s], pair.landed(2))
                        pe.wait_ge(select_done, pair.done())
                        if pair.has(2):
                            pe.wait_ge(h_ready, pair.before(2))
                        for j in range(2):
                            nc.tensor.matmul(agg_ps[:, b, j], c["ident"][:], own[:, s, j], start=True, stop=False)
                            blocks = tile_blocks(pair, j)
                            for k in blocks:
                                last = nc.tensor.matmul(agg_ps[:, b, j], select[:, b, k, j * P:(j + 1) * P],
                                                        c["rows"][:, pair.quad_slot, pair.odd + k],
                                                        start=False, stop=k == blocks[-1])
                        last.then_inc(agg_done, 1)

                pipeline(pe, step)

            @block.vector
            def _(dve):
                def step(at):
                    if pair := at(1):
                        if pair.has(2):
                            dve.wait_ge(agg_done, pair.before(2))
                        select_matrices(nc, c, pair, select[:, pair.slot % 2]).then_inc(select_done, 1)
                    if pair := at(4):
                        b = pair.slot % 2
                        dve.wait_ge(sd_ready, pair.done())
                        nc.vector.reciprocal(rs[:, b], sd[:, b]).then_inc(scale_steps, 1)
                        dve.wait_ge(scale_steps, pair.q * 2 + 1)
                        nc.vector.scalar_tensor_tensor(out=shift[:, b], in0=mv[:, b, :, 0], scalar=-1.0,
                                                       in1=rs[:, b], op0=ALU.mult, op1=ALU.mult)\
                            .then_inc(scale_steps, 1)
                    if pair := at(3):
                        b, s = pair.slot % 2, pair.slot
                        dve.wait_ge(agg_done, pair.done())
                        for j in range(2):
                            last = nc.vector.scalar_tensor_tensor(
                                out=h[:, b, j], in0=agg_ps[:, b, j], scalar=c["dinv"][:, bass.ds(pair.q * 2 + j, 1)],
                                in1=bias[:], op0=ALU.mult, op1=ALU.add)
                        last.then_inc(h_ready, 1)
                        dve.wait_ge(h_ready, pair.done())
                        dve.wait_ge(loaded[s], pair.landed(2))
                        if pair.has(2):
                            dve.wait_ge(y_ready, pair.before(2))
                        nc.vector.scalar_tensor_tensor(out=res[:, b], in0=h[:, b], scalar=0.0, in1=x1[:, s],
                                                       op0=ALU.max, op1=ALU.add).then_inc(res_added, 1)
                        dve.wait_ge(res_added, pair.done())
                        layer_stats(nc, dve, pair, res[:, b], stats[:, b], mv[:, b], stats_done, var_ready,
                                    c["spare"][:, 1:2])

                pipeline(dve, step)

            @block.scalar
            def _(act):
                def step(at):
                    if pair := at(4):
                        b, s = pair.slot % 2, pair.slot
                        act.wait_ge(scale_steps, pair.done(2))
                        if pair.has(RING):
                            act.wait_ge(stored[s], pair.turn * 16)
                        for j in range(2):
                            last = nc.scalar.activation(y[:, s, j], res[:, b, j], ACT.Identity,
                                                        bias=shift[:, b, j:j + 1], scale=rs[:, b, j:j + 1])
                        last.then_inc(y_ready, 1)
                    if pair := at(3):
                        b = pair.slot % 2
                        act.wait_ge(var_ready, pair.done())
                        nc.scalar.activation(sd[:, b], mv[:, b, :, 1], ACT.Sqrt, bias=c["ln_eps"][:, 0:1])\
                            .then_inc(sd_ready, 1)

                pipeline(act, step)


def gnn(nc, dram):
    with ExitStack() as stack:
        m = Memory(nc, stack)
        dram = dict(dram)
        dram["h2"] = nc.dram_tensor("h2_scratch", [NP, P, 2, D], F32).ap()
        for name in ("x1", "ga", "gb", "base"):
            dram[name] = nc.dram_tensor(name + "_scratch", [NPAD, D], F32).ap()
        keep = {
            "w_edge": m.sb("w_edge", [DE, D]),
            "below": m.sb("below", [P, P]), "two_ones": m.sb("two_ones", [2, P], F32R),
            "b_edge2": m.sb("b_edge2", [2, D], F32R),
            "ident": m.sb("ident", [P, P]), "ones": m.sb("ones", [P, P]),
            "ln_eps": m.sb("ln_eps", [P, 1]), "eps": m.sb("eps_sb", [P, 1]),
            "iota16": m.sb("iota16", [P, NT], F16), "iota32": m.sb("iota32", [P, QUAD]),
            "rows": m.sb("rows", [P, QUAD_RING, BLOCKS, D]), "index": m.sb("index", [P, QUAD_RING, BLOCKS], U32),
            "dinv": m.sb("dinv", [P, NT]), "starts": m.sb("starts_i", [P, NT], I32),
            "fast": m.sb("fast", [P, 1]), "fast_i": m.sb("fast_i", [P, 1], I32),
            "eps1": m.sb("eps1", [P, 2]), "self_w": m.sb("self_w", [P, 1]),
            "place": m.sb("place", [P, NQ, BLOCKS]), "node": m.sb("node_i", [P, NQ, BLOCKS], U32),
            "bn_stats": m.sb("bn_stats", [P, 2, NP, 6]), "bn_a": m.sb("bn_a", [P, 2]), "bn_c": m.sb("bn_c", [P, 2]),
            "rows_in": m.sem("rows_in"), "spare": m.sb("spare", [P, 3]),
            "general_sems": [m.sem(f"gen_{n}") for n in (
                "copy_in scaled copy_out block_in ids_steps turned same_ready index_steps index_ready "
                "attr_turned attr_copied edge_done msg_steps msg_ready summed gathered added "
                "scattered carried").split()],
        }
        for name in ("w1", "w2", "g1", "g2", "g3"):
            keep[name] = m.sb(name + "_sb", [P, 2, D])
        for name in SPLIT:
            for part in ("_hi", "_lo"):
                keep[name + part] = m.sb(name + part, [P, D] if name == "w_edge" else [P, 2, D], F32R)
        for name in ("b1", "b2", "gamma", "beta", "gb1", "gb2"):
            keep[name] = m.sb(name + "_sb", [P, 2])
        for name in ("b_edge", "gb3"):
            keep[name] = m.sb(name + "_sb", [P, D])

        constants(nc, keep, dram)
        degrees(nc, keep, dram)
        slot_tables(nc, keep, dram)
        general_sum(nc, keep, dram, 0, dram["x"], True)
        gin_pass(nc, keep, dram)
        batch_norm_scale(nc, keep)
        norm_pass(nc, keep, dram)
        general_sum(nc, keep, dram, 1, dram["ga"], False)
        gcn_pass(nc, keep, dram, "gcn1_", dram["ga"], dram["gb"], keep["gb1"], keep["g2"])
        general_sum(nc, keep, dram, 2, dram["gb"], False)
        gcn_pass(nc, keep, dram, "gcn2_", dram["gb"], dram["ga"], keep["gb2"], keep["g3"])
        general_sum(nc, keep, dram, 3, dram["ga"], False)
        last_pass(nc, keep, dram, dram["ga"], keep["gb3"])


def kernel(x, src, dst, edge_attr_128, L0_gnn_W_edge, L0_gnn_b_edge, L0_gnn_W1, L0_gnn_b1, L0_gnn_W2, L0_gnn_b2,
           L0_gnn_eps, L0_gnn_gamma, L0_gnn_beta, L1_gnn_W1, L1_gnn_b1, L1_gnn_W2, L1_gnn_b2, L1_gnn_W3, L1_gnn_b3):
    import numpy as np
    import concourse.bacc as bacc
    from concourse.bass_utils import run_bass_kernel_spmd

    def padded(a, rows, fill=0):
        a = np.asarray(a)
        return np.concatenate([a, np.full((rows - a.shape[0],) + a.shape[1:], fill, a.dtype)])

    edges = padded(np.stack([np.asarray(src), np.asarray(dst)], axis=1), EPAD, FAR)
    edges[E:, 0] = 0
    arrays = {
        "x": padded(x, NPAD), "edges": edges, "edge_attr": padded(edge_attr_128, EPAD),
        "w_edge": L0_gnn_W_edge, "b_edge": L0_gnn_b_edge, "w1": L0_gnn_W1, "b1": L0_gnn_b1, "w2": L0_gnn_W2,
        "b2": L0_gnn_b2, "eps": np.asarray(L0_gnn_eps).reshape(1), "gamma": L0_gnn_gamma, "beta": L0_gnn_beta,
        "g1": np.asarray(L1_gnn_W1).T, "gb1": L1_gnn_b1, "g2": np.asarray(L1_gnn_W2).T, "gb2": L1_gnn_b2,
        "g3": np.asarray(L1_gnn_W3).T, "gb3": L1_gnn_b3,
    }
    nc = bacc.Bacc("TRN2", target_bir_lowering=False, num_devices=1)
    arrays = {name: np.ascontiguousarray(a) for name, a in arrays.items()}
    dram = {name: nc.dram_tensor(name + "_in", a.shape, mybir.dt.from_np(a.dtype), kind="ExternalInput").ap()
            for name, a in arrays.items()}
    dram["out"] = nc.dram_tensor("out", (NPAD, D), F32, kind="ExternalOutput").ap()
    gnn(nc, dram)
    result = run_bass_kernel_spmd(nc, [{name + "_in": a for name, a in arrays.items()}], core_ids=[0])
    return result.results[0]["out"][:N]
```

```python
from contextlib import ExitStack

import concourse.bass as bass
from concourse import mybir

P = 128
D = 256
N = 50000
E = 50000
DE = 128
PAIR = 2 * P
NP = -(-N // PAIR)
NT = 2 * NP
NPAD = NP * PAIR
QUAD = 2 * PAIR
NQ = NP // 2
BLOCKS = 5
FIRST = 3
SLOTS = BLOCKS * P
EPAD = NPAD + SLOTS
TAIL = N - (NP - 1) * PAIR
NO_ROW = 1 << 20
FAR = 1 << 20
RING = 4
GROUP = 8
QUAD_RING = GROUP // 2
MAX_LAG = 14
GROUPS = -(-(NP + MAX_LAG) // GROUP)
PEEL = 3
LOOP_END = NP // GROUP - 1
BN_EPS = 1e-5
LN_EPS = 1e-5

ALU = mybir.AluOpType
ACT = mybir.ActivationFunctionType
AX = mybir.AxisListType
F32 = mybir.dt.float32
F32R = mybir.dt.float32r
F16 = mybir.dt.float16
BF16 = mybir.dt.bfloat16
I32 = mybir.dt.int32
U32 = mybir.dt.uint32


SPLIT = ("w_edge", "w1", "w2", "g1", "g2", "g3")


class Pair:

    def __init__(self, group, place):
        self.group = group
        self.q = group * GROUP + place
        self.turn, self.slot = group * (GROUP // RING) + place // RING, place % RING
        self.quad, self.quad_slot = group * QUAD_RING + place // 2, place // 2
        self.place, self.odd = place, place % 2
        self.blocks = (FIRST, BLOCKS) if self.odd else (0, FIRST)
        self.new = self.blocks[1] - self.blocks[0]
        self.block_life = 4 if self.odd else 3

    def done(self, per=1):
        return (self.q + 1) * per

    def before(self, back):
        return self.q + 1 - back

    def has(self, back):
        return not isinstance(self.q, int) or self.q >= back

    def landed(self, dmas):
        return (self.turn + 1) * (16 * dmas)

    def rows_landed(self):
        return (self.group + 1) * (16 * BLOCKS)

    def last(self):
        return isinstance(self.q, int) and self.q == NP - 1


def pipeline(eng, step):

    def group(number):
        for k in range(GROUP):
            def pair_at(lag, k=k):
                pair = Pair(number + (k - lag) // GROUP, (k - lag) % GROUP)
                if isinstance(pair.q, int) and not 0 <= pair.q < NP:
                    return None
                return pair
            step(pair_at)

    for number in range(PEEL):
        group(number)
    with eng.Fori(PEEL, LOOP_END) as number:
        group(number)
    for number in range(LOOP_END, GROUPS):
        group(number)


def rows_of(dram, q):
    return dram[bass.ds(q * PAIR, PAIR), :].rearrange("(j p) d -> p j d", p=P)


class Memory:

    def __init__(self, nc, stack):
        self.nc, self.stack = nc, stack

    def sb(self, name, shape, dt=F32):
        return self.stack.enter_context(self.nc.sbuf_tensor(name, shape, dt))

    def ps(self, name, shape=(P, 2, D)):
        return self.stack.enter_context(self.nc.psum_tensor(name, list(shape), F32))

    def sem(self, name):
        return self.stack.enter_context(self.nc.semaphore(name))


def constants(nc, keep, dram):
    c = keep
    with ExitStack() as stack:
        m = Memory(nc, stack)
        weights_in = m.sem("weights_in")
        pool_done = m.sem("const_pool_done")
        dve_done = m.sem("const_dve_done")
        iota_i = m.sb("iota_i", [P, QUAD], I32)
        pair_b = m.sb("b_edge_twice", [2, D])
        row_hi = m.sb("b_edge_hi", [2, D])
        row_i = m.sb("row_number_i", [2, 1], I32)
        row = m.sb("row_number", [2, 1])
        with nc.Block() as block:

            @block.sync
            def _(sp):
                def load(out, in_):
                    sp.dma_start(out, in_).then_inc(weights_in, 16)

                load(c["w_edge"][:], dram["w_edge"][:, :])
                for name in ("w1", "w2", "g1", "g2", "g3"):
                    load(c[name][:], dram[name].rearrange("(c p) m -> p c m", p=P))
                for name in ("b1", "b2", "gamma", "beta", "gb1", "gb2"):
                    for h in range(2):
                        load(c[name][:, h:h + 1], dram[name][h * P:(h + 1) * P].rearrange("(p o) -> p o", o=1))
                sp.wait_ge(weights_in, 16 * (6 + 12))

            @block.scalar
            def _(act):
                for name in ("b_edge", "gb3"):
                    act.dma_start(c[name][:], dram[name].rearrange("(o d) -> o d", o=1)
                                  .broadcast_to([P, D])).then_inc(c["rows_in"], 16)
                act.dma_start(c["eps"][:], dram["eps"].rearrange("(o d) -> o d", o=1)
                              .broadcast_to([P, 1])).then_inc(c["rows_in"], 16)
                act.dma_start(pair_b[:], dram["b_edge"].rearrange("(o d) -> o d", o=1)
                              .broadcast_to([2, D])).then_inc(c["rows_in"], 16)
                act.wait_ge(c["rows_in"], 16 * 4)

            @block.gpsimd
            def _(pool):
                nc.gpsimd.memset(c["ident"][:], 0.0).then_inc(pool_done, 1)
                nc.gpsimd.memset(c["ones"][:], 1.0).then_inc(pool_done, 1)
                nc.gpsimd.memset(c["ln_eps"][:], LN_EPS).then_inc(pool_done, 1)
                nc.gpsimd.iota(iota_i[:], pattern=[[1, QUAD]], base=0, channel_multiplier=0).then_inc(pool_done, 1)
                nc.gpsimd.iota(row_i[:], pattern=[[0, 1]], base=0, channel_multiplier=1).then_inc(pool_done, 1)
                pool.wait_ge(pool_done, 5)
                nc.gpsimd.affine_select(out=c["below"][:], in_=c["ones"][:], compare_op=ALU.is_gt, fill=0.0,
                                        base=0, pattern=[[-1, P]], channel_multiplier=1).then_inc(pool_done, 1)
                nc.gpsimd.affine_select(out=c["ident"][:], in_=c["ident"][:], compare_op=ALU.not_equal, fill=1.0,
                                        base=0, pattern=[[-1, P]], channel_multiplier=1).then_inc(pool_done, 1)

            @block.vector
            def _(dve):
                for s in range(QUAD_RING):
                    nc.vector.memset(c["rows"][:, s], 0.0)
                nc.vector.memset(c["eps1"][:, 1:2], 1.0)
                dve.wait_ge(pool_done, 7)
                nc.vector.tensor_copy(c["iota16"][:], iota_i[:, 0:NT])
                nc.vector.tensor_copy(c["iota32"][:], iota_i[:])
                dve.wait_ge(weights_in, 16 * (6 + 12))
                for name in SPLIT:
                    nc.vector.tensor_copy(c[name + "_hi"][:], c[name][:]).then_inc(dve_done, 1)
                dve.wait_ge(dve_done, len(SPLIT))
                for name in SPLIT:
                    nc.vector.tensor_tensor(c[name + "_lo"][:], c[name][:], c[name + "_hi"][:].bitcast(F32),
                                            ALU.subtract)
                dve.wait_ge(c["rows_in"], 16 * 4)
                nc.vector.tensor_copy(c["two_ones"][:], c["ones"][0:2, :])
                nc.vector.tensor_copy(c["b_edge2"][:], pair_b[:]).then_inc(dve_done, 1)
                nc.vector.tensor_copy(row[:], row_i[:]).then_inc(dve_done, 1)
                dve.wait_ge(dve_done, len(SPLIT) + 2)
                nc.vector.tensor_scalar(row_hi[:], c["b_edge2"][:].bitcast(F32), row[:, 0:1], None, ALU.mult)\
                    .then_inc(dve_done, 1)
                dve.wait_ge(dve_done, len(SPLIT) + 3)
                nc.vector.tensor_tensor(c["b_edge2"][:], pair_b[:], row_hi[:], ALU.subtract)


def degrees(nc, keep, dram):
    c = keep
    COLS = NT
    UNROLL = 8
    DEPTH = 4
    with ExitStack() as stack:
        m = Memory(nc, stack)
        edges = m.sb("edges_sb", [P, COLS, 2], I32)
        after = m.sb("edges_next", [P, COLS, 2], I32)
        hi_i = m.sb("hi_i", [P, COLS], I32)
        lo_i = m.sb("lo_i", [P, COLS], I32)
        hi = m.sb("hi", [P, COLS])
        lo = m.sb("lo", [P, COLS])
        hot_hi = m.sb("hot_hi", [P, DEPTH, NT], BF16)
        hot_lo = m.sb("hot_lo", [P, DEPTH, P], BF16)
        deg = m.sb("deg", [P, NT])
        deg1 = m.sb("deg1", [P, NT])
        root = m.sb("root", [P, NT])
        zero = m.sb("zero_row", [P, NT])
        counts = m.sb("counts", [P, NT])
        ends = m.sb("ends", [P, NT])
        starts = m.sb("starts", [P, NT])
        falls = m.sb("falls", [P, NT])
        nfalls = m.sb("nfalls", [P, 1])
        outside = m.sb("outside", [P, 6, NQ])
        most = m.sb("most", [P, 1])
        fits = m.sb("fits", [P, 1])
        root2 = m.sb("root2", [P, NT])
        hist = m.ps("hist", [P, NT])
        colsum = m.ps("colsum", [P, NT])
        fallsum = m.ps("fallsum", [P, 1])
        edges_in = m.sem("edges_in")
        split = m.sem("split")
        hot = m.sem("hot")
        used = m.sem("hot_used")
        chain = m.sem("deg_chain")
        deg_steps = m.sem("deg_steps")
        summed = m.sem("summed")
        rooted = m.sem("rooted")

        with nc.Block() as block:

            @block.sync
            def _(sp):
                sp.dma_start(edges[:], dram["edges"][0:P * COLS, :].rearrange("(p c) t -> p c t", p=P))\
                    .then_inc(edges_in, 16)
                sp.dma_start(after[:], dram["edges"][1:P * COLS + 1, :].rearrange("(p c) t -> p c t", p=P))\
                    .then_inc(edges_in, 16)

            @block.vector
            def _(dve):
                dve.wait_ge(edges_in, 32)
                nc.vector.tensor_scalar(hi_i[:], edges[:, :, 1], 7, None, ALU.arith_shift_right).then_inc(split, 1)
                nc.vector.tensor_scalar(lo_i[:], edges[:, :, 1], P - 1, None, ALU.bitwise_and).then_inc(split, 1)
                dve.wait_ge(split, 2)
                nc.vector.tensor_copy(hi[:], hi_i[:]).then_inc(split, 1)
                nc.vector.tensor_copy(lo[:], lo_i[:]).then_inc(split, 1)
                dve.wait_ge(split, 4)

                def hot_step(t, k):
                    if not isinstance(t, int) or t >= DEPTH:
                        dve.wait_ge(used, t - DEPTH + 1)
                    nc.vector.tensor_scalar(hot_lo[:, k % DEPTH], c["iota16"][:, 0:P], lo[:, bass.ds(t, 1)], None,
                                            ALU.is_equal)
                    nc.vector.tensor_scalar(hot_hi[:, k % DEPTH], c["iota16"][:], hi[:, bass.ds(t, 1)], None,
                                            ALU.is_equal).then_inc(hot, 1)

                for k in range(UNROLL):
                    hot_step(k, k)
                with dve.Fori(1, COLS // UNROLL) as i:
                    for k in range(UNROLL):
                        hot_step(i * UNROLL + k, k)

                dve.wait_ge(used, COLS)
                nc.vector.tensor_copy(deg[:], hist[:]).then_inc(deg_steps, 1)
                dve.wait_ge(deg_steps, 1)
                nc.vector.tensor_scalar(deg1[:], deg[:], 1.0, None, ALU.add).then_inc(deg_steps, 1)
                nc.vector.tensor_tensor(falls[:], edges[:, :, 1], after[:, :, 1], ALU.is_gt).then_inc(chain, 1)
                nc.vector.memset(zero[:], 0.0).then_inc(chain, 1)
                dve.wait_ge(chain, 2)
                nc.vector.tensor_reduce(nfalls[:], falls[:], AX.X, ALU.add).then_inc(chain, 1)
                dve.wait_ge(summed, 1)
                nc.vector.tensor_copy(counts[:], colsum[:]).then_inc(chain, 1)
                dve.wait_ge(chain, 4)
                nc.vector.tensor_tensor_scan(ends[:], counts[:], zero[:], 0.0, ALU.add, ALU.add).then_inc(chain, 1)
                dve.wait_ge(chain, 5)
                nc.vector.tensor_tensor(starts[:], ends[:], counts[:], ALU.subtract).then_inc(chain, 1)
                dve.wait_ge(chain, 6)
                nc.vector.tensor_copy(c["starts"][:], starts[:]).then_inc(chain, 1)
                quad_ends = ends[:].rearrange("p (q t) -> p q t", t=4)
                quad_start = starts[:].rearrange("p (q t) -> p q t", t=4)[:, :, 0]
                for t in range(4):
                    nc.vector.scalar_tensor_tensor(out=outside[:, t], in0=quad_ends[:, :, t],
                                                   scalar=float(-(t + 2) * P), in1=quad_start,
                                                   op0=ALU.add, op1=ALU.subtract).then_inc(chain, 1)
                for t in (1, 2):
                    nc.vector.scalar_tensor_tensor(out=outside[:, 3 + t], in0=quad_start, scalar=float(t * P),
                                                   in1=quad_ends[:, :, t], op0=ALU.add, op1=ALU.subtract)\
                        .then_inc(chain, 1)
                dve.wait_ge(chain, 13)
                nc.vector.tensor_reduce(most[:], outside[:].rearrange("p t q -> p (t q)"), AX.X, ALU.max)\
                    .then_inc(chain, 1)
                dve.wait_ge(chain, 14)
                nc.vector.tensor_scalar(fits[:], most[:], 0.0, None, ALU.is_le).then_inc(chain, 1)
                dve.wait_ge(chain, 15)
                dve.wait_ge(summed, 2)
                nc.vector.scalar_tensor_tensor(out=c["fast"][:], in0=fallsum[:], scalar=0.0, in1=fits[:],
                                               op0=ALU.is_equal, op1=ALU.mult).then_inc(chain, 1)
                dve.wait_ge(rooted, 1)
                nc.vector.reciprocal(falls[:], root[:]).then_inc(chain, 1)
                dve.wait_ge(chain, 17)
                nc.vector.tensor_tensor(zero[:], falls[:], deg1[:], ALU.mult).then_inc(chain, 1)
                dve.wait_ge(chain, 18)
                nc.vector.tensor_tensor(root2[:], zero[:], root[:], ALU.add).then_inc(chain, 1)
                dve.wait_ge(chain, 19)
                nc.vector.tensor_scalar(root2[:], root2[:], 0.5, None, ALU.mult).then_inc(chain, 1)
                dve.wait_ge(chain, 20)
                nc.vector.reciprocal(c["dinv"][:], root2[:]).then_inc(chain, 1)
                nc.vector.tensor_copy(c["fast_i"][:], c["fast"][:]).then_inc(chain, 1)
                nc.vector.tensor_scalar(c["eps1"][:, 0:1], c["eps"][:], 1.0, None, ALU.add).then_inc(chain, 1)
                nc.vector.tensor_scalar(c["self_w"][:], c["eps"][:], c["fast"][:, 0:1], 1.0, ALU.mult, ALU.add)\
                    .then_inc(chain, 1)

            @block.tensor
            def _(pe):
                def count_step(t, k):
                    pe.wait_ge(hot, t + 1)
                    nc.tensor.matmul(hist[:], hot_lo[:, k % DEPTH], hot_hi[:, k % DEPTH],
                                     start=isinstance(t, int) and t == 0,
                                     stop=isinstance(t, int) and t == COLS - 1,
                                     skip_group_check=True).then_inc(used, 1)

                for k in range(UNROLL):
                    count_step(k, k)
                with pe.Fori(1, COLS // UNROLL) as i:
                    for k in range(UNROLL):
                        count_step(i * UNROLL + k, k)
                pe.wait_ge(deg_steps, 1)
                nc.tensor.matmul(colsum[:], c["ones"][:], deg[:], start=True, stop=True).then_inc(summed, 1)
                pe.wait_ge(chain, 3)
                nc.tensor.matmul(fallsum[:], c["ones"][:], nfalls[:], start=True, stop=True).then_inc(summed, 1)

            @block.scalar
            def _(act):
                act.wait_ge(deg_steps, 2)
                nc.scalar.activation(root[:], deg1[:], ACT.Sqrt).then_inc(rooted, 1)


def slot_tables(nc, keep, dram):
    c = keep
    with ExitStack() as stack:
        m = Memory(nc, stack)
        window = m.sb("window", [P, NQ, BLOCKS, 2], I32)
        base_i = m.sb("base_i", [P, NQ, BLOCKS], I32)
        base = m.sb("base", [P, NQ, BLOCKS])
        place = m.sb("raw_place", [P, NQ, BLOCKS])
        low = m.sb("low", [P, NQ, BLOCKS])
        valid = m.sb("valid", [P, NQ, BLOCKS])
        node = m.sb("node", [P, NQ, BLOCKS])
        windows_in = m.sem("windows_in")
        chain = m.sem("slot_chain")
        UNROLL = 7

        def windows(eng, first):
            with eng.Fori(0, NQ // (2 * UNROLL)) as i:
                for k in range(UNROLL):
                    q = i * (2 * UNROLL) + 2 * k + first
                    start = eng.value_load(c["starts"][0:1, bass.ds(q * 4, 1)], min_val=0, max_val=E)
                    eng.dma_start(window[:, bass.ds(q, 1)].rearrange("p o b t -> p (o b) t"),
                                  dram["edges"][bass.ds(start, SLOTS), :].rearrange("(b p) t -> p b t", p=P))\
                       .then_inc(windows_in, 16)

        with nc.Block() as block:

            @block.sync
            def _(sp):
                windows(sp, 0)

            @block.scalar
            def _(act):
                windows(act, 1)

            @block.gpsimd
            def _(pool):
                nc.gpsimd.iota(base_i[:], pattern=[[QUAD, NQ], [0, BLOCKS]], base=0, channel_multiplier=0)\
                    .then_inc(chain, 1)

            @block.vector
            def _(dve):
                dve.wait_ge(chain, 1)
                nc.vector.tensor_copy(base[:], base_i[:]).then_inc(chain, 1)
                dve.wait_ge(chain, 2)
                dve.wait_ge(windows_in, 16 * NQ)
                nc.vector.tensor_tensor(place[:], window[:, :, :, 1], base[:], ALU.subtract).then_inc(chain, 1)
                dve.wait_ge(chain, 3)
                nc.vector.tensor_scalar(low[:], place[:], 0.0, c["fast"][:, 0:1], ALU.is_ge, ALU.mult)\
                    .then_inc(chain, 1)
                dve.wait_ge(chain, 4)
                nc.vector.scalar_tensor_tensor(out=valid[:], in0=place[:], scalar=float(QUAD), in1=low[:],
                                               op0=ALU.is_lt, op1=ALU.mult).then_inc(chain, 1)
                dve.wait_ge(chain, 5)
                nc.vector.scalar_tensor_tensor(out=node[:], in0=window[:, :, :, 0], scalar=float(-NO_ROW),
                                               in1=valid[:], op0=ALU.add, op1=ALU.mult).then_inc(chain, 1)
                nc.vector.scalar_tensor_tensor(out=base[:], in0=place[:], scalar=1.0, in1=valid[:],
                                               op0=ALU.add, op1=ALU.mult).then_inc(chain, 1)
                dve.wait_ge(chain, 7)
                nc.vector.tensor_scalar(c["node"][:], node[:], float(NO_ROW), None, ALU.add).then_inc(chain, 1)
                nc.vector.tensor_scalar(c["place"][:], base[:], -1.0, None, ALU.add).then_inc(chain, 1)


def gather_rows(nc, pool, c, pair, source, bound, index_copied, gathered, rows_free):
    s = pair.quad_slot
    if pair.has(GROUP):
        pool.wait_ge(rows_free, pair.before(GROUP - 1))
    nc.gpsimd.tensor_copy(c["index"][:, s], c["node"][:, bass.ds(pair.quad, 1), :]).then_inc(index_copied, 1)
    pool.wait_ge(index_copied, pair.quad + 1)
    nc.gpsimd.tensor_tensor(c["spare"][:, 0:1], c["ln_eps"][:], c["ln_eps"][:], ALU.add)
    for b in range(BLOCKS):
        pool.indirect_dma_start(out=c["rows"][:, s, b], out_offset=None, in_=source[:, :],
                                in_offset=bass.IndirectOffsetOnAxis(ap=c["index"][:, s, b:b + 1], axis=0),
                                bounds_check=bound, oob_is_err=False).then_inc(gathered[s], 16)


def tile_blocks(pair, j):
    t = 2 * pair.odd + j
    return range(max(t - 1, 0) - pair.odd, t + 2 - pair.odd)


def select_matrices(nc, c, pair, select):
    for b in range(FIRST + pair.odd):
        tiles = [j for j in range(2) if b in tile_blocks(pair, j)]
        first, end = tiles[0] * P, (tiles[-1] + 1) * P
        last = nc.vector.tensor_scalar(select[:, b, first:end],
                                       c["iota32"][:, pair.odd * PAIR + first:pair.odd * PAIR + end],
                                       c["place"][:, bass.ds(pair.quad, 1), pair.odd + b], None, ALU.is_equal)
    return last


def sum_into_nodes(nc, pair, out, select, parts):
    for j in range(2):
        terms = [(b, rows) for b in tile_blocks(pair, j) for rows in parts]
        for n, (b, rows) in enumerate(terms):
            last = nc.tensor.matmul(out[:, j], select[:, b, j * P:(j + 1) * P], rows[:, pair.odd + b],
                                    start=n == 0, stop=n == len(terms) - 1)
    return last


def transpose_rows(nc, c, out, rows):
    for j in range(2):
        for h in range(2):
            last = nc.tensor.transpose(out[:, h, j * P:(j + 1) * P], rows[:, j, h * P:(h + 1) * P], c["ident"][:])
    return last


def products(parts, weight):
    if len(parts) == 1:
        return [(parts[0], weight[0])]
    (hi, lo), (w_hi, w_lo) = parts, weight
    return [(hi, w_hi), (lo, w_hi), (hi, w_lo)]


def dense_rows(nc, out, parts, weight):
    terms = [(h, a, w) for h in range(2) for a, w in products(parts, weight)]
    for j in range(2):
        for n, (h, a, w) in enumerate(terms):
            last = nc.tensor.matmul(out[:, j], a[:, h, j * P:(j + 1) * P], w[:, h],
                                    start=n == 0, stop=n == len(terms) - 1)
    return last


def dense_cols(nc, out, parts, weight):
    terms = [(h, a, w) for h in range(2) for a, w in products(parts, weight)]
    for m in range(2):
        for n, (h, a, w) in enumerate(terms):
            last = nc.tensor.matmul(out[:, m], w[:, h, m * P:(m + 1) * P], a[:, h],
                                    start=n == 0, stop=n == len(terms) - 1)
    return last


def load_own(sp, fast, out, source, base, pair, landed, slot_free, ring=RING):
    for ran, rows in ((1, source), (0, base)):
        with sp.If(fast == ran):
            if pair.has(ring):
                sp.wait_ge(slot_free, pair.before(ring))
            sp.dma_start(out, rows_of(rows, pair.q)).then_inc(landed, 16)


def layer_stats(nc, rows, stats, stats_steps):
    for j in range(2):
        last = nc.vector.bn_stats(stats[:, j], rows[:, j])
    last.then_inc(stats_steps, 1)


def layer_variance(nc, dve, pair, stats, mv, stats_steps, spare):
    dve.wait_ge(stats_steps, pair.q * 2 + 1)
    nc.vector.memset(spare, 0.0)
    for j in range(2):
        last = nc.vector.bn_aggr(mv[:, j], stats[:, j])
    last.then_inc(stats_steps, 1)


def general_sum(nc, keep, dram, number, source, gin):
    c = keep
    base = dram["base"]
    sems = c["general_sems"]
    (copy_in, scaled, copy_out, block_in, ids_steps, turned, index_steps,
     attr_turned, attr_copied, edge_done, msg_steps, msg_ready, summed, gathered, added,
     scattered, carried) = sems
    done_pairs, done_blocks = number * NP, number * NT
    loads = 2 if gin else 1
    with ExitStack() as stack:
        m = Memory(nc, stack)
        name = f"gen{number}_"
        own = m.sb(name + "own", [P, 2, D])
        own_out = m.sb(name + "own_out", [P, 2, D])
        ids = m.sb(name + "ids", [P, 2], I32)
        src = m.sb(name + "src", [P, 1], U32)
        dst = m.sb(name + "dst", [P, 1])
        dst_cols = m.sb(name + "dst_cols", [P, P])
        same = m.sb(name + "same", [P, P])
        earlier = m.sb(name + "earlier", [P, P])
        count = m.sb(name + "count", [P, 1])
        first = m.sb(name + "first", [P, 1])
        index_f = m.sb(name + "index_f", [P, 1])
        index = m.sb(name + "index", [P, 1], U32)
        attr = m.sb(name + "attr", [P, DE])
        attr_t = m.sb(name + "attr_t", [P, P])
        msg0 = m.sb(name + "msg0", [P, D])
        msg1 = m.sb(name + "msg1", [P, D])
        msg = m.sb(name + "msg", [P, D])
        total = m.sb(name + "total", [P, D])
        rows = c["rows"][:, 0, 0]
        current = c["rows"][:, 0, 1]
        dst_ps = m.ps(name + "dst_ps", [P, P])
        attr_ps = m.ps(name + "attr_ps", [P, P])
        edge_ps = m.ps(name + "edge_ps", [P, D])
        sum_ps = m.ps(name + "sum_ps", [P, D])

        with nc.Block() as block:

            @block.sync
            def _(sp):
                fast = sp.value_load(c["fast_i"][0:1, 0:1], min_val=0, max_val=1)
                with sp.If(fast == 0):
                    def copy_rows(q):
                        sp.dma_start(own[:], rows_of(source, q)).then_inc(copy_in, 16)
                        sp.wait_ge(scaled, q + (done_pairs + 1))
                        sp.dma_start(rows_of(base, q), own_out[:]).then_inc(copy_out, 16)

                    def load_block(e):
                        sp.dma_start(ids[:], dram["edges"][bass.ds(e * P, P), :]).then_inc(block_in, 16)
                        if gin:
                            sp.dma_start(attr[:], dram["edge_attr"][bass.ds(e * P, P), :]).then_inc(block_in, 16)

                    copy_rows(0)
                    with sp.Fori(1, NP) as q:
                        sp.wait_ge(copy_out, (q + done_pairs) * 16)
                        copy_rows(q)
                    sp.wait_ge(copy_out, (done_pairs + NP) * 16)
                    load_block(0)
                    with sp.Fori(1, NT) as e:
                        sp.wait_ge(scattered, (e + done_blocks) * 16)
                        load_block(e)
                    sp.wait_ge(scattered, (done_blocks + NT) * 16)

            @block.gpsimd
            def _(pool):
                bound = pool.to_reg(NPAD - 1)
                fast = pool.value_load(c["fast_i"][0:1, 0:1], min_val=0, max_val=1)

                def carry():
                    nc.gpsimd.tensor_tensor(c["spare"][:, 2:3], c["ln_eps"][:], c["ln_eps"][:], ALU.add)\
                        .then_inc(carried, 1)

                with pool.If(fast == 0):
                    carry()
                    with pool.Fori(0, NT) as e:
                        turn = e + (done_blocks + 1)
                        pool.wait_ge(ids_steps, turn * 2 - 1)
                        pool.wait_ge(carried, turn * 3 + (number - 2))
                        carry()
                        pool.indirect_dma_start(out=rows, out_offset=None, in_=source[:, :],
                                                in_offset=bass.IndirectOffsetOnAxis(ap=src[:, 0:1], axis=0),
                                                bounds_check=bound, oob_is_err=False).then_inc(gathered, 16)
                        pool.wait_ge(index_steps, turn * 6)
                        pool.wait_ge(carried, turn * 3 + (number - 1))
                        carry()
                        pool.indirect_dma_start(out=current, out_offset=None, in_=base[:, :],
                                                in_offset=bass.IndirectOffsetOnAxis(ap=index[:, 0:1], axis=0),
                                                bounds_check=bound, oob_is_err=False).then_inc(gathered, 16)
                        pool.wait_ge(added, turn)
                        pool.wait_ge(carried, turn * 3 + (number - 0))
                        carry()
                        pool.indirect_dma_start(out=base[:, :], in_=total[:], in_offset=None,
                                                out_offset=bass.IndirectOffsetOnAxis(ap=index[:, 0:1], axis=0),
                                                bounds_check=bound, oob_is_err=False).then_inc(scattered, 16)

            @block.vector
            def _(dve):
                fast = dve.value_load(c["fast_i"][0:1, 0:1], min_val=0, max_val=1)
                with dve.If(fast == 0):
                    with dve.Fori(0, NP) as q:
                        dve.wait_ge(copy_in, (q + (done_pairs + 1)) * 16)
                        factor = c["eps1"][:, 0:1] if gin else c["eps1"][:, 1:2]
                        nc.vector.tensor_scalar(own_out[:], own[:], factor, None, ALU.mult).then_inc(scaled, 1)
                    with dve.Fori(0, NT) as e:
                        turn = e + (done_blocks + 1)
                        dve.wait_ge(block_in, (e + 1) * (16 * loads) + (0 if gin else 16 * (done_blocks + NT)))
                        nc.vector.tensor_copy(src[:], ids[:, 0:1])
                        nc.vector.tensor_copy(dst[:], ids[:, 1:2]).then_inc(ids_steps, 1)
                        dve.wait_ge(ids_steps, turn * 2 - 1)
                        nc.vector.tensor_scalar(dst_cols[:], c["ones"][:], dst[:, 0:1], None, ALU.mult)\
                            .then_inc(ids_steps, 1)
                        dve.wait_ge(turned, turn)
                        nc.vector.tensor_scalar(same[:], dst_ps[:], dst[:, 0:1], None, ALU.is_equal)\
                            .then_inc(index_steps, 1)
                        dve.wait_ge(index_steps, turn * 6 - 5)
                        nc.vector.tensor_tensor(earlier[:], same[:], c["below"][:], ALU.mult).then_inc(index_steps, 1)
                        dve.wait_ge(index_steps, turn * 6 - 4)
                        nc.vector.tensor_reduce(count[:], earlier[:], AX.X, ALU.add).then_inc(index_steps, 1)
                        dve.wait_ge(index_steps, turn * 6 - 3)
                        nc.vector.tensor_scalar(first[:], count[:], 0.0, None, ALU.is_equal).then_inc(index_steps, 1)
                        dve.wait_ge(index_steps, turn * 6 - 2)
                        nc.vector.scalar_tensor_tensor(out=index_f[:], in0=dst[:], scalar=float(-NO_ROW),
                                                       in1=first[:], op0=ALU.add, op1=ALU.mult)\
                            .then_inc(index_steps, 1)
                        dve.wait_ge(index_steps, turn * 6 - 1)
                        nc.vector.tensor_scalar(index[:], index_f[:], float(NO_ROW), None, ALU.add)\
                            .then_inc(index_steps, 1)
                        dve.wait_ge(gathered, turn * 32)
                        if gin:
                            dve.wait_ge(edge_done, e + 1)
                            nc.vector.tensor_tensor(msg0[:], edge_ps[:], rows, ALU.add).then_inc(msg_steps, 1)
                            dve.wait_ge(msg_steps, e * 2 + 1)
                            nc.vector.tensor_tensor(msg1[:], msg0[:], c["b_edge"][:], ALU.add).then_inc(msg_steps, 1)
                            dve.wait_ge(msg_steps, e * 2 + 2)
                            nc.vector.tensor_scalar(msg[:], msg1[:], 0.0, None, ALU.max).then_inc(msg_ready, 1)
                        else:
                            nc.vector.tensor_copy(msg[:], rows).then_inc(msg_ready, 1)
                        dve.wait_ge(summed, turn)
                        nc.vector.tensor_tensor(total[:], sum_ps[:], current, ALU.add).then_inc(added, 1)

            @block.tensor
            def _(pe):
                fast = pe.value_load(c["fast_i"][0:1, 0:1], min_val=0, max_val=1)
                with pe.If(fast == 0):
                    with pe.Fori(0, NT) as e:
                        turn = e + (done_blocks + 1)
                        pe.wait_ge(ids_steps, turn * 2)
                        nc.tensor.transpose(dst_ps[:], dst_cols[:], c["ident"][:]).then_inc(turned, 1)
                        if gin:
                            pe.wait_ge(block_in, (e + 1) * 32)
                            nc.tensor.transpose(attr_ps[:], attr[:], c["ident"][:]).then_inc(attr_turned, 1)
                            pe.wait_ge(attr_copied, e + 1)
                            nc.tensor.matmul(edge_ps[:], attr_t[:], c["w_edge"][:], start=True, stop=True)\
                                .then_inc(edge_done, 1)
                        pe.wait_ge(msg_ready, turn)
                        pe.wait_ge(index_steps, turn * 6 - 5)
                        nc.tensor.matmul(sum_ps[:], same[:], msg[:], start=True, stop=True).then_inc(summed, 1)

            if gin:
                @block.scalar
                def _(act):
                    fast = act.value_load(c["fast_i"][0:1, 0:1], min_val=0, max_val=1)
                    with act.If(fast == 0):
                        with act.Fori(0, NT) as e:
                            act.wait_ge(attr_turned, e + 1)
                            nc.scalar.copy(attr_t[:], attr_ps[:]).then_inc(attr_copied, 1)


def gin_pass(nc, keep, dram):
    c = keep
    with ExitStack() as stack:
        m = Memory(nc, stack)
        attr = m.sb("attr", [P, RING, FIRST, DE])
        own = m.sb("own", [P, GROUP, 2, D])
        attr_hi = m.sb("attr_hi", [P, 2, FIRST * P], F32R)
        attr_lo = m.sb("attr_lo", [P, 2, FIRST * P], F32R)
        raw = m.sb("raw", [P, 2, FIRST, D])
        msg_hi = m.sb("msg_hi", [P, 2, BLOCKS, D], F32R)
        msg_lo = m.sb("msg_lo", [P, 2, BLOCKS, D], F32R)
        select = m.sb("gin_select", [P, 2, FIRST + 1, PAIR], F32R)
        h0 = m.sb("h0", [P, RING, 2, D])
        h0t_hi = m.sb("h0t_hi", [P, 2, 2, D], F32R)
        h0t_lo = m.sb("h0t_lo", [P, 2, 2, D], F32R)
        h1t = m.sb("h1t", [P, 2, 2, D])
        h1t_hi = m.sb("h1t_hi", [P, 2, 2, D], F32R)
        h1t_lo = m.sb("h1t_lo", [P, 2, 2, D], F32R)
        h2t = m.sb("h2t", [P, RING, 2, D])
        attr_ps = m.ps("attr_ps", [P, 512])
        edge_ps = m.ps("edge_ps", [P, 4, D])
        agg_ps = m.ps("agg_ps")
        h0t_ps = m.ps("h0t_ps")
        h1t_ps = m.ps("h1t_ps")
        h2t_ps = m.ps("h2t_ps")
        loaded = [m.sem(f"gin_loaded{s}") for s in range(RING)]
        gathered = [m.sem(f"gin_gathered{s}") for s in range(RING)]
        stored = [m.sem(f"gin_stored{s}") for s in range(RING)]
        names = ("index_copied attr_turned attr_rounded attr_split edge_done select_done rows_added msg_rounded "
                 "msg_split agg_done h0_done h0_turned h0_rounded h0_split h1_done h1_ready h1_split h2_done h2_ready stats_done")
        (index_copied, attr_turned, attr_rounded, attr_split, edge_done, select_done, rows_added, msg_rounded,
         msg_split, agg_done, h0_done, h0_turned, h0_rounded, h0_split, h1_done, h1_ready, h1_split, h2_done, h2_ready,
         stats_done) = (m.sem("gin_" + n) for n in names.split())

        with nc.Block() as block:

            @block.sync
            def _(sp):
                fast = sp.value_load(c["fast_i"][0:1, 0:1], min_val=0, max_val=1)

                def step(at):
                    if pair := at(0):
                        s = pair.slot
                        start = sp.value_load(c["starts"][0:1, bass.ds(pair.quad * 4, 1)], min_val=0, max_val=E)
                        if pair.has(RING):
                            sp.wait_ge(attr_turned, pair.before(RING))
                        sp.dma_start(attr[:, s, 0:pair.new],
                                     dram["edge_attr"][bass.ds(start + pair.blocks[0] * P, pair.new * P), :]
                                     .rearrange("(b p) k -> p b k", p=P)).then_inc(loaded[s], 16)
                        load_own(sp, fast, own[:, pair.place], dram["x"], dram["base"], pair, loaded[s], h0_done, GROUP)
                    if pair := at(14):
                        sp.wait_ge(h2_ready, pair.done())
                        sp.dma_start(dram["h2"][bass.ds(pair.q, 1)].rearrange("o p c n -> p (o c) n"),
                                     h2t[:, pair.slot]).then_inc(stored[pair.slot], 16)

                pipeline(sp, step)
                for s in range(RING):
                    sp.wait_ge(stored[s], 16 * (NP // RING))

            @block.gpsimd
            def _(pool):
                bound = pool.to_reg(NPAD - 1)

                def step(at):
                    if (pair := at(0)) and not pair.odd:
                        gather_rows(nc, pool, c, pair, dram["x"], bound, index_copied, gathered, rows_added)

                pipeline(pool, step)

            @block.tensor
            def _(pe):
                def step(at):
                    if pair := at(6):
                        b, half = pair.slot % 2, pair.quad_slot % 2
                        pe.wait_ge(msg_split, pair.done())
                        pe.wait_ge(select_done, pair.done())
                        if pair.has(1):
                            pe.wait_ge(h0_done, pair.before(1))
                        sum_into_nodes(nc, pair, agg_ps, select[:, b], [msg_hi[:, half], msg_lo[:, half]]).then_inc(agg_done, 1)
                    if pair := at(3):
                        b = pair.slot % 2
                        pe.wait_ge(attr_split, pair.done())
                        if pair.has(1):
                            pe.wait_ge(rows_added, pair.before(1))
                        terms = products([attr_hi[:, b], attr_lo[:, b]], [c["w_edge_hi"], c["w_edge_lo"]])
                        for k in range(pair.new):
                            nc.tensor.matmul(edge_ps[:, k], c["two_ones"][:], c["b_edge2"][:], start=True, stop=False)
                            for n, (a, w) in enumerate(terms):
                                last = nc.tensor.matmul(edge_ps[:, k], a[:, k * P:(k + 1) * P], w[:],
                                                        start=False, stop=n == len(terms) - 1)
                        last.then_inc(edge_done, 1)
                    if pair := at(10):
                        b = pair.slot % 2
                        pe.wait_ge(h0_split, pair.done())
                        if pair.has(1):
                            pe.wait_ge(h1_ready, pair.before(1))
                        dense_cols(nc, h1t_ps, [h0t_hi[:, b], h0t_lo[:, b]], [c["w1_hi"], c["w1_lo"]])\
                            .then_inc(h1_done, 1)
                    if pair := at(12):
                        b = pair.slot % 2
                        pe.wait_ge(h1_split, pair.done())
                        if pair.has(1):
                            pe.wait_ge(h2_ready, pair.before(1))
                        dense_cols(nc, h2t_ps, [h1t_hi[:, b], h1t_lo[:, b]], [c["w2_hi"], c["w2_lo"]])\
                            .then_inc(h2_done, 1)
                    if pair := at(8):
                        pe.wait_ge(h0_done, pair.done())
                        if pair.has(1):
                            pe.wait_ge(h0_split, pair.before(1))
                        transpose_rows(nc, c, h0t_ps, h0[:, pair.slot]).then_inc(h0_turned, 1)
                    if pair := at(1):
                        s = pair.slot
                        pe.wait_ge(loaded[s], pair.landed(2))
                        if pair.has(1):
                            pe.wait_ge(attr_split, pair.before(1))
                        for k in range(pair.new):
                            last = nc.tensor.transpose(attr_ps[:, k * P:(k + 1) * P], attr[:, s, k], c["ident"][:])
                        last.then_inc(attr_turned, 1)

                pipeline(pe, step)

            @block.scalar
            def _(act):
                def step(at):
                    if pair := at(11):
                        b = pair.slot % 2
                        act.wait_ge(h1_done, pair.done())
                        if pair.has(2):
                            act.wait_ge(h2_done, pair.before(2))
                            act.wait_ge(h1_split, pair.before(2))
                        for out in (h1t_hi, h1t):
                            for h in range(2):
                                last = nc.scalar.activation(out[:, b, h], h1t_ps[:, h], ACT.Relu,
                                                            bias=c["b1"][:, h:h + 1])
                        last.then_inc(h1_ready, 1)
                    if pair := at(13):
                        s = pair.slot
                        act.wait_ge(h2_done, pair.done())
                        if pair.has(RING):
                            act.wait_ge(stored[s], pair.turn * 16)
                            act.wait_ge(stats_done, pair.before(RING))
                        for h in range(2):
                            last = nc.scalar.activation(h2t[:, s, h], h2t_ps[:, h], ACT.Identity,
                                                        bias=c["b2"][:, h:h + 1])
                        last.then_inc(h2_ready, 1)
                    if pair := at(9):
                        b = pair.slot % 2
                        act.wait_ge(h0_turned, pair.done())
                        if pair.has(2):
                            act.wait_ge(h1_done, pair.before(2))
                        nc.scalar.copy(h0t_hi[:, b], h0t_ps[:]).then_inc(h0_rounded, 1)
                    if pair := at(2):
                        b = pair.slot % 2
                        act.wait_ge(attr_turned, pair.done())
                        if pair.has(2):
                            act.wait_ge(edge_done, pair.before(2))
                        nc.scalar.copy(attr_hi[:, b, 0:pair.new * P], attr_ps[:, 0:pair.new * P]).then_inc(attr_rounded, 1)
                    if pair := at(5):
                        b = pair.slot % 2
                        act.wait_ge(rows_added, pair.done())
                        half, blocks = pair.quad_slot % 2, slice(*pair.blocks)
                        if pair.has(pair.block_life):
                            act.wait_ge(agg_done, pair.before(pair.block_life))
                        nc.scalar.activation(msg_hi[:, half, blocks], raw[:, b, 0:pair.new], ACT.Relu).then_inc(msg_rounded, 1)

                pipeline(act, step)

            @block.vector
            def _(dve):
                def step(at):
                    if pair := at(7):
                        b, s = pair.slot % 2, pair.slot
                        dve.wait_ge(agg_done, pair.done())
                        dve.wait_ge(loaded[s], pair.landed(2))
                        if pair.has(RING):
                            dve.wait_ge(h0_turned, pair.before(RING))
                        nc.vector.scalar_tensor_tensor(out=h0[:, s], in0=own[:, pair.place], scalar=c["self_w"][:, 0:1],
                                                       in1=agg_ps[:], op0=ALU.mult, op1=ALU.add).then_inc(h0_done, 1)
                    if pair := at(4):
                        b, s = pair.slot % 2, pair.slot
                        dve.wait_ge(edge_done, pair.done())
                        dve.wait_ge(gathered[pair.quad_slot], pair.rows_landed())
                        if pair.has(2):
                            dve.wait_ge(msg_rounded, pair.before(2))
                            dve.wait_ge(msg_split, pair.before(2))
                        nc.vector.tensor_tensor(raw[:, b, 0:pair.new], edge_ps[:, 0:pair.new],
                                                c["rows"][:, pair.quad_slot, slice(*pair.blocks)], ALU.add)\
                            .then_inc(rows_added, 1)
                    if pair := at(5):
                        b, s = pair.slot % 2, pair.slot
                        if pair.has(2):
                            dve.wait_ge(agg_done, pair.before(2))
                        select_matrices(nc, c, pair, select[:, b]).then_inc(select_done, 1)
                    if pair := at(11):
                        b = pair.slot % 2
                        dve.wait_ge(h1_ready, pair.done())
                        if pair.has(2):
                            dve.wait_ge(h2_done, pair.before(2))
                        nc.vector.tensor_tensor(h1t_lo[:, b], h1t[:, b], h1t_hi[:, b].bitcast(F32), ALU.subtract)\
                            .then_inc(h1_split, 1)
                    if pair := at(9):
                        b = pair.slot % 2
                        dve.wait_ge(h0_rounded, pair.done())
                        if pair.has(2):
                            dve.wait_ge(h1_done, pair.before(2))
                        nc.vector.tensor_tensor(h0t_lo[:, b], h0t_ps[:], h0t_hi[:, b].bitcast(F32),
                                                ALU.subtract).then_inc(h0_split, 1)
                    if pair := at(2):
                        b = pair.slot % 2
                        dve.wait_ge(attr_rounded, pair.done())
                        if pair.has(2):
                            dve.wait_ge(edge_done, pair.before(2))
                        nc.vector.tensor_tensor(attr_lo[:, b, 0:pair.new * P], attr_ps[:, 0:pair.new * P],
                                                attr_hi[:, b, 0:pair.new * P].bitcast(F32),
                                                ALU.subtract).then_inc(attr_split, 1)
                    if pair := at(14):
                        dve.wait_ge(h2_ready, pair.done())
                        nodes = TAIL if pair.last() else PAIR
                        for h in range(2):
                            last = nc.vector.bn_stats(c["bn_stats"][:, h, bass.ds(pair.q, 1), :],
                                                      h2t[:, pair.slot, h, 0:nodes])
                        last.then_inc(stats_done, 1)
                    if pair := at(5):
                        b = pair.slot % 2
                        half, blocks = pair.quad_slot % 2, slice(*pair.blocks)
                        dve.wait_ge(msg_rounded, pair.done())
                        nc.vector.scalar_tensor_tensor(out=msg_lo[:, half, blocks], in0=raw[:, b, 0:pair.new],
                                                       scalar=0.0, in1=msg_hi[:, half, blocks].bitcast(F32), op0=ALU.max, op1=ALU.subtract)\
                            .then_inc(msg_split, 1)

                pipeline(dve, step)


def batch_norm_scale(nc, keep):
    c = keep
    with ExitStack() as stack:
        m = Memory(nc, stack)
        mv = m.sb("bn_mv", [P, 2, 2])
        sd = m.sb("bn_sd", [P, 2])
        rs = m.sb("bn_rs", [P, 2])
        ma = m.sb("bn_ma", [P, 2])
        chain = m.sem("bn_chain")
        with nc.Block() as block:

            @block.vector
            def _(dve):
                for h in range(2):
                    nc.vector.bn_aggr(mv[:, h], c["bn_stats"][:, h].rearrange("p a b -> p (a b)")).then_inc(chain, 1)
                dve.wait_ge(chain, 3)
                nc.vector.reciprocal(rs[:], sd[:]).then_inc(chain, 1)
                dve.wait_ge(chain, 4)
                nc.vector.tensor_tensor(c["bn_a"][:], c["gamma"][:], rs[:], ALU.mult).then_inc(chain, 1)
                dve.wait_ge(chain, 5)
                nc.vector.tensor_tensor(ma[:], mv[:, :, 0], c["bn_a"][:], ALU.mult).then_inc(chain, 1)
                dve.wait_ge(chain, 6)
                nc.vector.tensor_tensor(c["bn_c"][:], c["beta"][:], ma[:], ALU.subtract).then_inc(chain, 1)

            @block.scalar
            def _(act):
                act.wait_ge(chain, 2)
                nc.scalar.activation(sd[:], mv[:, :, 1], ACT.Sqrt, bias=c["ln_eps"][:, 0:1]).then_inc(chain, 1)


def norm_pass(nc, keep, dram):
    c = keep
    with ExitStack() as stack:
        m = Memory(nc, stack)
        h2t = m.sb("h2t_in", [P, RING, 2, D])
        own = m.sb("x_sb", [P, RING, 2, D])
        zt = m.sb("zt", [P, 2, 2, D])
        res = m.sb("res", [P, RING, 2, D])
        x1 = m.sb("x1", [P, RING, 2, D])
        x1t_hi = m.sb("x1t_hi", [P, 2, 2, D], F32R)
        x1t_lo = m.sb("x1t_lo", [P, 2, 2, D], F32R)
        g = m.sb("g_out", [P, RING, 2, D])
        stats = m.sb("ln_stats", [P, 2, 2, 6])
        mv = m.sb("ln_mv", [P, 2, 2, 2])
        sd = m.sb("ln_sd", [P, 2, 2])
        rs = m.sb("ln_rs", [P, 2, 2])
        z_ps = m.ps("z_ps", (P, 2, 2, D))
        x1t_ps = m.ps("x1t_ps", (P, 2, 2, D))
        g_ps = m.ps("g_ps", (P, 2, 2, D))
        loaded = [m.sem(f"nrm_loaded{s}") for s in range(RING)]
        x1_stored = [m.sem(f"nrm_x1_stored{s}") for s in range(RING)]
        g_stored = [m.sem(f"nrm_g_stored{s}") for s in range(RING)]
        names = ("z_ready z_turned res_added stats_steps sd_ready rs_ready x1_ready x1_turned x1_rounded "
                 "x1_split dense_done g_ready")
        (z_ready, z_turned, res_added, stats_steps, sd_ready, rs_ready, x1_ready, x1_turned, x1_rounded,
         x1_split, dense_done, g_ready) = (m.sem("nrm_" + n) for n in names.split())

        with nc.Block() as block:

            @block.sync
            def _(sp):
                def step(at):
                    if pair := at(0):
                        s = pair.slot
                        if pair.has(RING):
                            sp.wait_ge(z_ready, pair.before(RING))
                            sp.wait_ge(res_added, pair.before(RING))
                        sp.dma_start(h2t[:, s], dram["h2"][bass.ds(pair.q, 1)].rearrange("o p c n -> p (o c) n"))\
                            .then_inc(loaded[s], 16)
                        sp.dma_start(own[:, s], rows_of(dram["x"], pair.q)).then_inc(loaded[s], 16)
                    if pair := at(7):
                        sp.wait_ge(x1_ready, pair.done())
                        sp.dma_start(rows_of(dram["x1"], pair.q), x1[:, pair.slot]).then_inc(x1_stored[pair.slot], 16)
                    if pair := at(11):
                        sp.wait_ge(g_ready, pair.done())
                        sp.dma_start(rows_of(dram["ga"], pair.q), g[:, pair.slot]).then_inc(g_stored[pair.slot], 16)

                pipeline(sp, step)
                for s in range(RING):
                    sp.wait_ge(x1_stored[s], 16 * (NP // RING))
                    sp.wait_ge(g_stored[s], 16 * (NP // RING))

            @block.scalar
            def _(act):
                def step(at):
                    if pair := at(8):
                        b = pair.slot % 2
                        act.wait_ge(x1_turned, pair.done())
                        if pair.has(2):
                            act.wait_ge(dense_done, pair.before(2))
                        nc.scalar.copy(x1t_hi[:, b], x1t_ps[:, b]).then_inc(x1_rounded, 1)
                    if pair := at(2):
                        b, s = pair.slot % 2, pair.slot
                        act.wait_ge(loaded[s], pair.landed(2))
                        if pair.has(2):
                            act.wait_ge(z_turned, pair.before(2))
                        for h in range(2):
                            last = nc.scalar.activation(zt[:, b, h], h2t[:, s, h], ACT.Relu,
                                                        bias=c["bn_c"][:, h:h + 1], scale=c["bn_a"][:, h:h + 1])
                        last.then_inc(z_ready, 1)
                    if pair := at(10):
                        s = pair.slot
                        act.wait_ge(dense_done, pair.done())
                        if pair.has(RING):
                            act.wait_ge(g_stored[s], pair.turn * 16)
                        for j in range(2):
                            last = nc.scalar.activation(g[:, s, j], g_ps[:, s % 2, j], ACT.Identity,
                                                        scale=c["dinv"][:, bass.ds(pair.q * 2 + j, 1)])
                        last.then_inc(g_ready, 1)
                    if pair := at(5):
                        b = pair.slot % 2
                        act.wait_ge(stats_steps, pair.done(2))
                        nc.scalar.activation(sd[:, b], mv[:, b, :, 1], ACT.Sqrt, bias=c["ln_eps"][:, 0:1])\
                            .then_inc(sd_ready, 1)

                pipeline(act, step)

            @block.tensor
            def _(pe):
                def step(at):
                    if pair := at(3):
                        b = pair.slot % 2
                        pe.wait_ge(z_ready, pair.done())
                        if pair.has(2):
                            pe.wait_ge(res_added, pair.before(2))
                        for j in range(2):
                            for h in range(2):
                                last = nc.tensor.transpose(z_ps[:, b, j, h * P:(h + 1) * P],
                                                           zt[:, b, h, j * P:(j + 1) * P], c["ident"][:])
                        last.then_inc(z_turned, 1)
                    if pair := at(7):
                        b = pair.slot % 2
                        pe.wait_ge(x1_ready, pair.done())
                        if pair.has(2):
                            pe.wait_ge(x1_split, pair.before(2))
                        transpose_rows(nc, c, x1t_ps[:, b], x1[:, pair.slot]).then_inc(x1_turned, 1)
                    if pair := at(9):
                        b = pair.slot % 2
                        pe.wait_ge(x1_split, pair.done())
                        if pair.has(2):
                            pe.wait_ge(g_ready, pair.before(2))
                        dense_rows(nc, g_ps[:, b], [x1t_hi[:, b], x1t_lo[:, b]], [c["g1_hi"], c["g1_lo"]])\
                            .then_inc(dense_done, 1)

                pipeline(pe, step)

            @block.vector
            def _(dve):
                def step(at):
                    added, scaled, turned = at(4), at(6), at(8)
                    if pair := added:
                        b, s = pair.slot % 2, pair.slot
                        dve.wait_ge(z_turned, pair.done())
                        dve.wait_ge(loaded[s], pair.landed(2))
                        if pair.has(RING):
                            dve.wait_ge(x1_ready, pair.before(RING))
                        nc.vector.tensor_tensor(res[:, s], z_ps[:, b], own[:, s], ALU.add).then_inc(res_added, 1)
                    if pair := scaled:
                        b = pair.slot % 2
                        dve.wait_ge(sd_ready, pair.done())
                        nc.vector.reciprocal(rs[:, b], sd[:, b]).then_inc(rs_ready, 1)
                    if pair := added:
                        dve.wait_ge(res_added, pair.done())
                        layer_stats(nc, res[:, pair.slot], stats[:, pair.slot % 2], stats_steps)
                    if pair := scaled:
                        b, s = pair.slot % 2, pair.slot
                        dve.wait_ge(rs_ready, pair.done())
                        if pair.has(RING):
                            dve.wait_ge(x1_stored[s], pair.turn * 16)
                            dve.wait_ge(x1_turned, pair.before(RING))
                        for j in range(2):
                            last = nc.vector.tensor_scalar(x1[:, s, j], res[:, s, j], mv[:, b, j, 0:1],
                                                           rs[:, b, j:j + 1], ALU.subtract, ALU.mult)
                        last.then_inc(x1_ready, 1)
                    if pair := turned:
                        b = pair.slot % 2
                        dve.wait_ge(x1_rounded, pair.done())
                        if pair.has(2):
                            dve.wait_ge(dense_done, pair.before(2))
                        nc.vector.tensor_tensor(x1t_lo[:, b], x1t_ps[:, b], x1t_hi[:, b].bitcast(F32),
                                                ALU.subtract).then_inc(x1_split, 1)
                    if pair := added:
                        b = pair.slot % 2
                        if pair.has(2):
                            dve.wait_ge(x1_ready, pair.before(2))
                        layer_variance(nc, dve, pair, stats[:, b], mv[:, b], stats_steps, c["spare"][:, 1:2])

                pipeline(dve, step)


def gcn_pass(nc, keep, dram, name, source, target, bias, weight):
    c = keep
    with ExitStack() as stack:
        m = Memory(nc, stack)
        own = m.sb(name + "own", [P, RING, 2, D])
        rows_hi = m.sb(name + "rows_hi", [P, 2, BLOCKS, D], F32R)
        rows_lo = m.sb(name + "rows_lo", [P, 2, BLOCKS, D], F32R)
        select = m.sb(name + "select", [P, 2, FIRST + 1, PAIR], F32R)
        total = m.sb(name + "total", [P, 2, 2, D])
        scaled = m.sb(name + "scaled", [P, 2, 2, D])
        ht = m.sb(name + "ht", [P, 2, 2, D])
        ht_hi = m.sb(name + "ht_hi", [P, 2, 2, D], F32R)
        ht_lo = m.sb(name + "ht_lo", [P, 2, 2, D], F32R)
        g = m.sb(name + "g", [P, RING, 2, D])
        agg_ps = m.ps(name + "agg_ps", (P, 2, 2, D))
        ht_ps = m.ps(name + "ht_ps", (P, 2, 2, D))
        g_ps = m.ps(name + "g_ps", (P, 2, 2, D))
        loaded = [m.sem(f"{name}loaded{s}") for s in range(RING)]
        gathered = [m.sem(f"{name}gathered{s}") for s in range(RING)]
        stored = [m.sem(f"{name}stored{s}") for s in range(RING)]
        names = ("index_copied rows_rounded rows_split select_done agg_done total_done total_scaled h_turned h_copied "
                 "h_split dense_done g_ready")
        (index_copied, rows_rounded, rows_split, select_done, agg_done, total_done, total_scaled, h_turned, h_copied,
         h_split, dense_done, g_ready) = (m.sem(name + n) for n in names.split())

        with nc.Block() as block:

            @block.sync
            def _(sp):
                fast = sp.value_load(c["fast_i"][0:1, 0:1], min_val=0, max_val=1)

                def step(at):
                    if pair := at(0):
                        s = pair.slot
                        load_own(sp, fast, own[:, s], source, dram["base"], pair, loaded[s], total_done)
                    if pair := at(11):
                        s = pair.slot
                        sp.wait_ge(g_ready, pair.done())
                        sp.dma_start(rows_of(target, pair.q), g[:, s]).then_inc(stored[s], 16)

                pipeline(sp, step)
                for s in range(RING):
                    sp.wait_ge(stored[s], 16 * (NP // RING))

            @block.gpsimd
            def _(pool):
                bound = pool.to_reg(NPAD - 1)

                def step(at):
                    if (pair := at(0)) and not pair.odd:
                        gather_rows(nc, pool, c, pair, source, bound, index_copied, gathered, rows_split)

                pipeline(pool, step)

            @block.tensor
            def _(pe):
                def step(at):
                    if pair := at(6):
                        b = pair.slot % 2
                        pe.wait_ge(total_scaled, pair.done())
                        if pair.has(2):
                            pe.wait_ge(h_copied, pair.before(2))
                        transpose_rows(nc, c, ht_ps[:, b], scaled[:, b]).then_inc(h_turned, 1)
                    if pair := at(3):
                        b, half = pair.slot % 2, pair.quad_slot % 2
                        pe.wait_ge(rows_split, pair.done())
                        pe.wait_ge(select_done, pair.done())
                        if pair.has(2):
                            pe.wait_ge(total_done, pair.before(2))
                        sum_into_nodes(nc, pair, agg_ps[:, b], select[:, b], [rows_hi[:, half], rows_lo[:, half]])\
                            .then_inc(agg_done, 1)
                    if pair := at(9):
                        b = pair.slot % 2
                        pe.wait_ge(h_split, pair.done(2))
                        if pair.has(2):
                            pe.wait_ge(g_ready, pair.before(2))
                        dense_rows(nc, g_ps[:, b], [ht_hi[:, b], ht_lo[:, b]], weight)\
                            .then_inc(dense_done, 1)

                pipeline(pe, step)

            @block.vector
            def _(dve):
                def step(at):
                    if pair := at(2):
                        b = pair.slot % 2
                        if pair.has(2):
                            dve.wait_ge(agg_done, pair.before(2))
                        select_matrices(nc, c, pair, select[:, b]).then_inc(select_done, 1)
                    if pair := at(4):
                        b, s = pair.slot % 2, pair.slot
                        dve.wait_ge(agg_done, pair.done())
                        dve.wait_ge(loaded[s], pair.landed(1))
                        if pair.has(2):
                            dve.wait_ge(total_scaled, pair.before(2))
                        nc.vector.tensor_tensor(total[:, b], agg_ps[:, b], own[:, s], ALU.add).then_inc(total_done, 1)
                    if pair := at(8):
                        b = pair.slot % 2
                        if pair.has(2):
                            dve.wait_ge(dense_done, pair.before(2))
                        dve.wait_ge(h_copied, pair.done())
                        nc.vector.tensor_copy(ht_hi[:, b], ht[:, b]).then_inc(h_split, 1)
                    if pair := at(2):
                        half, blocks = pair.quad_slot % 2, slice(*pair.blocks)
                        dve.wait_ge(rows_rounded, pair.done())
                        if pair.has(pair.block_life):
                            dve.wait_ge(agg_done, pair.before(pair.block_life))
                        nc.vector.tensor_tensor(rows_lo[:, half, blocks], c["rows"][:, pair.quad_slot, blocks],
                                                rows_hi[:, half, blocks].bitcast(F32), ALU.subtract)\
                            .then_inc(rows_split, 1)
                    if pair := at(8):
                        b = pair.slot % 2
                        dve.wait_ge(h_split, pair.q * 2 + 1)
                        nc.vector.tensor_tensor(ht_lo[:, b], ht[:, b], ht_hi[:, b].bitcast(F32), ALU.subtract)\
                            .then_inc(h_split, 1)

                pipeline(dve, step)

            @block.scalar
            def _(act):
                def step(at):
                    if pair := at(1):
                        half, blocks = pair.quad_slot % 2, slice(*pair.blocks)
                        act.wait_ge(gathered[pair.quad_slot], pair.rows_landed())
                        if pair.has(pair.block_life):
                            act.wait_ge(agg_done, pair.before(pair.block_life))
                        nc.scalar.copy(rows_hi[:, half, blocks], c["rows"][:, pair.quad_slot, blocks])\
                            .then_inc(rows_rounded, 1)
                    if pair := at(10):
                        act.wait_ge(dense_done, pair.done())
                        if pair.has(RING):
                            act.wait_ge(stored[pair.slot], pair.turn * 16)
                    if pair := at(7):
                        b = pair.slot % 2
                        act.wait_ge(h_turned, pair.done())
                        if pair.has(2):
                            act.wait_ge(h_split, pair.before(2) * 2)
                        for h in range(2):
                            last = nc.scalar.activation(ht[:, b, h], ht_ps[:, b, h], ACT.Relu, bias=bias[:, h:h + 1])
                        last.then_inc(h_copied, 1)
                    if pair := at(10):
                        s = pair.slot
                        for j in range(2):
                            last = nc.scalar.activation(g[:, s, j], g_ps[:, s % 2, j], ACT.Identity,
                                                        scale=c["dinv"][:, bass.ds(pair.q * 2 + j, 1)])
                        last.then_inc(g_ready, 1)
                    if pair := at(5):
                        b = pair.slot % 2
                        act.wait_ge(total_done, pair.done())
                        if pair.has(2):
                            act.wait_ge(h_turned, pair.before(2))
                        for j in range(2):
                            last = nc.scalar.activation(scaled[:, b, j], total[:, b, j], ACT.Identity,
                                                        scale=c["dinv"][:, bass.ds(pair.q * 2 + j, 1)])
                        last.then_inc(total_scaled, 1)

                pipeline(act, step)


def last_pass(nc, keep, dram, source, bias):
    c = keep
    with ExitStack() as stack:
        m = Memory(nc, stack)
        own = m.sb("fin_own", [P, RING, 2, D])
        x1 = m.sb("fin_x1", [P, RING, 2, D])
        select = m.sb("fin_select", [P, RING, FIRST + 1, PAIR])
        h = m.sb("fin_h", [P, 2, 2, D])
        res = m.sb("fin_res", [P, RING, 2, D])
        y = m.sb("fin_y", [P, RING, 2, D])
        stats = m.sb("fin_stats", [P, 2, 2, 6])
        mv = m.sb("fin_mv", [P, 2, 2, 2])
        sd = m.sb("fin_sd", [P, 2, 2])
        rs = m.sb("fin_rs", [P, 2, 2])
        shift = m.sb("fin_shift", [P, 2, 2])
        agg_ps = m.ps("fin_agg_ps", [P, 2, 2, D])
        loaded = [m.sem(f"fin_loaded{s}") for s in range(RING)]
        gathered = [m.sem(f"fin_gathered{s}") for s in range(RING)]
        stored = [m.sem(f"fin_stored{s}") for s in range(RING)]
        names = ("index_copied select_done agg_done h_ready res_added stats_steps sd_ready "
                 "scale_steps y_ready")
        (index_copied, select_done, agg_done, h_ready, res_added, stats_steps, sd_ready,
         scale_steps, y_ready) = (m.sem("fin_" + n) for n in names.split())

        with nc.Block() as block:

            @block.sync
            def _(sp):
                fast = sp.value_load(c["fast_i"][0:1, 0:1], min_val=0, max_val=1)

                def step(at):
                    if pair := at(0):
                        s = pair.slot
                        load_own(sp, fast, own[:, s], source, dram["base"], pair, loaded[s], agg_done)
                        if pair.has(RING):
                            sp.wait_ge(res_added, pair.before(RING))
                        sp.dma_start(x1[:, s], rows_of(dram["x1"], pair.q)).then_inc(loaded[s], 16)
                    if pair := at(7):
                        s = pair.slot
                        sp.wait_ge(y_ready, pair.done())
                        sp.dma_start(rows_of(dram["out"], pair.q), y[:, s]).then_inc(stored[s], 16)

                pipeline(sp, step)
                for s in range(RING):
                    sp.wait_ge(stored[s], 16 * (NP // RING))

            @block.gpsimd
            def _(pool):
                bound = pool.to_reg(NPAD - 1)

                def step(at):
                    if (pair := at(0)) and not pair.odd:
                        gather_rows(nc, pool, c, pair, source, bound, index_copied, gathered, agg_done)

                pipeline(pool, step)

            @block.tensor
            def _(pe):
                def step(at):
                    if pair := at(2):
                        b, s = pair.slot % 2, pair.slot
                        pe.wait_ge(gathered[pair.quad_slot], pair.rows_landed())
                        pe.wait_ge(loaded[s], pair.landed(2))
                        pe.wait_ge(select_done, pair.done())
                        if pair.has(2):
                            pe.wait_ge(h_ready, pair.before(2))
                        for j in range(2):
                            nc.tensor.matmul(agg_ps[:, b, j], c["ident"][:], own[:, s, j], start=True, stop=False)
                            blocks = tile_blocks(pair, j)
                            for k in blocks:
                                last = nc.tensor.matmul(agg_ps[:, b, j], select[:, s, k, j * P:(j + 1) * P],
                                                        c["rows"][:, pair.quad_slot, pair.odd + k],
                                                        start=False, stop=k == blocks[-1])
                        last.then_inc(agg_done, 1)

                pipeline(pe, step)

            @block.vector
            def _(dve):
                def step(at):
                    chosen, summed, scaled = at(0), at(3), at(5)
                    if pair := summed:
                        b = pair.slot % 2
                        dve.wait_ge(agg_done, pair.done())
                        for j in range(2):
                            last = nc.vector.scalar_tensor_tensor(
                                out=h[:, b, j], in0=agg_ps[:, b, j], scalar=c["dinv"][:, bass.ds(pair.q * 2 + j, 1)],
                                in1=bias[:], op0=ALU.mult, op1=ALU.add)
                        last.then_inc(h_ready, 1)
                    if pair := scaled:
                        b = pair.slot % 2
                        dve.wait_ge(sd_ready, pair.done())
                        nc.vector.reciprocal(rs[:, b], sd[:, b]).then_inc(scale_steps, 1)
                    if pair := summed:
                        b, s = pair.slot % 2, pair.slot
                        dve.wait_ge(h_ready, pair.done())
                        dve.wait_ge(loaded[s], pair.landed(2))
                        if pair.has(RING):
                            dve.wait_ge(y_ready, pair.before(RING))
                        nc.vector.scalar_tensor_tensor(out=res[:, s], in0=h[:, b], scalar=0.0, in1=x1[:, s],
                                                       op0=ALU.max, op1=ALU.add).then_inc(res_added, 1)
                    if pair := scaled:
                        b = pair.slot % 2
                        dve.wait_ge(scale_steps, pair.q * 2 + 1)
                        nc.vector.scalar_tensor_tensor(out=shift[:, b], in0=mv[:, b, :, 0], scalar=-1.0,
                                                       in1=rs[:, b], op0=ALU.mult, op1=ALU.mult)\
                            .then_inc(scale_steps, 1)
                    if pair := summed:
                        dve.wait_ge(res_added, pair.done())
                        layer_stats(nc, res[:, pair.slot], stats[:, pair.slot % 2], stats_steps)
                    if pair := chosen:
                        if pair.has(RING):
                            dve.wait_ge(agg_done, pair.before(RING))
                        select_matrices(nc, c, pair, select[:, pair.slot]).then_inc(select_done, 1)
                    if pair := summed:
                        b = pair.slot % 2
                        if pair.has(2):
                            dve.wait_ge(scale_steps, pair.before(2) * 2)
                        layer_variance(nc, dve, pair, stats[:, b], mv[:, b], stats_steps, c["spare"][:, 1:2])

                pipeline(dve, step)

            @block.scalar
            def _(act):
                def step(at):
                    if pair := at(6):
                        b, s = pair.slot % 2, pair.slot
                        act.wait_ge(scale_steps, pair.done(2))
                        if pair.has(RING):
                            act.wait_ge(stored[s], pair.turn * 16)
                        for j in range(2):
                            last = nc.scalar.activation(y[:, s, j], res[:, s, j], ACT.Identity,
                                                        bias=shift[:, b, j:j + 1], scale=rs[:, b, j:j + 1])
                        last.then_inc(y_ready, 1)
                    if pair := at(4):
                        b = pair.slot % 2
                        act.wait_ge(stats_steps, pair.done(2))
                        nc.scalar.activation(sd[:, b], mv[:, b, :, 1], ACT.Sqrt, bias=c["ln_eps"][:, 0:1])\
                            .then_inc(sd_ready, 1)

                pipeline(act, step)


def gnn(nc, dram):
    with ExitStack() as stack:
        m = Memory(nc, stack)
        dram = dict(dram)
        dram["h2"] = nc.dram_tensor("h2_scratch", [NP, P, 2, D], F32).ap()
        for name in ("x1", "ga", "gb", "base"):
            dram[name] = nc.dram_tensor(name + "_scratch", [NPAD, D], F32).ap()
        keep = {
            "w_edge": m.sb("w_edge", [DE, D]),
            "below": m.sb("below", [P, P]), "two_ones": m.sb("two_ones", [2, P], F32R),
            "b_edge2": m.sb("b_edge2", [2, D], F32R),
            "ident": m.sb("ident", [P, P]), "ones": m.sb("ones", [P, P]),
            "ln_eps": m.sb("ln_eps", [P, 1]), "eps": m.sb("eps_sb", [P, 1]),
            "iota16": m.sb("iota16", [P, NT], F16), "iota32": m.sb("iota32", [P, QUAD]),
            "rows": m.sb("rows", [P, QUAD_RING, BLOCKS, D]), "index": m.sb("index", [P, QUAD_RING, BLOCKS], U32),
            "dinv": m.sb("dinv", [P, NT]), "starts": m.sb("starts_i", [P, NT], I32),
            "fast": m.sb("fast", [P, 1]), "fast_i": m.sb("fast_i", [P, 1], I32),
            "eps1": m.sb("eps1", [P, 2]), "self_w": m.sb("self_w", [P, 1]),
            "place": m.sb("place", [P, NQ, BLOCKS]), "node": m.sb("node_i", [P, NQ, BLOCKS], U32),
            "bn_stats": m.sb("bn_stats", [P, 2, NP, 6]), "bn_a": m.sb("bn_a", [P, 2]), "bn_c": m.sb("bn_c", [P, 2]),
            "rows_in": m.sem("rows_in"), "spare": m.sb("spare", [P, 3]),
            "general_sems": [m.sem(f"gen_{n}") for n in (
                "copy_in scaled copy_out block_in ids_steps turned index_steps "
                "attr_turned attr_copied edge_done msg_steps msg_ready summed gathered added "
                "scattered carried").split()],
        }
        for name in ("w1", "w2", "g1", "g2", "g3"):
            keep[name] = m.sb(name + "_sb", [P, 2, D])
        for name in SPLIT:
            for part in ("_hi", "_lo"):
                keep[name + part] = m.sb(name + part, [P, D] if name == "w_edge" else [P, 2, D], F32R)
        for name in ("b1", "b2", "gamma", "beta", "gb1", "gb2"):
            keep[name] = m.sb(name + "_sb", [P, 2])
        for name in ("b_edge", "gb3"):
            keep[name] = m.sb(name + "_sb", [P, D])

        constants(nc, keep, dram)
        degrees(nc, keep, dram)
        slot_tables(nc, keep, dram)
        general_sum(nc, keep, dram, 0, dram["x"], True)
        gin_pass(nc, keep, dram)
        batch_norm_scale(nc, keep)
        norm_pass(nc, keep, dram)
        general_sum(nc, keep, dram, 1, dram["ga"], False)
        gcn_pass(nc, keep, dram, "gcn1_", dram["ga"], dram["gb"], keep["gb1"], (keep["g2_hi"], keep["g2_lo"]))
        general_sum(nc, keep, dram, 2, dram["gb"], False)
        gcn_pass(nc, keep, dram, "gcn2_", dram["gb"], dram["ga"], keep["gb2"], (keep["g3_hi"], keep["g3_lo"]))
        general_sum(nc, keep, dram, 3, dram["ga"], False)
        last_pass(nc, keep, dram, dram["ga"], keep["gb3"])


def kernel(x, src, dst, edge_attr_128, L0_gnn_W_edge, L0_gnn_b_edge, L0_gnn_W1, L0_gnn_b1, L0_gnn_W2, L0_gnn_b2,
           L0_gnn_eps, L0_gnn_gamma, L0_gnn_beta, L1_gnn_W1, L1_gnn_b1, L1_gnn_W2, L1_gnn_b2, L1_gnn_W3, L1_gnn_b3):
    import numpy as np
    import concourse.bacc as bacc
    from concourse.bass_utils import run_bass_kernel_spmd

    def padded(a, rows, fill=0):
        a = np.asarray(a)
        return np.concatenate([a, np.full((rows - a.shape[0],) + a.shape[1:], fill, a.dtype)])

    edges = padded(np.stack([np.asarray(src), np.asarray(dst)], axis=1), EPAD, FAR)
    edges[E:, 0] = 0
    arrays = {
        "x": padded(x, NPAD), "edges": edges, "edge_attr": padded(edge_attr_128, EPAD),
        "w_edge": L0_gnn_W_edge, "b_edge": L0_gnn_b_edge, "w1": L0_gnn_W1, "b1": L0_gnn_b1, "w2": L0_gnn_W2,
        "b2": L0_gnn_b2, "eps": np.asarray(L0_gnn_eps).reshape(1), "gamma": L0_gnn_gamma, "beta": L0_gnn_beta,
        "g1": np.asarray(L1_gnn_W1).T, "gb1": L1_gnn_b1, "g2": np.asarray(L1_gnn_W2).T, "gb2": L1_gnn_b2,
        "g3": np.asarray(L1_gnn_W3).T, "gb3": L1_gnn_b3,
    }
    nc = bacc.Bacc("TRN2", target_bir_lowering=False, num_devices=1)
    arrays = {name: np.ascontiguousarray(a) for name, a in arrays.items()}
    dram = {name: nc.dram_tensor(name + "_in", a.shape, mybir.dt.from_np(a.dtype), kind="ExternalInput").ap()
            for name, a in arrays.items()}
    dram["out"] = nc.dram_tensor("out", (NPAD, D), F32, kind="ExternalOutput").ap()
    gnn(nc, dram)
    result = run_bass_kernel_spmd(nc, [{name + "_in": a for name, a in arrays.items()}], core_ids=[0])
    return result.results[0]["out"][:N]
```
